# Optimizing a Trainium2 kernel written in Bass

```python
import numpy as np
import jax
import jax.numpy as jnp

def _softmax(x, axis=-1):
    return jax.nn.softmax(x, axis=axis)

def _gelu(x):
    return jax.nn.gelu(x, approximate=True)

def _silu(x):
    return jax.nn.silu(x)

def _sigmoid(x):
    return jax.nn.sigmoid(x)

def _layernorm(x, axis=-1, eps=1e-05):
    m = jnp.mean(x, axis=axis, keepdims=True)
    v = jnp.var(x, axis=axis, keepdims=True)
    return (x - m) / jnp.sqrt(v + eps)

def _scatter_add(tgt, idx, src, axis=0):
    return tgt.at[idx].add(src)

def _segment_sum(src, seg, n):
    return jax.ops.segment_sum(src, seg, n)
kernel_name = 'mk_flamingo_gated_d1_seqx_r8_923132'

def setup_inputs(seed: int=0):
    np.random.seed(seed)
    _w = jnp.asarray

    def _rec_inputs():
        import jax
        import jax.numpy as jnp
        _rk = jax.random.key(seed)
        x = -0.0002928 + 1 * jax.random.normal(jax.random.fold_in(_rk, 1), (32, 64, 512), jnp.float32)
        _lenS = 64 - jax.random.randint(jax.random.fold_in(_rk, 7), (32,), 0, max(1, 64 // 4) + 1, jnp.int32)
        _lenS2 = 64 - jax.random.randint(jax.random.fold_in(_rk, 8), (32,), 0, max(1, 64 // 4) + 1, jnp.int32)
        _ctx_4096P = jax.random.normal(jax.random.fold_in(_rk, 11), (32, 16, 512), jnp.float32)
        _ctx_4096c = jax.random.dirichlet(jax.random.fold_in(_rk, 511), 0.3 * jnp.ones((16,), jnp.float32), (32, 64))
        _ctx_4096t = jnp.einsum('bsk,bkd->bsd', _ctx_4096c, _ctx_4096P)
        _ctx_4096t = _ctx_4096t * jax.lax.rsqrt(jnp.mean(jnp.square(_ctx_4096t)) + 1e-12) * 0.953939
        ctx_4096 = -2.8382e-05 + 0.999851 * (_ctx_4096t + 0.3 * jax.random.normal(jax.random.fold_in(_rk, 611), (32, 64, 512), jnp.float32))
        _validS = jnp.arange(64)[None, :] < _lenS[:, None]
        _validS2 = jnp.arange(64)[None, :] < _lenS2[:, None]
        _causal = jnp.tril(jnp.ones((64, 64), dtype=bool))
        mask_1x1xSxS2_ff0 = jnp.where(jnp.ones((1, 1, 64, 64), dtype=bool), 0.0, -1000000000.0).astype(jnp.float32)
        _g = jax.random.normal(jax.random.fold_in(_rk, 9001), (2, 1), jnp.float32)
        _g = jnp.sign(_g) * jnp.maximum(jnp.abs(_g), 1.0) + (_g == 0) * 1.0
        g_xattn = _g[0]
        g_ffn = _g[1]
        return (x, ctx_4096, mask_1x1xSxS2_ff0, g_xattn, g_ffn)
    x, ctx_4096, mask_1x1xSxS2_ff0, g_xattn, g_ffn = _rec_inputs()

    def _L0_xattn_setup():
        import jax, jax.numpy as jnp
        import numpy as np
        B, Q, K, D = (1, 128, 6404, 512)
        H, KVH, HD = (32, 8, 128)
        GROUPS = H // KVH
        EPS = 1e-05

        def _rmsnorm(x, w):
            xf = x.astype(jnp.float32)
            var = jnp.mean(xf * xf, axis=-1, keepdims=True)
            return (xf * jax.lax.rsqrt(var + EPS)).astype(x.dtype) * w
        key = jax.random.key(seed)
        ks = jax.random.split(key, 8)
        s = 0.02
        return {'hidden_states': jax.random.normal(ks[0], (B, Q, D), jnp.float32), 'cross_attention_states': jax.random.normal(ks[1], (B, K, D), jnp.float32), 'attention_mask': jnp.zeros((B, 1, Q, K), jnp.float32), 'Wq': jax.random.normal(ks[2], (H * HD, D), jnp.float32) * s, 'Wk': jax.random.normal(ks[3], (KVH * HD, D), jnp.float32) * s, 'Wv': jax.random.normal(ks[4], (KVH * HD, D), jnp.float32) * s, 'Wo': jax.random.normal(ks[5], (D, H * HD), jnp.float32) * s, 'q_norm_w': jnp.ones((HD,), jnp.float32), 'k_norm_w': jnp.ones((HD,), jnp.float32)}
    _L0_xattn_all = _L0_xattn_setup()
    _L0_xattn_in = {k: v for k, v in _L0_xattn_all.items() if k in ('Wq', 'Wk', 'Wv', 'Wo', 'q_norm_w', 'k_norm_w')}
    del _L0_xattn_all

    def _L0_ffn_setup():
        import jax, jax.numpy as jnp
        import numpy as np
        HIDDEN = 512
        MOE_INTER = 128
        SHARED_INTER = 512
        NUM_EXPERTS = 16
        TOP_K = 2

        def _moe_forward(x, gate_w, w_gate_up, w_down, shared_w_gate_up, shared_w_down):
            orig_shape = x.shape
            x2 = x.reshape(-1, orig_shape[-1])
            gu_s = x2 @ shared_w_gate_up.T
            g_s, u_s = jnp.split(gu_s, 2, axis=-1)
            shared_out = jax.nn.silu(g_s) * u_s @ shared_w_down.T
            logits = x2 @ gate_w.T
            probs = jax.nn.softmax(logits, axis=-1)
            topk_vals, topk_idx = jax.lax.top_k(probs, TOP_K)
            topk_vals = topk_vals / jnp.sum(topk_vals, axis=-1, keepdims=True)
            combine = jnp.sum(jax.nn.one_hot(topk_idx, NUM_EXPERTS, dtype=x2.dtype) * topk_vals[..., None], axis=1)
            gu = jnp.einsum('th,eih->eti', x2, w_gate_up)
            g, u = jnp.split(gu, 2, axis=-1)
            act = jax.nn.silu(g) * u
            out_e = jnp.einsum('eti,ehi->eth', act, w_down)
            moe_out = jnp.einsum('eth,te->th', out_e, combine)
            return (moe_out + shared_out).reshape(orig_shape)
        key = jax.random.key(seed)
        ks = jax.random.split(key, 6)
        s = 0.02
        hidden_states = jax.random.normal(ks[0], (2, 256, HIDDEN), dtype=jnp.float32)
        gate_w = jax.random.normal(ks[1], (NUM_EXPERTS, HIDDEN), dtype=jnp.float32) * s
        w_gate_up = jax.random.normal(ks[2], (NUM_EXPERTS, 2 * MOE_INTER, HIDDEN), dtype=jnp.float32) * s
        w_down = jax.random.normal(ks[3], (NUM_EXPERTS, HIDDEN, MOE_INTER), dtype=jnp.float32) * s
        shared_w_gate_up = jax.random.normal(ks[4], (2 * SHARED_INTER, HIDDEN), dtype=jnp.float32) * s
        shared_w_down = jax.random.normal(ks[5], (HIDDEN, SHARED_INTER), dtype=jnp.float32) * s
        return {'hidden_states': hidden_states, 'gate_w': gate_w, 'w_gate_up': w_gate_up, 'w_down': w_down, 'shared_w_gate_up': shared_w_gate_up, 'shared_w_down': shared_w_down}
    _L0_ffn_all = _L0_ffn_setup()
    _L0_ffn_in = {k: v for k, v in _L0_ffn_all.items() if k in ('gate_w', 'w_gate_up', 'w_down', 'shared_w_gate_up', 'shared_w_down')}
    del _L0_ffn_all
    return {'x': x, 'ctx_4096': ctx_4096, 'mask_1x1xSxS2_ff0': mask_1x1xSxS2_ff0, 'g_xattn': g_xattn, 'g_ffn': g_ffn, 'L0_xattn_Wq': _L0_xattn_in['Wq'], 'L0_xattn_Wk': _L0_xattn_in['Wk'], 'L0_xattn_Wv': _L0_xattn_in['Wv'], 'L0_xattn_Wo': _L0_xattn_in['Wo'], 'L0_xattn_q_norm_w': _L0_xattn_in['q_norm_w'], 'L0_xattn_k_norm_w': _L0_xattn_in['k_norm_w'], 'L0_ffn_gate_w': _L0_ffn_in['gate_w'], 'L0_ffn_w_gate_up': _L0_ffn_in['w_gate_up'], 'L0_ffn_w_down': _L0_ffn_in['w_down'], 'L0_ffn_shared_w_gate_up': _L0_ffn_in['shared_w_gate_up'], 'L0_ffn_shared_w_down': _L0_ffn_in['shared_w_down']}

def reference(x, ctx_4096, mask_1x1xSxS2_ff0, g_xattn, g_ffn, L0_xattn_Wq, L0_xattn_Wk, L0_xattn_Wv, L0_xattn_Wo, L0_xattn_q_norm_w, L0_xattn_k_norm_w, L0_ffn_gate_w, L0_ffn_w_gate_up, L0_ffn_w_down, L0_ffn_shared_w_gate_up, L0_ffn_shared_w_down):
    import jax
    import jax.numpy as jnp

    def _L0_xattn_ref(hidden_states, cross_attention_states, attention_mask, Wq, Wk, Wv, Wo, q_norm_w, k_norm_w):
        import jax, jax.numpy as jnp
        import numpy as np
        B, Q, K, D = (1, 128, 6404, 512)
        H, KVH, HD = (32, 8, 128)
        GROUPS = H // KVH
        EPS = 1e-05

        def _rmsnorm(x, w):
            xf = x.astype(jnp.float32)
            var = jnp.mean(xf * xf, axis=-1, keepdims=True)
            return (xf * jax.lax.rsqrt(var + EPS)).astype(x.dtype) * w
        bsz, q_len, _ = hidden_states.shape
        kv_len = cross_attention_states.shape[1]
        q = (hidden_states @ Wq.T).reshape(bsz, q_len, H, HD).transpose(0, 2, 1, 3)
        k = (cross_attention_states @ Wk.T).reshape(bsz, kv_len, KVH, HD).transpose(0, 2, 1, 3)
        v = (cross_attention_states @ Wv.T).reshape(bsz, kv_len, KVH, HD).transpose(0, 2, 1, 3)
        q = _rmsnorm(q, q_norm_w)
        k = jnp.repeat(k, GROUPS, axis=1)
        v = jnp.repeat(v, GROUPS, axis=1)
        k = _rmsnorm(k, k_norm_w)
        scale = 1.0 / np.sqrt(HD)
        scores = jnp.einsum('bhqd,bhkd->bhqk', q, k) * scale
        scores = scores + attention_mask[:, :, :, :kv_len]
        probs = jax.nn.softmax(scores.astype(jnp.float32), axis=-1).astype(q.dtype)
        out = jnp.einsum('bhqk,bhkd->bhqd', probs, v)
        out = out.transpose(0, 2, 1, 3).reshape(bsz, q_len, H * HD)
        return out @ Wo.T

    def _L0_ffn_ref(hidden_states, gate_w, w_gate_up, w_down, shared_w_gate_up, shared_w_down):
        import jax, jax.numpy as jnp
        import numpy as np
        HIDDEN = 512
        MOE_INTER = 128
        SHARED_INTER = 512
        NUM_EXPERTS = 16
        TOP_K = 2

        def _moe_forward(x, gate_w, w_gate_up, w_down, shared_w_gate_up, shared_w_down):
            orig_shape = x.shape
            x2 = x.reshape(-1, orig_shape[-1])
            gu_s = x2 @ shared_w_gate_up.T
            g_s, u_s = jnp.split(gu_s, 2, axis=-1)
            shared_out = jax.nn.silu(g_s) * u_s @ shared_w_down.T
            logits = x2 @ gate_w.T
            probs = jax.nn.softmax(logits, axis=-1)
            topk_vals, topk_idx = jax.lax.top_k(probs, TOP_K)
            topk_vals = topk_vals / jnp.sum(topk_vals, axis=-1, keepdims=True)
            combine = jnp.sum(jax.nn.one_hot(topk_idx, NUM_EXPERTS, dtype=x2.dtype) * topk_vals[..., None], axis=1)
            gu = jnp.einsum('th,eih->eti', x2, w_gate_up)
            g, u = jnp.split(gu, 2, axis=-1)
            act = jax.nn.silu(g) * u
            out_e = jnp.einsum('eti,ehi->eth', act, w_down)
            moe_out = jnp.einsum('eth,te->th', out_e, combine)
            return (moe_out + shared_out).reshape(orig_shape)
        return _moe_forward(hidden_states, gate_w, w_gate_up, w_down, shared_w_gate_up, shared_w_down)
    x = x + jnp.tanh(g_xattn[0]) * _L0_xattn_ref(_layernorm(x, axis=-1), ctx_4096, mask_1x1xSxS2_ff0, L0_xattn_Wq, L0_xattn_Wk, L0_xattn_Wv, L0_xattn_Wo, L0_xattn_q_norm_w, L0_xattn_k_norm_w)
    x = x + jnp.tanh(g_ffn[0]) * _L0_ffn_ref(_layernorm(x, axis=-1), L0_ffn_gate_w, L0_ffn_w_gate_up, L0_ffn_w_down, L0_ffn_shared_w_gate_up, L0_ffn_shared_w_down)
    return x

_drawn_inputs = setup_inputs


def setup_inputs(seed=0):
    import zlib

    import numpy as np

    out = dict(_drawn_inputs(seed))
    spreads = {'L0_xattn_q_norm_w': (1.0, 0.6), 'L0_xattn_k_norm_w': (1.0, 0.6)}
    factors = {'L0_ffn_gate_w': 3.747, 'L0_ffn_w_gate_up': 3.513, 'L0_ffn_w_down': 3.511}
    for name, (base, spread) in spreads.items():
        noise = np.random.default_rng([zlib.crc32(name.encode()), seed]).standard_normal(out[name].shape)
        drawn = base * np.exp(spread * noise) if base else spread * noise
        out[name] = jnp.asarray(drawn.astype(out[name].dtype))
    for name, factor in factors.items():
        out[name] = (out[name] * factor).astype(out[name].dtype)
    return out
```

```python
from contextlib import ExitStack

import numpy as np

import concourse.bass as bass
from concourse import mybir

F32 = mybir.dt.float32
F32R = mybir.dt.float32r
BF16 = mybir.dt.bfloat16
I32 = mybir.dt.int32
U32 = mybir.dt.uint32
ALU = mybir.AluOpType
ACT = mybir.ActivationFunctionType
AX = mybir.AxisListType.X

P = 128
B, S, D = 32, 64, 512
T = B * S
KD = D // P
H, KVH, HD = 32, 8, 128
HG = H // KVH
NT = T // P
CT = 2 * P
NC = T // CT
CB = CT // S
STEPS = KVH * NC
E, EI = 16, 128
SI = 512
NB = (2 * T + E * (P - 1)) // P + 1
NBX = NB + 2
EPS = 1e-5


def build(nc, x, ctxT, wk, wv, w_att, w_shd, mask, g_x, g_f, q_w, k_w, gate, w_gu, w_dn, out):
    kbuf = nc.dram_tensor("kbuf", [STEPS, P, CT], F32, kind="Internal").ap()
    vbuf = nc.dram_tensor("vbuf", [STEPS, P, CT], F32, kind="Internal").ap()
    h2buf = nc.dram_tensor("h2buf", [T, D], F32, kind="Internal").ap()
    ybuf = nc.dram_tensor("ybuf", [NB * P, D], F32, kind="Internal").ap()
    slotbuf = nc.dram_tensor("slotbuf", [NB * P, 1], I32, kind="Internal").ap()
    k_st = kbuf.rearrange("(g c) p (b t) -> c b p g t", g=KVH, b=2)
    v_st = vbuf.rearrange("(g c) p (b t) -> c b p g t", g=KVH, b=2)
    h2_t = h2buf.rearrange("(n p) d -> n p d", p=P)
    y_t = ybuf.rearrange("(n p) d -> n p d", p=P)

    with ExitStack() as ctx:
        def sb(name, shape, dt=F32, stack=ctx):
            return stack.enter_context(nc.sbuf_tensor(name, shape, dt))

        def sem(name):
            return ctx.enter_context(nc.semaphore(name))

        ident = sb("ident", [P, P])
        mhalf = sb("mhalf", [P, 16])
        maskb = sb("maskb", [P, S])
        gcol = sb("gcol", [P, 2])
        tg = sb("tg", [P, 2])
        qkw = sb("qkw", [P, 2])
        wqk = sb("wqk", [P, 1])
        tok = sb("tok", [P, NT], I32)
        tri = sb("tri", [P, P])
        ones = sb("ones", [P, P])
        iota_e = sb("iota_e", [P, E])
        iota_b = sb("iota_b", [P, NBX])
        sidx = sb("sidx", [P, NBX], I32)
        zi = sb("zi", [P, NB], I32)
        acc = sb("acc", [P, NT, D])
        accf = acc[:].rearrange("p n d -> p (n d)")
        with ExitStack() as a:
            hT = sb("hT", [P, NC, 2, KD, CT], F32R, a)
        wgu = sb("wgu", [P, E, KD * 2 * EI])
        with ExitStack() as a:
            W = [[sb(f"w{p}{'hl'[q]}", [P, 4096], F32R, a) for q in range(2)] for p in range(2)]
        with ExitStack() as a:
            xg = [sb(f"xg{q}", [P, D], F32, a) for q in range(2)]
            xgT = [sb(f"xgT{q}", [P, KD, P], F32, a) for q in range(2)]
            sge = sb("sge", [P, EI], F32, a)
            acte = sb("acte", [P, EI], F32, a)
            acteT = sb("acteT", [P, P], F32, a)
            ye = [sb(f"ye{q}", [P, D], F32, a) for q in range(2)]
            y1 = [sb(f"y1{q}", [P, D], F32, a) for q in range(2)]
            y2 = [sb(f"y2{q}", [P, D], F32, a) for q in range(2)]
        wpad = sb("wpad", [P, 4 * 4096])
        with ExitStack() as a:
            craw = sb("craw", [P, KD, CT], F32, a)
            c_hi = [sb(f"c_hi{q}", [P, KD, CT], F32R, a) for q in range(2)]
            c_lo = [sb(f"c_lo{q}", [P, KD, CT], F32R, a) for q in range(2)]
            vo = sb("vo", [P, KVH * HD], F32, a)
            kn = sb("kn", [P, KVH, HD], F32, a)
            ko = sb("ko", [P, KVH, P], F32, a)
            ksq = sb("ksq", [P, 2, 4, HD], F32, a)
            kss = sb("kss", [P, KVH], F32, a)
            kv_ = sb("kv_", [P, KVH], F32, a)
            kr = sb("kr", [P, KVH], F32, a)
            xt = [sb(f"xt{q}", [P, D], F32, a) for q in range(2)]
            h1 = sb("h1", [P, D], F32, a)
            st1 = sb("st1", [P, 6], F32, a)
            mv1 = sb("mv1", [P, 2], F32, a)
            ve1 = sb("ve1", [P, 1], F32, a)
            rs1 = sb("rs1", [P, 1], F32, a)
        with ExitStack() as a:
            qs = sb("qs", [P, 2, CB, 2, S], F32, a)
            sq = sb("sq", [P, 2, CB, 2, S], F32, a)
            pb = sb("pb", [P, 8, S], F32, a)
            sqb = sb("sqb", [P, 3, 2, CB, 2, S], BF16, a)
            pt = [sb(f"pt{'hl'[q]}", [P, 2, HG * S], F32R, a) for q in range(2)]
            ah = sb("ah", [P, 2, HG, 2, S], F32R, a)
            al = sb("al", [P, 2, HG, 2, S], F32R, a)
            kt = sb("kt", [P, CB, S], F32, a)
            vt = sb("vt", [P, 2, HD], F32, a)
            wraw = sb("wraw", [P, 512], F32, a)
            vhl = [sb(f"vt{'hl'[q]}", [P, 2, HD], F32R, a) for q in range(2)]
            onec = sb("onec", [P, 1], BF16, a)
            qv = sb("qv", [P, 8], F32, a)
            qr = sb("qr", [P, 8], F32, a)
            mx = sb("mx", [P, 8], F32, a)
            sm = sb("sm", [P, 8], F32, a)
            rc = sb("rc", [P, 8], F32, a)
        with ExitStack() as a:
            xt3 = [sb(f"xt3{q}", [P, D], F32, a) for q in range(2)]
            h2 = [sb(f"h2{q}", [P, D], F32, a) for q in range(4)]
            lgT = sb("lgT", [E, T], F32, a)
            draw = sb("draw", [P, 4 * D], F32, a)
            g_hi = sb("g_hi", [P, KD, P], F32R, a)
            g_lo = sb("g_lo", [P, KD, P], F32R, a)
        wdn = sb("wdn", [P, E, D])
        st3 = sb("st3", [P, NT, 6])
        mv3 = sb("mv3", [P, NT, 2])
        ve3 = sb("ve3", [P, NT])
        rs3 = sb("rs3", [P, NT])
        graw = sb("graw", [P, KD * E])
        sgt = [sb(f"sgt{q}", [P, D]) for q in range(1)]
        aft = [sb(f"aft{q}", [P, D]) for q in range(1)]
        ra = sb("ra", [P, NT, E])
        rb = sb("rb", [P, NT, E])
        oh1 = sb("oh1", [P, NT, E])
        oh2 = sb("oh2", [P, NT, E])
        m8 = sb("m8", [P, NT, 8])
        i8 = sb("i8", [P, NT, 8], U32)
        rsm = sb("rsm", [P, NT])
        rsr = sb("rsr", [P, NT])
        cw = sb("cw", [P, 2, NT])
        slf = sb("slf", [P, 2, NT])
        sli = sb("sli", [P, 2, NT], I32)
        nbk = sb("nbk", [P, E])
        endb = sb("endb", [P, E])
        stb = sb("stb", [P, E])
        ebf = sb("ebf", [1, NBX])
        ebi = sb("ebi", [1, NBX], I32)
        srow = sb("srow", [NB, P], I32)
        srowf = sb("srowf", [NB, P])
        icur = [sb(f"icur{q}", [P, 1], I32) for q in range(2)]

        PS = [ctx.enter_context(nc.psum_tensor(f"ps{q}", [P, 512], F32)) for q in range(8)]

        setup_in, ident_ok, pool_const, const_act, const_dve = (
            sem("setup_in"), sem("ident_ok"), sem("pool_const"), sem("const_act"), sem("const_dve"))
        ctx_in, x_in, k_stored, v_stored = sem("ctx_in"), sem("x_in"), sem("k_stored"), sem("v_stored")
        kvw_in = [sem(f"kvw_in{q}") for q in range(4)]
        kvw_hi, kvw_lo, ctx_hi, ctx_lo = sem("kvw_hi"), sem("kvw_lo"), sem("ctx_hi"), sem("ctx_lo")
        k_done, k_sq, k_ss, k_var, k_rt, kn_done = (
            sem("k_done"), sem("k_sq"), sem("k_ss"), sem("k_var"), sem("k_rt"), sem("kn_done"))
        v_done, v_evac, kT_done, kT_evac = sem("v_done"), sem("v_evac"), sem("kT_done"), sem("kT_evac")
        ln_st, ln_mv, ln_var, ln_rt, h_done, hT_done, hT_hi, hT_lo = (
            sem("ln_st"), sem("ln_mv"), sem("ln_var"), sem("ln_rt"), sem("h_done"), sem("hT_done"),
            sem("hT_hi"), sem("hT_lo"))
        w0_in, w_hi, w_lo, acc_zero = sem("w0_in"), sem("w_hi"), sem("w_lo"), sem("acc_zero")
        wr_in, kt_in, vt_in = sem("wr_in"), sem("kt_in"), sem("vt_in")
        q_done, q_copy, q_sq, ss_done, q_var, q_rt = (
            sem("q_done"), sem("q_copy"), sem("q_sq"), sem("ss_done"), sem("q_var"), sem("q_rt"))
        s_done, s_scaled, s_masked, s_max, s_sub, s_exp, s_sum, s_rcp, p_ready = (
            sem("s_done"), sem("s_scaled"), sem("s_masked"), sem("s_max"), sem("s_sub"), sem("s_exp"),
            sem("s_sum"), sem("s_rcp"), sem("p_ready"))
        sq_pool, sq_b1, sq_r, sq_b2, sq_b3, v_split, pT_hi = (
            sem("sq_pool"), sem("sq_b1"), sem("sq_r"), sem("sq_b2"), sem("sq_b3"), sem("v_split"), sem("pT_hi"))
        pT_done, pT_evac, pv_done, a_hi, a_lo, o_done, acc_done = (
            sem("pT_done"), sem("pT_evac"), sem("pv_done"), sem("a_hi"), sem("a_lo"), sem("o_done"),
            sem("acc_done"))
        x3_in, x1_done, st_done, mv_done, var3, rt3, h2_done, h2_stored, h2T_done, h2T_hi, h2T_lo = (
            sem("x3_in"), sem("x1_done"), sem("st_done"), sem("mv_done"), sem("var3"), sem("rt3"),
            sem("h2_done"), [sem(f"h2_stored{q}") for q in range(4)], sem("h2T_done"), sem("h2T_hi"), sem("h2T_lo"))
        shd_in, shd_hi, shd_lo = sem("shd_in"), sem("shd_hi"), sem("shd_lo")
        g_in, g_hi_ok, g_lo_ok, lg_done, lg_evac, lgt_done = (
            sem("g_in"), sem("g_hi_ok"), sem("g_lo_ok"), sem("lg_done"), sem("lg_evac"), sem("lgt_done"))
        rt_sub, rt_exp, rt_dve, rank_in, rank_done, slot_ok = (
            sem("rt_sub"), sem("rt_exp"), sem("rt_dve"), sem("rank_in"), sem("rank_done"), sem("slot_ok"))
        zero_st, scat, srow_in, srow_f, srowT, sidx_ok = (
            sem("zero_st"), sem("scat"), sem("srow_in"), sem("srow_f"), sem("srowT"),
            sem("sidx_ok"))
        gu_done, sil, act_f, act_hi, act_lo, dn_done, sh_done = (
            sem("gu_done"), sem("sil"), sem("act_f"), sem("act_hi"), sem("act_lo"), sem("dn_done"),
            sem("sh_done"))
        wgu_in, wdn_in = sem("wgu_in"), sem("wdn_in")
        ic_ok, xg_in, xgT_done, xgT_evac, eg_done, e_sil, e_act, eT_done, eT_evac, ed_done, ye_ok, y_st = (
            sem("ic_ok"), [sem("xg_in0"), sem("xg_in1")], sem("xgT_done"), sem("xgT_evac"), sem("eg_done"),
            sem("e_sil"), sem("e_act"), sem("eT_done"), sem("eT_evac"), sem("ed_done"), sem("ye_ok"),
            [sem("y_st0"), sem("y_st1")])
        y1_in, y2_in, add1, add2, out_st = (
            [sem(f"y1_in{q}") for q in range(2)], [sem(f"y2_in{q}") for q in range(2)], sem("add1"), sem("add2"), sem("out_st"))

        dve_mark, pool_mark = sem("dve_mark"), sem("pool_mark")

        block = ctx.enter_context(nc.Block())

        @block.sync
        def _(sp):
            for s in (v_stored, k_stored, *y_st, *h2_stored):
                sp.sem_inc(s, 16)
            for j, g in enumerate((g_x, g_f)):
                sp.dma_start(gcol[:, j:j + 1], g.to_broadcast([P, 1])).then_inc(setup_in, 16)
            sp.dma_start(qkw[:, 0:1], q_w).then_inc(setup_in, 16)
            sp.dma_start(qkw[:, 1:2], k_w).then_inc(setup_in, 16)
            for j in range(2):
                sp.dma_start(maskb[j * S:(j + 1) * S, :], mask).then_inc(setup_in, 16)
            sp.dma_start(craw[:], ctxT[0]).then_inc(ctx_in, 16)
            for j in range(4):
                src = (wk, wv)[j // 2][:, (j % 2) * 2048:(j % 2 + 1) * 2048]
                sp.dma_start(accf[:, j * 2048:(j + 1) * 2048], src).then_inc(kvw_in[j], 16)
            sp.dma_start(xt[0][:], x[0]).then_inc(x_in, 16)
            for n in range(NT):
                if n + 1 < NT:
                    if n >= 1:
                        sp.wait_ge(h_done, n)
                    sp.wait_ge(x_in, 16 * (n + 1))
                    sp.dma_start(xt[(n + 1) % 2][:], x[n + 1]).then_inc(x_in, 16)
                if n % 2 == 0:
                    c = n // 2 + 1
                    sp.wait_ge(ctx_hi, c)
                    sp.wait_ge(ctx_lo, c)
                    sp.dma_start(craw[:], ctxT[c % NC]).then_inc(ctx_in, 16)
                if n == 1:
                    sp.wait_ge(kvw_lo, 2)
                    sp.dma_start(accf[:, 0:4096].rearrange("p (s n) -> p s n", s=NC),
                                 w_att[0:NC].rearrange("s p n -> p s n")).then_inc(w0_in, 16)
                sp.wait_ge(v_evac, 2 * n + 4)
                sp.dma_start(v_st[n // 2, n % 2], vo[:].rearrange("p (g t) -> p g t", g=KVH)).then_inc(v_stored, 16)
                sp.wait_ge(kT_evac, 2 * n + 4)
                sp.dma_start(k_st[n // 2, n % 2], ko[:]).then_inc(k_stored, 16)
            sp.wait_ge(v_stored, 16 * NT + 16)
            sp.wait_ge(k_stored, 16 * NT + 16)
            sp.wait_ge(w_hi, 8)
            sp.wait_ge(w_lo, 8)
            sp.dma_start(kt[:].rearrange("p b t -> p (b t)"), kbuf[0]).then_inc(kt_in, 16)
            sp.dma_start(vt[:].rearrange("p b t -> p (b t)"), vbuf[0]).then_inc(vt_in, 16)
            with sp.Fori(0, STEPS - 1) as i:
                sp.wait_ge(s_done, i + 1)
                sp.dma_start(kt[:].rearrange("p b t -> p (b t)"), kbuf[i + 1]).then_inc(kt_in, 16)
                sp.wait_ge(v_split, 2 * i + 2)
                sp.dma_start(vt[:].rearrange("p b t -> p (b t)"), vbuf[i + 1]).then_inc(vt_in, 16)
                sp.wait_ge(w_hi, i + 8)
                sp.wait_ge(w_lo, i + 8)
                sp.dma_start(wraw[:], w_att[i + NC]).then_inc(wr_in, 16)
            sp.wait_ge(w_hi, STEPS + 7)
            sp.wait_ge(w_lo, STEPS + 7)
            sp.dma_start(wraw[:], w_att[STEPS - 1 + NC]).then_inc(wr_in, 16)
            sp.wait_ge(s_done, STEPS)
            sp.dma_start(kt[:].rearrange("p b t -> p (b t)"), kbuf[0]).then_inc(kt_in, 16)
            sp.wait_ge(p_ready, 2 * STEPS + 2)
            sp.wait_ge(a_lo, 4 * STEPS + 4)
            sp.wait_ge(o_done, 2 * STEPS + 1)
            sp.wait_ge(w_lo, STEPS + 8)
            sp.dma_start(graw[:], gate).then_inc(g_in, 16)
            sp.dma_start(draw[:], w_shd).then_inc(shd_in, 16)
            sp.dma_start(slotbuf.rearrange("(p b) o -> p (b o)", p=P), zi[:]).then_inc(zero_st, 16)
            for n in range(NT):
                if n >= 1:
                    sp.wait_ge(x3_in, 16 * n)
                if n >= 2:
                    sp.wait_ge(x1_done, n - 1)
                sp.dma_start(xt3[n % 2][:], x[n]).then_inc(x3_in, 16)
            with sp.Fori(0, NT // 4) as m:
                for q in range(4):
                    sp.wait_ge(h2_done, 4 * m + q + 1)
                    sp.dma_start(h2_t[4 * m + q], h2[q][:]).then_inc(h2_stored[q], 16)
            for q in range(4):
                sp.wait_ge(h2_stored[q], 16 * (NT // 4) + 16)
            sp.wait_ge(shd_lo, 1)
            sp.wait_ge(slot_ok, 1)
            sp.dma_start(wdn[:], w_dn.rearrange("e p n -> p e n")).then_inc(wdn_in, 16)
            def load_gate_up(c):
                sp.wait_ge(gu_done, 8 * c + 8)
                sp.dma_start(wgu[:, bass.ds(4 * c, 4), :],
                             w_gu[bass.ds(4 * c, 4)].rearrange("e p n -> p e n")).then_inc(wgu_in, 16)

            with sp.Fori(0, 3) as c:
                load_gate_up(c)
            sp.wait_ge(scat, 16 * 2 * NT)
            sp.dma_start(srow[:], slotbuf.rearrange("(b p) o -> b (p o)", p=P)).then_inc(srow_in, 16)
            load_gate_up(3)
            with sp.Fori(0, NB // 2) as bb:
                for q in range(2):
                    b = 2 * bb + q
                    sp.wait_ge(ye_ok, b + 3)
                    sp.dma_start(y_t[b], ye[q][:]).then_inc(y_st[q], 16)
            with sp.Fori(0, NT) as n:
                sp.wait_ge(add2, n + 3)
                sp.dma_start(out[n], acc[:, n, :]).then_inc(out_st, 16)
            sp.wait_ge(out_st, 16 * NT)
            sp.wait_ge(wdn_in, 16)

        @block.gpsimd
        def _(pool):
            pool.memset(mhalf[:], -0.5).then_inc(pool_const, 1)
            pool.memset(ident[:], 0.0).then_inc(ident_ok, 1)
            pool.wait_ge(ident_ok, 1)
            pool.affine_select(out=ident[:], in_=ident[:], compare_op=ALU.not_equal, fill=1.0, base=0,
                               pattern=[[-1, P]], channel_multiplier=1).then_inc(ident_ok, 1)
            pool.memset(zi[:], 0).then_inc(pool_const, 1)
            pool.memset(sidx[:], 0).then_inc(pool_const, 1)
            pool.memset(ones[:], 1.0).then_inc(pool_const, 1)
            pool.memset(tri[:], 1.0).then_inc(pool_const, 1)
            pool.wait_ge(pool_const, 5)
            pool.affine_select(out=tri[:], in_=tri[:], compare_op=ALU.is_gt, fill=0.0, base=0,
                               pattern=[[1, P]], channel_multiplier=-1).then_inc(pool_const, 1)
            pool.iota(iota_e[:], pattern=[[1, E]], base=0, channel_multiplier=0,
                      allow_small_or_imprecise_dtypes=True).then_inc(pool_const, 1)
            pool.iota(iota_b[:], pattern=[[1, NBX]], base=0, channel_multiplier=0,
                      allow_small_or_imprecise_dtypes=True).then_inc(pool_const, 1)
            pool.iota(tok[:], pattern=[[P, NT]], base=0, channel_multiplier=1).then_inc(pool_const, 1)
            pool.wait_ge(pool_const, 9)
            with pool.Fori(0, NT) as n:
                pool.wait_ge(ln_var, n + 1)
                pool.tensor_tensor(rs1[:], ve1[:], mhalf[:, 0:1], ALU.pow).then_inc(ln_rt, 1)
                pool.wait_ge(k_var, n + 1)
                pool.tensor_tensor(kr[:], kv_[:], mhalf[:, 0:KVH], ALU.pow).then_inc(k_rt, 1)
            pool.wait_ge(w_hi, 8)
            pool.wait_ge(w_lo, 8)
            pool.wait_ge(v_stored, 16 * NT + 16)
            pool.wait_ge(k_stored, 16 * NT + 16)
            pool.memset(onec[:], 1.0).then_inc(acc_zero, 1)
            for t in (ah, al):
                pool.memset(t[:, 1].rearrange("p h b s -> p (h b s)").bitcast(F32), 0.0).then_inc(acc_zero, 1)
            pool.memset(accf, 0.0).then_inc(acc_zero, 1)

            def split_squares(j):
                flat = lambda t: t.rearrange("p b h s -> p (b h s)")
                part = [flat(sqb[:, z, 0]) for z in range(3)]
                pool.wait_ge(q_sq, 2 * j + 1)
                pool.wait_ge(sq_b1, 2 * j + 1)
                pool.tensor_tensor(flat(sq[:, 0]), flat(sq[:, 0]), part[0], ALU.subtract).then_inc(sq_pool, 1)
                pool.wait_ge(sq_pool, 3 * j + 1)
                pool.sem_inc(pool_mark, 1)
                pool.tensor_copy(part[1], flat(sq[:, 0])).then_inc(sq_pool, 1)
                pool.wait_ge(sq_pool, 3 * j + 2)
                pool.tensor_tensor(part[2], flat(sq[:, 0]), part[1], ALU.subtract).then_inc(sq_pool, 1)

            def inverse_root(j):
                pool.wait_ge(q_var, j + 1)
                pool.tensor_tensor(qr[:], qv[:], mhalf[:, 0:8], ALU.pow).then_inc(q_rt, 1)

            with pool.Fori(0, STEPS) as j:
                split_squares(j)
                inverse_root(j)
                pool.wait_ge(vt_in, 16 * j + 16)
                pool.wait_ge(pv_done, 2 * j + 2)
                pool.sem_inc(pool_mark, 1)
                pool.tensor_copy(vhl[0][:], vt[:]).then_inc(v_split, 1)
                pool.wait_ge(v_split, 2 * j + 1)
                pool.tensor_tensor(vhl[1][:], vt[:], vhl[0][:], ALU.subtract).then_inc(v_split, 1)
            split_squares(STEPS)
            inverse_root(STEPS)
            pool.wait_ge(var3, 1)
            pool.tensor_tensor(rs3[:], ve3[:], mhalf[:, 0:NT], ALU.pow).then_inc(rt3, 1)
            pool.wait_ge(slot_ok, 1)
            pool.wait_ge(zero_st, 16)
            for s in range(2):
                for n in range(NT):
                    pool.indirect_dma_start(slotbuf, bass.IndirectOffsetOnAxis(sli[:, s, n:n + 1], 0),
                                            tok[:, n:n + 1], None).then_inc(scat, 16)
            pool.wait_ge(sidx_ok, 1)
            for q in range(4):
                pool.wait_ge(h2_stored[q], 16 * (NT // 4) + 16)
            pool.wait_ge(gu_done, 32)
            with pool.Fori(0, NBX // 2) as m:
                for q in range(2):
                    b = 2 * m + q
                    pool.wait_ge(xgT_done, b + 1)
                    pool.tensor_copy(icur[q][:], sidx[:, bass.ds(b, 1)]).then_inc(ic_ok, 1)
                    pool.wait_ge(ic_ok, b + 1)
                    pool.sem_inc(pool_mark, 1)
                    pool.indirect_dma_start(xg[q][:], None, h2buf,
                                            bass.IndirectOffsetOnAxis(icur[q][:, 0:1], 0)).then_inc(xg_in[q], 16)
            pool.wait_ge(y_st[0], 16 * (NB // 2) + 16)
            pool.wait_ge(y_st[1], 16 * (NB // 2) + 16)
            for n in range(NT):
                pool.wait_ge(add2, n + 1)
                for s, (y, y_in) in enumerate(((y1, y1_in), (y2, y2_in))):
                    pool.indirect_dma_start(y[n % 2][:], None, ybuf,
                                            bass.IndirectOffsetOnAxis(sli[:, s, n:n + 1], 0)).then_inc(y_in[n % 2], 16)

        def pv_view(bp, b2):
            return PS[4 + b2][:, bp * 256:(bp + 1) * 256].rearrange("p (h s) -> p h s", s=S)

        def split_product(pe, dst, l_hi, l_lo, r_hi, r_lo, first, last):
            pe.matmul(dst, l_hi, r_lo, start=first, stop=False)
            pe.matmul(dst, l_lo, r_hi, start=False, stop=False)
            return pe.matmul(dst, l_hi, r_hi, start=False, stop=last)

        @block.tensor
        def _(pe):
            pe.wait_ge(ident_ok, 2)
            pe.sem_inc(xgT_done, 2)
            pe.sem_inc(ss_done, 1)
            pe.sem_inc(pv_done, 2)

            def kv_half(j, cp, tt):
                for k in range(KD):
                    w = slice((j % 2) * 2048 + k * 512, (j % 2) * 2048 + (k + 1) * 512)
                    ts = slice(tt * P, (tt + 1) * P)
                    mm = split_product(pe, PS[j][:], c_hi[cp][:, k, ts], c_lo[cp][:, k, ts],
                                       W[j // 2][0][:, w], W[j // 2][1][:, w], k == 0, k == KD - 1)
                return mm

            with pe.Fori(0, NC // 2) as m:
                for cp in range(2):
                    for tt in range(2):
                        c = 2 * m + cp
                        n = 4 * m + 2 * cp + tt
                        if tt == 0:
                            pe.wait_ge(ctx_hi, c + 1)
                            pe.wait_ge(ctx_lo, c + 1)
                        for j in range(2):
                            pe.wait_ge(kvw_lo, j + 1)
                            pe.wait_ge(kn_done, 2 * n + 1 + j)
                            kv_half(j, cp, tt).then_inc(k_done, 1)
                        pe.wait_ge(h_done, n + 1)
                        for k in range(KD):
                            mm = pe.transpose(PS[6][:, k * P:(k + 1) * P], h1[:, k * P:(k + 1) * P], ident[:])
                        mm.then_inc(hT_done, 1)
                        for j in range(2):
                            pe.wait_ge(kvw_lo, j + 3)
                            pe.wait_ge(v_evac, 2 * n + 1 + j)
                            kv_half(2 + j, cp, tt).then_inc(v_done, 1)
                        for j in range(2):
                            pe.wait_ge(kn_done, 2 * n + 3 + j)
                            pe.wait_ge(kT_evac, 2 * n + 1 + j)
                            for q in range(4):
                                mm = pe.transpose(PS[4 + j][:, q * P:(q + 1) * P], kn[:, 4 * j + q, :], ident[:])
                            mm.then_inc(kT_done, 1)

            def q_head(hp, h, chunk, w):
                for k in range(KD):
                    c0 = k * 512 + (2 * hp + h) * P
                    hc = [hT[:, bass.ds(chunk, 1), x_, k, :].rearrange("p a t -> p (a t)") for x_ in range(2)]
                    mm = split_product(pe, PS[hp][:, h * CT:(h + 1) * CT], w[0][:, c0:c0 + P],
                                       w[1][:, c0:c0 + P], hc[0], hc[1], k == 0, k == KD - 1)
                return mm

            def scores(j):
                pe.wait_ge(q_copy, 2 * j + 2)
                pe.wait_ge(kt_in, 16 * j + 16)
                for hp in range(2):
                    for b in range(CB):
                        for h in range(2):
                            mm = pe.matmul(PS[3][h * S:(h + 1) * S, (CB * hp + b) * S:(CB * hp + b + 1) * S],
                                           qs[:, hp, b, h], kt[:, b, :], start=True, stop=True)
                mm.then_inc(s_done, 1)

            def q_sums(j):
                pe.wait_ge(sq_pool, 3 * j + 3)
                pe.wait_ge(sq_b1, 2 * j + 2)
                pe.wait_ge(sq_b2, j + 1)
                pe.wait_ge(sq_b3, j + 1)
                for hp in range(2):
                    for b in range(CB):
                        for z in range(3):
                            mm = pe.matmul(PS[2][:, CB * hp + b:CB * hp + b + 1],
                                           sqb[:, z, hp, b].rearrange("p h s -> p (h s)"), onec[:],
                                           start=(z == 0), stop=(z == 2))
                mm.then_inc(ss_done, 1)

            def project_out(bp, w_o, heads):
                for h in heads:
                    c0 = 2048 + h * 512
                    lh, ll = (t[:, bp, h].rearrange("p b s -> p (b s)") for t in (ah, al))
                    mm = split_product(pe, PS[6 + bp][:], lh, ll, w_o[0][:, c0:c0 + 512],
                                       w_o[1][:, c0:c0 + 512], h == 0, h == HG - 1)
                if heads[-1] == HG - 1:
                    mm.then_inc(o_done, 1)

            def step(i, chunk_q, w_q, w_o, w_before, q_ready, o_ready):
                if q_ready is not None:
                    pe.wait_ge(w_lo, q_ready)
                pe.wait_ge(sq_b1, 2 * i + 1)
                q_head(0, 0, chunk_q, w_q)
                q_head(0, 1, chunk_q, w_q).then_inc(q_done, 1)
                pe.wait_ge(sq_b1, 2 * i + 2)
                q_head(1, 0, chunk_q, w_q)
                for m in range(4):
                    if m % 2 == 0:
                        pe.wait_ge(p_ready, 2 * i + 1 + m // 2)
                    src = pb[:, CB * (m // 2) + 2 * (m % 2):CB * (m // 2) + 2 * (m % 2) + 2, :]
                    mm = pe.transpose(PS[2 + m % 2][:, m // 2 * P:(m // 2 + 1) * P], src.rearrange("p b s -> p (b s)"), ident[:])
                mm.then_inc(pT_done, 1)
                q_head(1, 1, chunk_q, w_q).then_inc(q_done, 1)
                pe.wait_ge(v_split, 2 * i + 2)
                pe.wait_ge(a_hi, 4 * i + 4)
                pe.wait_ge(a_lo, 4 * i + 4)
                for b2 in range(2):
                    rows = slice(b2 * S, (b2 + 1) * S)
                    for bp in range(2):
                        if b2 == 0:
                            pe.wait_ge(pT_hi, 2 * i + 1 + bp)
                            pe.wait_ge(pT_evac, 2 * i + 1 + bp)
                        probs = [t[rows, bp, :] for t in pt]
                        mm = split_product(pe, PS[4 + b2][:, bp * 256:(bp + 1) * 256], vhl[0][rows, bp, :],
                                           vhl[1][rows, bp, :], probs[0], probs[1], True, True)
                    mm.then_inc(pv_done, 1)
                scores(i + 1)
                pe.wait_ge(acc_done, 2 * i + 1)
                project_out(1, w_before, (0, 1, 2))
                q_sums(i + 1)
                project_out(1, w_before, (3,))
                pe.wait_ge(w_lo, o_ready)
                pe.wait_ge(a_hi, 4 * i + 6)
                pe.wait_ge(a_lo, 4 * i + 6)
                pe.wait_ge(acc_done, 2 * i + 2)
                project_out(0, w_o, (0, 1, 2, 3))

            pe.wait_ge(w_lo, 4)
            for hp in range(2):
                q_head(hp, 0, 0, W[0])
                q_head(hp, 1, 0, W[0]).then_inc(q_done, 1)
            scores(0)
            pe.wait_ge(acc_zero, 3)
            q_sums(0)
            with pe.Fori(0, KVH // 2) as gg:
                for p in range(2):
                    i0 = 2 * NC * gg + NC * p
                    step(i0, 1, W[p], W[p], W[1 - p], None, i0 + 8)
                    with pe.Fori(0, NC - 2) as t:
                        step(i0 + 1 + t, t + 2, W[p], W[p], W[p], None, i0 + 8)
                    step(i0 + NC - 1, 0, W[1 - p], W[p], W[p], i0 + 12, i0 + 8)
            pe.wait_ge(a_hi, 4 * STEPS + 4)
            pe.wait_ge(a_lo, 4 * STEPS + 4)
            pe.wait_ge(acc_done, 2 * STEPS + 1)
            project_out(1, W[1], (0, 1, 2, 3))

            with pe.Fori(0, NT // 4) as m:
                for q in range(4):
                    pe.wait_ge(h2_done, 4 * m + q + 1)
                    for k in range(KD):
                        mm = pe.transpose(PS[q][:, k * P:(k + 1) * P], h2[q][:, k * P:(k + 1) * P], ident[:])
                    mm.then_inc(h2T_done, 1)
            pe.wait_ge(h2T_hi, NT)
            pe.wait_ge(h2T_lo, NT)
            pe.wait_ge(g_lo_ok, 1)
            for c in range(4):
                for k in range(KD):
                    mm = split_product(pe, PS[4 + c][:], g_hi[:, k, :], g_lo[:, k, :],
                                       hT[:, 2 * c:2 * c + 2, 0, k, :], hT[:, 2 * c:2 * c + 2, 1, k, :],
                                       k == 0, k == KD - 1)
                mm.then_inc(lg_done, 1)
            pe.wait_ge(lg_evac, 4)
            for n in range(NT):
                mm = pe.transpose(PS[0][:, n * E:(n + 1) * E], lgT[:, n * P:(n + 1) * P], ident[0:E, 0:E])
            mm.then_inc(lgt_done, 1)
            pe.wait_ge(rank_in, 1)
            pe.matmul(PS[1][:, 0:NT * E], tri[:], ra[:].rearrange("p n e -> p (n e)"), start=True, stop=False)
            pe.matmul(PS[1][:, 0:NT * E], ones[:], rb[:].rearrange("p n e -> p (n e)"), start=False, stop=True)
            pe.matmul(PS[2][:, 0:E], ones[:], nbk[:], start=True, stop=True).then_inc(rank_done, 1)
            pe.wait_ge(slot_ok, 1)

            def gate_up(c, it):
                pe.wait_ge(act_f, 4 * c + it + 1)
                for u in range(2):
                    for k in range(KD):
                        c0 = k * 2 * SI + u * SI + it * P
                        mm = split_product(pe, PS[2 * (it % 2) + u][:], W[0][0][:, c0:c0 + P],
                                           W[0][1][:, c0:c0 + P], hT[:, bass.ds(2 * c, 2), 0, k, :],
                                           hT[:, bass.ds(2 * c, 2), 1, k, :], k == 0, k == KD - 1)
                    mm.then_inc(gu_done, 1)

            def down(c, it):
                pe.wait_ge(act_lo, 4 * c + it + 1)
                for tl in range(4):
                    if it == 0:
                        pe.wait_ge(sh_done, 4 * c + tl + 1)
                    c0 = it * 512
                    mm = split_product(pe, PS[4 + tl][:], W[1][1][:, c0 + tl * P:c0 + (tl + 1) * P],
                                       W[1][1][:, 2048 + c0 + tl * P:2048 + c0 + (tl + 1) * P],
                                       W[1][0][:, c0:c0 + 512], W[1][0][:, 2048 + c0:2048 + c0 + 512],
                                       it == 0, it == 3)
                    if it == 3:
                        mm.then_inc(dn_done, 1)

            def shared(c):
                for it in range(3):
                    gate_up(c, it)
                down(c, 0)
                gate_up(c, 3)
                for it in range(1, 4):
                    down(c, it)

            pe.wait_ge(shd_lo, 1)
            with pe.Fori(0, 3) as c:
                shared(c)
            pe.wait_ge(srow_f, 1)
            pe.wait_ge(sh_done, 16)
            pe.transpose(PS[7][:, 0:NB], srowf[:], ident[0:NB, 0:NB]).then_inc(srowT, 1)
            pe.wait_ge(sidx_ok, 1)
            shared(3)

            def expert_T(b, q):
                pe.wait_ge(xg_in[q], 8 * (b - q) + 16)
                for k in range(KD):
                    mm = pe.transpose(PS[q][:, k * P:(k + 1) * P], xg[q][:, k * P:(k + 1) * P], ident[:])
                mm.then_inc(xgT_done, 1)

            def expert_gate_up(b, q):
                e = pe.value_load(ebi[0:1, bass.ds(b, 1)], min_val=0, max_val=E - 1)
                pe.wait_ge(xgT_evac, b + 1)
                for k in range(KD):
                    mm = pe.matmul(PS[2 + q][:, 0:2 * EI], xgT[q][:, k, :],
                                   wgu[:, bass.ds(e, 1), k * 2 * EI:(k + 1) * 2 * EI].rearrange("p a n -> p (a n)"),
                                   start=(k == 0), stop=(k == KD - 1))
                mm.then_inc(eg_done, 1)

            def expert_down(b, q):
                e = pe.value_load(ebi[0:1, bass.ds(b, 1)], min_val=0, max_val=E - 1)
                pe.wait_ge(eT_evac, b + 1)
                pe.wait_ge(ye_ok, b + 1)
                pe.matmul(PS[5 + q][:], acteT[:], wdn[:, bass.ds(e, 1), :].rearrange("p a n -> p (a n)"),
                          start=True, stop=True).then_inc(ed_done, 1)

            pe.wait_ge(wdn_in, 16)
            pe.wait_ge(wgu_in, 64)
            pe.wait_ge(sh_done, 20)
            expert_T(0, 0)
            expert_T(1, 1)
            expert_gate_up(0, 0)
            with pe.Fori(0, NB // 2) as m:
                for q in range(2):
                    b = 2 * m + q
                    expert_T(b + 2, q)
                    pe.wait_ge(e_act, b + 1)
                    pe.transpose(PS[4][:, 0:P], acte[:], ident[:]).then_inc(eT_done, 1)
                    expert_gate_up(b + 1, 1 - q)
                    expert_down(b, q)

        @block.scalar
        def _(act):
            act.sem_inc(v_evac, 2)
            act.sem_inc(kT_evac, 2)
            act.sem_inc(a_hi, 4)
            act.wait_ge(setup_in, 96)
            act.activation(tg[:], gcol[:], ACT.Tanh).then_inc(const_act, 1)
            act.wait_ge(ctx_in, 16)
            act.copy(c_hi[0][:], craw[:]).then_inc(ctx_hi, 1)
            for j in range(4):
                act.wait_ge(kvw_in[j], 16)
                act.copy(W[j // 2][0][:, (j % 2) * 2048:(j % 2 + 1) * 2048],
                         accf[:, j * 2048:(j + 1) * 2048]).then_inc(kvw_hi, 1)
            act.wait_ge(const_dve, 1)
            with act.Fori(0, NC // 2) as m:
                for cp in range(2):
                    for tt in range(2):
                        c = 2 * m + cp
                        n = 4 * m + 2 * cp + tt
                        if tt == 1:
                            act.wait_ge(ctx_in, 16 * c + 32)
                            act.copy(c_hi[1 - cp][:], craw[:]).then_inc(ctx_hi, 1)
                        for j in range(2):
                            act.wait_ge(k_done, 2 * n + 1 + j)
                            act.activation(ksq[:, j].rearrange("p g d -> p (g d)"), PS[j][:],
                                           ACT.Square).then_inc(k_sq, 1)
                        act.wait_ge(hT_done, n + 1)
                        act.copy(hT[:, bass.ds(c, 1), 0, :, tt * P:(tt + 1) * P].rearrange("p a k t -> p (a k) t"),
                                 PS[6][:].rearrange("p (k t) -> p k t", k=KD)).then_inc(hT_hi, 1)
                        act.wait_ge(v_stored, 16 * n + 16)
                        for j in range(2):
                            act.wait_ge(v_done, 2 * n + 1 + j)
                            act.copy(vo[:, j * 512:(j + 1) * 512], PS[2 + j][:]).then_inc(v_evac, 1)
                        act.wait_ge(k_stored, 16 * n + 16)
                        for j in range(2):
                            act.wait_ge(kT_done, 2 * n + 1 + j)
                            act.activation(ko[:, 4 * j:4 * j + 4, :].rearrange("p g t -> p (g t)"), PS[4 + j][:],
                                           ACT.Copy, scale=wqk[:, 0:1]).then_inc(kT_evac, 1)
            act.wait_ge(w0_in, 16)
            for s in range(8):
                act.copy(W[0][0][:, s * 512:(s + 1) * 512], accf[:, s * 512:(s + 1) * 512]).then_inc(w_hi, 1)
            act.wait_ge(v_stored, 16 * NT + 16)
            act.wait_ge(k_stored, 16 * NT + 16)
            act.wait_ge(w_lo, 8)

            q_view = lambda hp: PS[hp][:].rearrange("p (h b s) -> p b h s", h=2, b=CB)

            def q_out(hp, j):
                act.wait_ge(q_done, 2 * j + 1 + hp)
                act.copy(qs[:, hp], q_view(hp)).then_inc(q_copy, 1)

            def squares(hp, j):
                act.wait_ge(ss_done, j + 1)
                act.activation(sq[:, hp], q_view(hp), ACT.Square).then_inc(q_sq, 1)
                act.activation(sqb[:, 0, hp], q_view(hp), ACT.Square).then_inc(sq_b1, 1)


            def squares_2(j):
                act.wait_ge(sq_r, j + 1)
                act.copy(sqb[:, 1, 1], sq[:, 1]).then_inc(sq_b2, 1)

            def exps(j):
                for hp in range(2):
                    act.wait_ge(s_sub, 2 * j + 1 + hp)
                    act.activation(pb[:, CB * hp:CB * hp + CB, :], pb[:, CB * hp:CB * hp + CB, :], ACT.Exp).then_inc(
                        s_exp, 1)

            for hp in range(2):
                q_out(hp, 0)
                squares(hp, 0)
            squares_2(0)
            exps(0)

            def act_step(i, w, sl):
                act.wait_ge(s_done, i + 1)
                q_out(0, i + 1)
                squares(0, i + 1)
                act.wait_ge(pT_done, i + 1)
                for bp in range(2):
                    act.copy(pt[0][:, bp, :], PS[2 + bp][:, 0:HG * S]).then_inc(pT_hi, 1)
                q_out(1, i + 1)
                squares(1, i + 1)
                for b2 in range(2):
                    act.wait_ge(pv_done, 2 * i + 3 + b2)
                    act.copy(ah[:, 0, :, b2, :], pv_view(0, b2)).then_inc(a_hi, 1)
                squares_2(i + 1)
                act.wait_ge(o_done, 2 * i + 1)
                act.wait_ge(a_lo, 4 * i + 6)
                for b2 in range(2):
                    act.copy(ah[:, 1, :, b2, :], pv_view(1, b2)).then_inc(a_hi, 1)
                act.wait_ge(wr_in, 16 * i + 16)
                act.copy(w[0][:, bass.ds(sl * 512, 512)] if not isinstance(sl, int) else
                         w[0][:, sl * 512:(sl + 1) * 512], wraw[:]).then_inc(w_hi, 1)
                exps(i + 1)

            with act.Fori(0, KVH // 2) as gg:
                for p in range(2):
                    i0 = 2 * NC * gg + NC * p
                    with act.Fori(0, NC - 1) as t:
                        act_step(i0 + t, W[1 - p], t)
                    act_step(i0 + NC - 1, W[1 - p], NC - 1)

            act.wait_ge(o_done, 2 * STEPS + 1)
            act.wait_ge(shd_in, 16)
            act.copy(W[1][0][:, 0:2048], draw[:]).then_inc(shd_hi, 1)
            act.wait_ge(g_in, 16)
            act.wait_ge(const_dve, 4)
            act.copy(g_hi[:, :, 0:E], graw[:].rearrange("p (k e) -> p k e", k=KD)).then_inc(g_hi_ok, 1)
            with act.Fori(0, NT // 4) as m:
                for q in range(4):
                    act.wait_ge(h2T_done, 4 * m + q + 1)
                    act.copy(hT[:, bass.ds(2 * m + q // 2, 1), 0, :, (q % 2) * P:(q % 2 + 1) * P].rearrange(
                        "p a k t -> p (a k) t"), PS[q][:].rearrange("p (k t) -> p k t", k=KD)).then_inc(h2T_hi, 1)
            for c in range(4):
                act.wait_ge(lg_done, c + 1)
                act.copy(lgT[:, c * 512:(c + 1) * 512], PS[4 + c][0:E, :]).then_inc(lg_evac, 1)
            act.wait_ge(rt_sub, 1)
            act.activation(rb[:], ra[:], ACT.Exp).then_inc(rt_exp, 1)

            def silu_split(c):
                for it in range(4):
                    act.wait_ge(gu_done, 8 * c + 2 * it + 1)
                    act.wait_ge(act_f, 4 * c + it + 2)
                    act.activation(sgt[0][:], PS[2 * (it % 2)][:], ACT.Silu).then_inc(sil, 1)
                    act.wait_ge(act_f, 4 * c + it + 3)
                    act.copy(W[1][1][:, it * 512:(it + 1) * 512], aft[0][:]).then_inc(act_hi, 1)

            with act.Fori(0, 4) as c:
                silu_split(c)

            def xT_out(b, q):
                act.wait_ge(xgT_done, b + 3)
                act.copy(xgT[q][:].rearrange("p k t -> p (k t)"), PS[q][:]).then_inc(xgT_evac, 1)

            def silu(b, q):
                act.wait_ge(eg_done, b + 1)
                act.activation(sge[:], PS[2 + q][:, 0:EI], ACT.Silu).then_inc(e_sil, 1)

            xT_out(0, 0)
            xT_out(1, 1)
            silu(0, 0)
            with act.Fori(0, NB // 2) as m:
                for q in range(2):
                    b = 2 * m + q
                    act.wait_ge(eg_done, b + 1)
                    xT_out(b + 2, q)
                    act.wait_ge(e_act, b + 1)
                    silu(b + 1, 1 - q)

        @block.vector
        def _(dve):
            dve.sem_inc(kn_done, 2)
            dve.sem_inc(a_lo, 4)
            dve.sem_inc(acc_done, 2)
            dve.sem_inc(act_f, 2)
            dve.sem_inc(sh_done, 4)
            dve.sem_inc(ye_ok, 2)
            dve.sem_inc(add2, 2)
            dve.wait_ge(setup_in, 96)
            dve.tensor_tensor(wqk[:], qkw[:, 0:1], qkw[:, 1:2], ALU.mult).then_inc(const_dve, 1)
            dve.wait_ge(ctx_hi, 1)
            dve.tensor_tensor(c_lo[0][:], craw[:], c_hi[0][:], ALU.subtract).then_inc(ctx_lo, 1)
            for j in range(4):
                dve.wait_ge(kvw_hi, j + 1)
                cs = slice((j % 2) * 2048, (j % 2 + 1) * 2048)
                dve.tensor_tensor(W[j // 2][1][:, cs], accf[:, j * 2048:(j + 1) * 2048],
                                  W[j // 2][0][:, cs], ALU.subtract).then_inc(kvw_lo, 1)
            with dve.Fori(0, NC // 2) as m:
                for cp in range(2):
                    for tt in range(2):
                        c = 2 * m + cp
                        n = 4 * m + 2 * cp + tt
                        dve.wait_ge(x_in, 16 * n + 16)
                        dve.bn_stats(st1[:], xt[tt][:]).then_inc(ln_st, 1)
                        dve.wait_ge(ln_st, n + 1)
                        dve.sem_inc(dve_mark, 1)
                        dve.bn_aggr(mv1[:], st1[:]).then_inc(ln_mv, 1)
                        dve.wait_ge(ln_mv, n + 1)
                        dve.tensor_scalar(ve1[:], mv1[:, 1:2], EPS, None, ALU.add).then_inc(ln_var, 1)
                        if tt == 1:
                            dve.wait_ge(ctx_hi, c + 2)
                            dve.tensor_tensor(c_lo[1 - cp][:], craw[:], c_hi[1 - cp][:],
                                              ALU.subtract).then_inc(ctx_lo, 1)
                        dve.wait_ge(ln_rt, n + 1)
                        dve.tensor_scalar(h1[:], xt[tt][:], mv1[:, 0:1], rs1[:, 0:1], ALU.subtract,
                                          ALU.mult).then_inc(h_done, 1)
                        dve.wait_ge(k_sq, 2 * n + 2)
                        dve.tensor_reduce(kss[:], ksq[:].rearrange("p j g d -> p (j g) d"), AX,
                                          ALU.add).then_inc(k_ss, 1)
                        dve.wait_ge(k_ss, n + 1)
                        dve.tensor_scalar(kv_[:], kss[:], 1.0 / HD, EPS, ALU.mult, ALU.add).then_inc(k_var, 1)
                        dve.wait_ge(hT_hi, n + 1)
                        ts = slice(tt * P, (tt + 1) * P)
                        dve.tensor_tensor(hT[:, bass.ds(c, 1), 1, :, ts].rearrange("p a k t -> p (a k) t"),
                                          PS[6][:].rearrange("p (k t) -> p k t", k=KD),
                                          hT[:, bass.ds(c, 1), 0, :, ts].rearrange("p a k t -> p (a k) t"),
                                          ALU.subtract).then_inc(hT_lo, 1)
                        dve.wait_ge(k_rt, n + 1)
                        for j in range(2):
                            dve.tensor_tensor(kn[:, 4 * j:4 * j + 4, :],
                                              PS[j][:].rearrange("p (g d) -> p g d", d=HD),
                                              kr[:, 4 * j:4 * j + 4].unsqueeze(2).to_broadcast([P, 4, HD]),
                                              ALU.mult).then_inc(kn_done, 1)
            for s in range(8):
                dve.wait_ge(w_hi, s + 1)
                cs = slice(s * 512, (s + 1) * 512)
                dve.tensor_tensor(W[0][1][:, cs], accf[:, cs], W[0][0][:, cs], ALU.subtract).then_inc(w_lo, 1)

            def squares_rest(j):
                dve.wait_ge(sq_b1, 2 * j + 2)
                dve.wait_ge(q_sq, 2 * j + 2)
                dve.tensor_tensor(sq[:, 1], sq[:, 1], sqb[:, 0, 1], ALU.subtract).then_inc(sq_r, 1)

            def squares_last(j):
                dve.wait_ge(sq_r, j + 1)
                dve.wait_ge(sq_b2, j + 1)
                dve.tensor_tensor(sqb[:, 2, 1], sq[:, 1], sqb[:, 1, 1], ALU.subtract).then_inc(sq_b3, 1)

            def add_out(count, bp, tile):
                dve.wait_ge(o_done, count)
                dst = accf[:, bass.ds(tile * D, D)] if not isinstance(tile, int) else \
                    accf[:, tile * D:(tile + 1) * D]
                dve.tensor_tensor(dst, PS[6 + bp][:], dst, ALU.add).then_inc(acc_done, 1)

            def a_rest(i, bp):
                for b2 in range(2):
                    dve.wait_ge(a_hi, 4 * i + 5 + 2 * bp + b2)
                    dve.tensor_tensor(al[:, bp, :, b2, :], pv_view(bp, b2), ah[:, bp, :, b2, :],
                                      ALU.subtract).then_inc(a_lo, 1)

            def softmax(j, *meanwhile):
                per_row = lambda t: t[:].unsqueeze(2).to_broadcast([P, 8, S])
                dve.wait_ge(ss_done, j + 2)
                dve.tensor_scalar(qv[:], PS[2][:, 0:8], HD * EPS, None, ALU.add).then_inc(q_var, 1)
                half = lambda t, hp: t[:, CB * hp:CB * hp + CB, :]
                half_row = lambda t, hp: t[:, CB * hp:CB * hp + CB].unsqueeze(2).to_broadcast([P, CB, S])
                if meanwhile:
                    meanwhile[0]()
                dve.wait_ge(q_rt, j + 1)
                dve.wait_ge(s_done, j + 1)
                dve.tensor_tensor(pb[:], PS[3][:].rearrange("p (b s) -> p b s", s=S), per_row(qr),
                                  ALU.mult).then_inc(s_scaled, 1)
                dve.wait_ge(s_scaled, j + 1)
                dve.tensor_tensor(pb[:], pb[:], maskb[:].unsqueeze(1).to_broadcast([P, 8, S]),
                                  ALU.add).then_inc(s_masked, 1)
                dve.wait_ge(s_masked, j + 1)
                dve.tensor_reduce(mx[:], pb[:], AX, ALU.max).then_inc(s_max, 1)
                dve.wait_ge(s_max, j + 1)
                for hp in range(2):
                    dve.tensor_tensor(half(pb, hp), half(pb, hp), half_row(mx, hp), ALU.subtract).then_inc(s_sub, 1)
                if meanwhile:
                    meanwhile[1]()
                dve.wait_ge(s_exp, 2 * j + 2)
                dve.tensor_reduce(sm[:], pb[:], AX, ALU.add).then_inc(s_sum, 1)
                dve.wait_ge(s_sum, j + 1)
                dve.reciprocal(rc[:], sm[:]).then_inc(s_rcp, 1)
                dve.wait_ge(s_rcp, j + 1)
                for hp in range(2):
                    dve.tensor_tensor(half(pb, hp), half(pb, hp), half_row(rc, hp), ALU.mult).then_inc(p_ready, 1)

            def dve_step(i, w, sl, tile, tile_before):
                for bp in range(2):
                    dve.wait_ge(pT_hi, 2 * i + 1 + bp)
                    dve.tensor_tensor(pt[1][:, bp, :], PS[2 + bp][:, 0:HG * S], pt[0][:, bp, :],
                                      ALU.subtract).then_inc(pT_evac, 1)
                squares_rest(i + 1)
                a_rest(i, 0)
                squares_last(i + 1)

                def while_root():
                    add_out(2 * i + 1, 1, tile_before)
                    a_rest(i, 1)

                softmax(i + 1, while_root, lambda: add_out(2 * i + 2, 0, tile))
                dve.wait_ge(w_hi, i + 9)
                ws = bass.ds(sl * 512, 512) if not isinstance(sl, int) else slice(sl * 512, (sl + 1) * 512)
                dve.tensor_tensor(w[1][:, ws], wraw[:], w[0][:, ws], ALU.subtract).then_inc(w_lo, 1)

            dve.wait_ge(v_stored, 16 * NT + 16)
            dve.wait_ge(k_stored, 16 * NT + 16)
            dve.wait_ge(acc_zero, 4)
            squares_rest(0)
            squares_last(0)
            softmax(0)
            with dve.Fori(0, KVH // 2) as gg:
                for p in range(2):
                    i0 = 2 * NC * gg + NC * p
                    dve_step(i0, W[1 - p], 0, 0, NT - 1)
                    with dve.Fori(0, NC - 2) as t:
                        dve_step(i0 + 1 + t, W[1 - p], t + 1, 2 * t + 2, 2 * t + 1)
                    dve_step(i0 + NC - 1, W[1 - p], NC - 1, NT - 2, NT - 3)
            add_out(2 * STEPS + 1, 1, NT - 1)

            dve.wait_ge(const_act, 1)
            dve.wait_ge(acc_done, 2 * STEPS + 3)
            for n in range(NT):
                dve.wait_ge(x3_in, 16 * n + 16)
                dve.scalar_tensor_tensor(out=acc[:, n, :], in0=acc[:, n, :], scalar=tg[:, 0:1], in1=xt3[n % 2][:],
                                         op0=ALU.mult, op1=ALU.add).then_inc(x1_done, 1)
                dve.wait_ge(x1_done, n + 1)
                dve.bn_stats(st3[:, n, :], acc[:, n, :]).then_inc(st_done, 1)
                dve.wait_ge(st_done, n + 1)
                dve.bn_aggr(mv3[:, n, :], st3[:, n, :]).then_inc(mv_done, 1)
            dve.wait_ge(mv_done, NT)
            dve.tensor_scalar(ve3[:], mv3[:, :, 1], EPS, None, ALU.add).then_inc(var3, 1)
            dve.memset(g_hi[:].rearrange("p k e -> p (k e)").bitcast(F32), 0.0).then_inc(const_dve, 1)
            dve.memset(g_lo[:].rearrange("p k e -> p (k e)").bitcast(F32), 0.0).then_inc(const_dve, 1)
            dve.memset(rb[:, 0, :], 0.0).then_inc(const_dve, 1)
            dve.wait_ge(shd_hi, 1)
            dve.tensor_tensor(W[1][0][:, 2048:4096], draw[:], W[1][0][:, 0:2048], ALU.subtract).then_inc(shd_lo, 1)
            dve.wait_ge(g_hi_ok, 1)
            dve.wait_ge(const_dve, 4)
            dve.tensor_tensor(g_lo[:, :, 0:E], graw[:].rearrange("p (k e) -> p k e", k=KD), g_hi[:, :, 0:E],
                              ALU.subtract).then_inc(g_lo_ok, 1)
            dve.wait_ge(rt3, 1)
            with dve.Fori(0, NT // 4) as m:
                for q in range(4):
                    n = 4 * m + q
                    dve.wait_ge(h2_stored[q], 16 * m + 16)
                    dve.tensor_scalar(h2[q][:], acc[:, bass.ds(n, 1), :].rearrange("p a d -> p (a d)"),
                                      mv3[:, bass.ds(n, 1), 0], rs3[:, bass.ds(n, 1)], ALU.subtract,
                                      ALU.mult).then_inc(h2_done, 1)
                for q in range(4):
                    n = 4 * m + q
                    dve.wait_ge(h2T_hi, n + 1)
                    part = [hT[:, bass.ds(2 * m + q // 2, 1), x_, :, (q % 2) * P:(q % 2 + 1) * P].rearrange(
                        "p a k t -> p (a k) t") for x_ in range(2)]
                    dve.tensor_tensor(part[1], PS[q][:].rearrange("p (k t) -> p k t", k=KD), part[0],
                                      ALU.subtract).then_inc(h2T_lo, 1)

            links = [0]

            def link(ins):
                links[0] += 1
                ins.then_inc(rt_dve, 1)
                dve.wait_ge(rt_dve, links[0])

            over_e = lambda t: t.unsqueeze(2).to_broadcast([P, NT, E])
            over_n = lambda t: t.unsqueeze(1).to_broadcast([P, NT, E])
            dve.wait_ge(lgt_done, 1)
            logits = PS[0][:, 0:NT * E].rearrange("p (n e) -> p n e", e=E)
            link(dve.tensor_reduce(rsm[:], logits, AX, ALU.max))
            dve.tensor_tensor(ra[:], logits, over_e(rsm[:]), ALU.subtract).then_inc(rt_sub, 1)
            dve.wait_ge(rt_exp, 1)
            link(dve.tensor_reduce(rsm[:], rb[:], AX, ALU.add))
            link(dve.reciprocal(rsr[:], rsm[:]))
            link(dve.tensor_tensor(rb[:], rb[:], over_e(rsr[:]), ALU.mult))
            for n in range(NT):
                dve.max(m8[:, n, :], rb[:, n, :]).then_inc(mv_done, 1)
            for n in range(NT):
                dve.wait_ge(mv_done, NT + n + 1)
                dve.max_index(i8[:, n, :], m8[:, n, :], rb[:, n, :]).then_inc(st_done, 1)
            link(dve.tensor_tensor(rsm[:], m8[:, :, 0], m8[:, :, 1], ALU.add))
            link(dve.reciprocal(rsr[:], rsm[:]))
            link(dve.tensor_tensor(cw[:, 0, :], m8[:, :, 0], rsr[:], ALU.mult))
            link(dve.tensor_tensor(cw[:, 1, :], m8[:, :, 1], rsr[:], ALU.mult))
            link(dve.tensor_scalar(cw[:], cw[:], tg[:, 1:2], None, ALU.mult))
            dve.wait_ge(st_done, 2 * NT)
            dve.wait_ge(pool_const, 9)
            for s, oh in enumerate((oh1, oh2)):
                link(dve.tensor_copy(slf[:, s, :], i8[:, :, s]))
                link(dve.tensor_tensor(oh[:], over_n(iota_e[:]), over_e(slf[:, s, :]), ALU.is_equal))
            link(dve.tensor_tensor(ra[:], oh1[:], oh2[:], ALU.add))
            link(dve.memset(rb[:, 0, :], 0.0))
            for n in range(NT - 1):
                link(dve.tensor_tensor(rb[:, n + 1, :], rb[:, n, :], ra[:, n, :], ALU.add))
            dve.tensor_tensor(nbk[:], rb[:, NT - 1, :], ra[:, NT - 1, :], ALU.add).then_inc(rank_in, 1)
            dve.wait_ge(rank_done, 1)
            link(dve.tensor_scalar(stb[:], PS[2][:, 0:E], 1.0 / P, None, ALU.mult))
            link(dve.tensor_tensor(rb[:], over_e(stb[:]), over_n(iota_e[:]), ALU.is_gt))
            link(dve.tensor_reduce(nbk[:], rb[:], AX, ALU.add))
            link(dve.tensor_tensor_scan(endb[:], ones[:, 0:E], nbk[:], 0.0, ALU.mult, ALU.add))
            link(dve.tensor_tensor(stb[:], endb[:], nbk[:], ALU.subtract))
            link(dve.tensor_scalar(stb[:], stb[:], float(P), None, ALU.mult))
            link(dve.tensor_tensor(ra[:], PS[1][:, 0:NT * E].rearrange("p (n e) -> p n e", e=E),
                                   over_n(stb[:]), ALU.add))
            for s, oh in enumerate((oh1, oh2)):
                link(dve.tensor_tensor(rb[:], oh[:], ra[:], ALU.mult))
                link(dve.tensor_reduce(slf[:, s, :], rb[:], AX, ALU.add))
            ebt = lgT[0:1, 0:NBX * E].rearrange("p (b e) -> p b e", e=E)
            link(dve.tensor_tensor(ebt, endb[0:1, :].unsqueeze(1).to_broadcast([1, NBX, E]),
                                   iota_b[0:1, :].unsqueeze(2).to_broadcast([1, NBX, E]), ALU.is_le))
            link(dve.tensor_reduce(ebf[:], ebt, AX, ALU.add))
            link(dve.tensor_scalar(ebf[:], ebf[:], float(E - 1), None, ALU.min))
            link(dve.tensor_copy(ebi[:], ebf[:]))
            dve.tensor_copy(sli[:], slf[:]).then_inc(slot_ok, 1)

            def shared(c):
                for it in range(4):
                    dve.wait_ge(sil, 4 * c + it + 1)
                    dve.wait_ge(gu_done, 8 * c + 2 * it + 2)
                    if it >= 1:
                        dve.wait_ge(act_lo, 4 * c + it)
                    dve.tensor_tensor(aft[0][:], PS[2 * (it % 2) + 1][:], sgt[0][:], ALU.mult).then_inc(act_f, 1)
                    dve.wait_ge(act_f, 4 * c + it + 3)
                    dve.wait_ge(act_hi, 4 * c + it + 1)
                    dve.tensor_tensor(W[1][1][:, 2048 + it * 512:2048 + (it + 1) * 512], aft[0][:],
                                      W[1][1][:, it * 512:(it + 1) * 512], ALU.subtract).then_inc(act_lo, 1)
                for tl in range(4):
                    dve.wait_ge(dn_done, 4 * c + tl + 1)
                    n = 4 * c + tl
                    dst = accf[:, n * D:(n + 1) * D] if isinstance(n, int) else accf[:, bass.ds(n * D, D)]
                    dve.scalar_tensor_tensor(out=dst, in0=PS[4 + tl][:], scalar=tg[:, 1:2], in1=dst,
                                             op0=ALU.mult, op1=ALU.add).then_inc(sh_done, 1)

            with dve.Fori(0, 3) as c:
                shared(c)
            dve.wait_ge(srow_in, 16)
            dve.tensor_copy(srowf[:], srow[:]).then_inc(srow_f, 1)
            dve.wait_ge(srowT, 1)
            dve.tensor_copy(sidx[:, 0:NB], PS[7][:, 0:NB]).then_inc(sidx_ok, 1)
            shared(3)

            def gated(b, q):
                dve.wait_ge(e_sil, b + 1)
                dve.tensor_tensor(acte[:], PS[2 + q][:, EI:2 * EI], sge[:], ALU.mult).then_inc(e_act, 1)

            gated(0, 0)
            with dve.Fori(0, NB // 2) as m:
                for q in range(2):
                    b = 2 * m + q
                    dve.wait_ge(eT_done, b + 1)
                    dve.tensor_copy(acteT[:], PS[4][:, 0:P]).then_inc(eT_evac, 1)
                    gated(b + 1, 1 - q)
                    dve.wait_ge(ed_done, b + 1)
                    dve.wait_ge(y_st[q], 16 * m + 16)
                    dve.tensor_copy(ye[q][:], PS[5 + q][:]).then_inc(ye_ok, 1)

            with dve.Fori(0, NT // 2) as m:
                for q in range(2):
                    n = 2 * m + q
                    row = acc[:, bass.ds(n, 1), :].rearrange("p a d -> p (a d)")
                    dve.wait_ge(y1_in[q], 16 * m + 16)
                    dve.scalar_tensor_tensor(out=row, in0=y1[q][:], scalar=cw[:, 0, bass.ds(n, 1)], in1=row,
                                             op0=ALU.mult, op1=ALU.add).then_inc(add1, 1)
                    dve.wait_ge(add1, n + 1)
                    dve.wait_ge(y2_in[q], 16 * m + 16)
                    dve.scalar_tensor_tensor(out=row, in0=y2[q][:], scalar=cw[:, 1, bass.ds(n, 1)], in1=row,
                                             op0=ALU.mult, op1=ALU.add).then_inc(add2, 1)


def kernel(**inputs):
    import numpy as np
    import concourse.bacc as bacc
    from concourse.bass_utils import run_bass_kernel_spmd

    a = {k: np.asarray(v) for k, v in inputs.items()}
    pt = np.ascontiguousarray

    def by_k(w):
        return w.reshape(w.shape[0], KD, P).transpose(2, 1, 0)

    def halves(w):
        return pt(by_k(w).reshape(P, KD, 2, 512).transpose(0, 2, 1, 3).reshape(P, 4096))

    wq = a["L0_xattn_Wq"].reshape(KVH, HG * HD, KD, P).transpose(0, 3, 2, 1).reshape(KVH, P, 2048)
    wo = a["L0_xattn_Wo"].reshape(D, KVH, HG, HD).transpose(1, 3, 2, 0).reshape(KVH, P, 2048)
    shared = by_k(a["L0_ffn_shared_w_gate_up"]).reshape(1, P, 4096)
    w_att = np.concatenate([np.concatenate([wq, wo], axis=2), shared], axis=0)
    w_att = w_att.reshape(KVH + 1, P, NC, 512).transpose(0, 2, 1, 3).reshape(-1, P, 512)
    arrays = {
        "x": pt(a["x"].reshape(NT, P, D)),
        "ctxT": pt(a["ctx_4096"].reshape(NC, CT, KD, P).transpose(0, 3, 2, 1)),
        "wk": halves(a["L0_xattn_Wk"]),
        "wv": halves(a["L0_xattn_Wv"]),
        "w_att": pt(w_att),
        "w_shd": pt(a["L0_ffn_shared_w_down"].reshape(D, SI // P, P).transpose(2, 1, 0).reshape(P, 2048)),
        "mask": pt(a["mask_1x1xSxS2_ff0"].reshape(S, S)),
        "g_x": pt(a["g_xattn"].reshape(1, 1)),
        "g_f": pt(a["g_ffn"].reshape(1, 1)),
        "q_w": pt(a["L0_xattn_q_norm_w"].reshape(HD, 1)),
        "k_w": pt(a["L0_xattn_k_norm_w"].reshape(HD, 1)),
        "gate": pt(by_k(a["L0_ffn_gate_w"]).reshape(P, KD * E)),
        "w_gu": pt(a["L0_ffn_w_gate_up"].reshape(E, 2 * EI, KD, P).transpose(0, 3, 2, 1).reshape(E, P, KD * 2 * EI)),
        "w_dn": pt(a["L0_ffn_w_down"].transpose(0, 2, 1)),
    }
    nc = bacc.Bacc("TRN2", target_bir_lowering=False, num_devices=1)
    aps = {k: nc.dram_tensor(f"in_{k}", v.shape, mybir.dt.from_np(v.dtype), kind="ExternalInput").ap()
           for k, v in arrays.items()}
    out = nc.dram_tensor("out_0", (NT, P, D), F32, kind="ExternalOutput").ap()
    build(nc, **aps, out=out)
    r = run_bass_kernel_spmd(nc, [{f"in_{k}": v for k, v in arrays.items()}], core_ids=[0])
    return np.asarray(r.results[0]["out_0"]).reshape(B, S, D)
```

```python
from contextlib import ExitStack

import numpy as np

import concourse.bass as bass
from concourse import mybir

F32 = mybir.dt.float32
F32R = mybir.dt.float32r
BF16 = mybir.dt.bfloat16
I32 = mybir.dt.int32
U32 = mybir.dt.uint32
ALU = mybir.AluOpType
ACT = mybir.ActivationFunctionType
AX = mybir.AxisListType.X

P = 128
B, S, D = 32, 64, 512
T = B * S
KD = D // P
H, KVH, HD = 32, 8, 128
HG = H // KVH
NT = T // P
CT = 2 * P
NC = T // CT
CB = CT // S
STEPS = KVH * NC
E, EI = 16, 128
SI = 512
NB = (2 * T + E * (P - 1)) // P + 1
NBX = NB + 2
EPS = 1e-5


def build(nc, x, ctxT, wk, wv, w_att, w_shd, mask, g_x, g_f, q_w, k_w, gate, w_gu, w_dn, out):
    kbuf = nc.dram_tensor("kbuf", [STEPS, P, CT], F32, kind="Internal").ap()
    vbuf = nc.dram_tensor("vbuf", [STEPS, P, CT], F32, kind="Internal").ap()
    h2buf = nc.dram_tensor("h2buf", [T, D], F32, kind="Internal").ap()
    ybuf = nc.dram_tensor("ybuf", [NB * P, D], F32, kind="Internal").ap()
    slotbuf = nc.dram_tensor("slotbuf", [NB * P, 1], I32, kind="Internal").ap()
    k_st = kbuf.rearrange("(g c) p (b t) -> c b p g t", g=KVH, b=2)
    v_st = vbuf.rearrange("(g c) p (b t) -> c b p g t", g=KVH, b=2)
    h2_t = h2buf.rearrange("(n p) d -> n p d", p=P)
    y_t = ybuf.rearrange("(n p) d -> n p d", p=P)

    with ExitStack() as ctx:
        def sb(name, shape, dt=F32, stack=ctx):
            return stack.enter_context(nc.sbuf_tensor(name, shape, dt))

        def sem(name):
            return ctx.enter_context(nc.semaphore(name))

        ident = sb("ident", [P, P])
        mhalf = sb("mhalf", [P, 16])
        maskb = sb("maskb", [P, S])
        gcol = sb("gcol", [P, 2])
        tg = sb("tg", [P, 2])
        qkw = sb("qkw", [P, 2])
        wqk = sb("wqk", [P, 1])
        tok = sb("tok", [P, NT], I32)
        tri = sb("tri", [P, P])
        trib = sb("trib", [P, P], BF16)
        onesb = sb("onesb", [P, P], BF16)
        ones = sb("ones", [P, E])
        iota_e = sb("iota_e", [P, E])
        iota_b = sb("iota_b", [P, NBX])
        sidx = sb("sidx", [P, NBX], I32)
        zi = sb("zi", [P, NB], I32)
        acc = sb("acc", [P, NT, D])
        accf = acc[:].rearrange("p n d -> p (n d)")
        with ExitStack() as a:
            hT = sb("hT", [P, NC, 2, KD, CT], F32R, a)
        wgu = sb("wgu", [P, E, KD * 2 * EI])
        with ExitStack() as a:
            W = [[sb(f"w{p}{'hl'[q]}", [P, 4096], F32R, a) for q in range(2)] for p in range(2)]
        with ExitStack() as a:
            xg = [sb(f"xg{q}", [P, D], F32, a) for q in range(2)]
            xgT = [sb(f"xgT{q}", [P, KD, P], F32, a) for q in range(2)]
            sge = sb("sge", [P, EI], F32, a)
            acte = sb("acte", [P, EI], F32, a)
            acteT = sb("acteT", [P, P], F32, a)
            ye = [sb(f"ye{q}", [P, D], F32, a) for q in range(2)]
            y1 = [sb(f"y1{q}", [P, D], F32, a) for q in range(4)]
            y2 = [sb(f"y2{q}", [P, D], F32, a) for q in range(4)]
        wpad = sb("wpad", [P, 4 * 4096])
        with ExitStack() as a:
            craw = sb("craw", [P, KD, CT], F32, a)
            c_hi = [sb(f"c_hi{q}", [P, KD, CT], F32R, a) for q in range(2)]
            c_lo = [sb(f"c_lo{q}", [P, KD, CT], F32R, a) for q in range(2)]
            vo = sb("vo", [P, KVH * HD], F32, a)
            kn = sb("kn", [P, KVH, HD], F32, a)
            ko = sb("ko", [P, KVH, P], F32, a)
            ksq = sb("ksq", [P, 2, 4, HD], F32, a)
            kss = sb("kss", [P, KVH], F32, a)
            kv_ = sb("kv_", [P, KVH], F32, a)
            kr = sb("kr", [P, KVH], F32, a)
            xt = [sb(f"xt{q}", [P, D], F32, a) for q in range(2)]
            h1 = sb("h1", [P, D], F32, a)
            st1 = sb("st1", [P, 6], F32, a)
            mv1 = sb("mv1", [P, 2], F32, a)
            ve1 = sb("ve1", [P, 1], F32, a)
            rs1 = sb("rs1", [P, 1], F32, a)
        with ExitStack() as a:
            qs = sb("qs", [P, 2, CB, 2, S], F32, a)
            sq = sb("sq", [P, 2, CB, 2, S], F32, a)
            pb = sb("pb", [P, 8, S], F32, a)
            sqb = sb("sqb", [P, 3, 2, CB, 2, S], BF16, a)
            pt = [sb(f"pt{'hl'[q]}", [P, 2, HG * S], F32R, a) for q in range(2)]
            ah = sb("ah", [P, 2, HG, 2, S], F32R, a)
            al = sb("al", [P, 2, HG, 2, S], F32R, a)
            kt = sb("kt", [P, CB, S], F32, a)
            vt = sb("vt", [P, 2, HD], F32, a)
            wraw = sb("wraw", [P, 512], F32, a)
            vhl = [sb(f"vt{'hl'[q]}", [P, 2, HD], F32R, a) for q in range(2)]
            onec = sb("onec", [P, 1], BF16, a)
            qv = sb("qv", [P, 8], F32, a)
            qr = sb("qr", [P, 8], F32, a)
            mx = sb("mx", [P, 8], F32, a)
            sm = sb("sm", [P, 8], F32, a)
            rc = sb("rc", [P, 8], F32, a)
        with ExitStack() as a:
            h2 = [sb(f"h2{q}", [P, D], F32, a) for q in range(4)]
            draw = sb("draw", [P, 4 * D], F32, a)
            lgT = sb("lgT", [E, T], F32, a)
        wdn = sb("wdn", [P, E, D])
        m8 = sb("m8", [P, NT, 8])
        i8 = sb("i8", [P, NT, 8], U32)
        rsm = sb("rsm", [P, NT])
        rsr = sb("rsr", [P, NT])
        cw = sb("cw", [P, 2, NT])
        slf = sb("slf", [P, 2, NT])
        sli = sb("sli", [P, 2, NT], I32)
        nbk = sb("nbk", [P, E])
        endb = sb("endb", [P, E])
        stb = sb("stb", [P, E])
        ebf = sb("ebf", [1, NBX])
        ebi = sb("ebi", [1, NBX], I32)
        srow = sb("srow", [NB, P], I32)
        srowf = sb("srowf", [NB, P])
        icur = [sb(f"icur{q}", [P, 1], I32) for q in range(2)]
        st3 = sb("st3", [P, NT, 6])
        mv3 = sb("mv3", [P, NT, 2])
        ve3 = sb("ve3", [P, NT])
        rs3 = sb("rs3", [P, NT])
        graw = sb("graw", [P, KD * E])
        with ExitStack() as a:
            g_hi = sb("g_hi", [P, KD, P], F32R, a)
            g_lo = sb("g_lo", [P, KD, P], F32R, a)
        ra = sb("ra", [P, NT, E])
        rb = sb("rb", [P, NT, E])
        oh1 = sb("oh1", [P, NT, E])
        oh2 = sb("oh2", [P, NT, E])
        sgt = [sb(f"sgt{q}", [P, D]) for q in range(1)]
        aft = [sb(f"aft{q}", [P, D]) for q in range(1)]
        rab = sb("rab", [P, NT, E], BF16)
        xt3 = (sgt[0], aft[0])

        PS = [ctx.enter_context(nc.psum_tensor(f"ps{q}", [P, 512], F32)) for q in range(8)]

        setup_in, ident_ok, pool_const, const_act, const_dve = (
            sem("setup_in"), sem("ident_ok"), sem("pool_const"), sem("const_act"), sem("const_dve"))
        ctx_in, x_in, k_stored, v_stored = sem("ctx_in"), sem("x_in"), sem("k_stored"), sem("v_stored")
        kvw_in = [sem(f"kvw_in{q}") for q in range(4)]
        kvw_hi, kvw_lo, ctx_hi, ctx_lo = sem("kvw_hi"), sem("kvw_lo"), sem("ctx_hi"), sem("ctx_lo")
        k_done, k_sq, k_ss, k_var, k_rt, kn_done = (
            sem("k_done"), sem("k_sq"), sem("k_ss"), sem("k_var"), sem("k_rt"), sem("kn_done"))
        v_done, v_evac, kT_done, kT_evac = sem("v_done"), sem("v_evac"), sem("kT_done"), sem("kT_evac")
        ln_st, ln_mv, ln_var, ln_rt, h_done, hT_done, hT_hi, hT_lo = (
            sem("ln_st"), sem("ln_mv"), sem("ln_var"), sem("ln_rt"), sem("h_done"), sem("hT_done"),
            sem("hT_hi"), sem("hT_lo"))
        w0_in, w_hi, w_lo, acc_zero = sem("w0_in"), sem("w_hi"), sem("w_lo"), sem("acc_zero")
        wr_in, kt_in, vt_in = sem("wr_in"), sem("kt_in"), sem("vt_in")
        q_done, q_copy, q_sq, ss_done, q_var, q_rt = (
            sem("q_done"), sem("q_copy"), sem("q_sq"), sem("ss_done"), sem("q_var"), sem("q_rt"))
        s_done, s_scaled, s_masked, s_max, s_sub, s_exp, s_sum, s_rcp, p_ready = (
            sem("s_done"), sem("s_scaled"), sem("s_masked"), sem("s_max"), sem("s_sub"), sem("s_exp"),
            sem("s_sum"), sem("s_rcp"), sem("p_ready"))
        sq_pool, sq_b1, sq_r, sq_b2, sq_b3, v_split, pT_hi = (
            sem("sq_pool"), sem("sq_b1"), sem("sq_r"), sem("sq_b2"), sem("sq_b3"), sem("v_split"), sem("pT_hi"))
        pT_done, pT_evac, pv_done, a_hi, a_lo, o_done, acc_done = (
            sem("pT_done"), sem("pT_evac"), sem("pv_done"), sem("a_hi"), sem("a_lo"), sem("o_done"),
            sem("acc_done"))
        x3_in, x1_done, st_done, mv_done, var3, rt3, h2_done, h2_stored, h2T_done, h2T_hi, h2T_lo = (
            [sem("x3_in0"), sem("x3_in1")], sem("x1_done"), sem("st_done"), sem("mv_done"), sem("var3"), sem("rt3"),
            sem("h2_done"), [sem(f"h2_stored{q}") for q in range(4)], sem("h2T_done"), sem("h2T_hi"), sem("h2T_lo"))
        shd_in, shd_hi, shd_lo = sem("shd_in"), sem("shd_hi"), sem("shd_lo")
        g_in, g_hi_ok, g_lo_ok, lg_done, lg_evac, lgt_done = (
            sem("g_in"), sem("g_hi_ok"), sem("g_lo_ok"), sem("lg_done"), sem("lg_evac"), sem("lgt_done"))
        tri_ok, rank_out = sem("tri_ok"), sem("rank_out")
        rt_sub, rt_exp, rt_dve, rank_in, rank_done, slot_ok = (
            sem("rt_sub"), sem("rt_exp"), sem("rt_dve"), sem("rank_in"), sem("rank_done"), sem("slot_ok"))
        zero_st, scat, srow_in, srow_f, srowT, sidx_ok = (
            sem("zero_st"), sem("scat"), sem("srow_in"), sem("srow_f"), sem("srowT"),
            sem("sidx_ok"))
        gu_done, sil, act_f, act_hi, act_lo, dn_done, sh_done = (
            sem("gu_done"), sem("sil"), sem("act_f"), sem("act_hi"), sem("act_lo"), sem("dn_done"),
            sem("sh_done"))
        wgu_in, wdn_in = sem("wgu_in"), sem("wdn_in")
        ic_ok, xg_in, xgT_done, xgT_evac, eg_done, e_sil, e_act, eT_done, eT_evac, ed_done, ye_ok, y_st = (
            sem("ic_ok"), [sem("xg_in0"), sem("xg_in1")], sem("xgT_done"), sem("xgT_evac"), sem("eg_done"),
            sem("e_sil"), sem("e_act"), sem("eT_done"), sem("eT_evac"), sem("ed_done"), sem("ye_ok"),
            [sem("y_st0"), sem("y_st1")])
        y1_in, y2_in, add1, add2, out_st = (
            [sem(f"y1_in{q}") for q in range(4)], [sem(f"y2_in{q}") for q in range(4)], sem("add1"), sem("add2"), sem("out_st"))

        dve_mark, pool_mark = sem("dve_mark"), sem("pool_mark")

        block = ctx.enter_context(nc.Block())

        @block.sync
        def _(sp):
            for s in (v_stored, k_stored, *y_st, *h2_stored):
                sp.sem_inc(s, 16)
            for j, g in enumerate((g_x, g_f)):
                sp.dma_start(gcol[:, j:j + 1], g.to_broadcast([P, 1])).then_inc(setup_in, 16)
            sp.dma_start(qkw[:, 0:1], q_w).then_inc(setup_in, 16)
            sp.dma_start(qkw[:, 1:2], k_w).then_inc(setup_in, 16)
            for j in range(2):
                sp.dma_start(maskb[j * S:(j + 1) * S, :], mask).then_inc(setup_in, 16)
            sp.dma_start(craw[:], ctxT[0]).then_inc(ctx_in, 16)
            for j in range(4):
                src = (wk, wv)[j // 2][:, (j % 2) * 2048:(j % 2 + 1) * 2048]
                sp.dma_start(accf[:, j * 2048:(j + 1) * 2048], src).then_inc(kvw_in[j], 16)
            sp.dma_start(xt[0][:], x[0]).then_inc(x_in, 16)
            for n in range(NT):
                if n + 1 < NT:
                    if n >= 1:
                        sp.wait_ge(h_done, n)
                    sp.wait_ge(x_in, 16 * (n + 1))
                    sp.dma_start(xt[(n + 1) % 2][:], x[n + 1]).then_inc(x_in, 16)
                if n % 2 == 0:
                    c = n // 2 + 1
                    sp.wait_ge(ctx_hi, c)
                    sp.wait_ge(ctx_lo, c)
                    sp.dma_start(craw[:], ctxT[c % NC]).then_inc(ctx_in, 16)
                if n == 1:
                    sp.wait_ge(kvw_lo, 2)
                    sp.dma_start(accf[:, 0:4096].rearrange("p (s n) -> p s n", s=NC),
                                 w_att[0:NC].rearrange("s p n -> p s n")).then_inc(w0_in, 16)
                sp.wait_ge(v_evac, 2 * n + 4)
                sp.dma_start(v_st[n // 2, n % 2], vo[:].rearrange("p (g t) -> p g t", g=KVH)).then_inc(v_stored, 16)
                sp.wait_ge(kT_evac, 2 * n + 4)
                sp.dma_start(k_st[n // 2, n % 2], ko[:]).then_inc(k_stored, 16)
            sp.wait_ge(v_stored, 16 * NT + 16)
            sp.wait_ge(k_stored, 16 * NT + 16)
            sp.wait_ge(w_hi, 8)
            sp.wait_ge(w_lo, 8)
            sp.dma_start(kt[:].rearrange("p b t -> p (b t)"), kbuf[0]).then_inc(kt_in, 16)
            sp.dma_start(vt[:].rearrange("p b t -> p (b t)"), vbuf[0]).then_inc(vt_in, 16)
            sp.dma_start(graw[:], gate).then_inc(g_in, 16)

            def next_loads(i, x_tiles=None):
                sp.wait_ge(s_done, i + 1)
                sp.dma_start(kt[:].rearrange("p b t -> p (b t)"), kbuf[i + 1]).then_inc(kt_in, 16)
                sp.wait_ge(v_split, 2 * i + 2)
                sp.dma_start(vt[:].rearrange("p b t -> p (b t)"), vbuf[i + 1]).then_inc(vt_in, 16)
                if x_tiles is not None:
                    x_tiles()
                sp.wait_ge(w_hi, i + 8)
                sp.wait_ge(w_lo, i + 8)
                sp.dma_start(wraw[:], w_att[i + NC]).then_inc(wr_in, 16)

            with sp.Fori(0, STEPS - NC) as i:
                next_loads(i)
            next_loads(STEPS - NC)
            sp.dma_start(xt3[0][:], x[0]).then_inc(x3_in[0], 16)
            sp.dma_start(xt3[1][:], x[1]).then_inc(x3_in[1], 16)
            next_loads(STEPS - NC + 1)
            with sp.Fori(0, NC - 3) as t:
                def x_tiles():
                    for q in range(2):
                        sp.wait_ge(x1_done, 2 * t + 1 + q)
                        sp.dma_start(xt3[q][:], x[2 * t + 2 + q]).then_inc(x3_in[q], 16)

                next_loads(t + STEPS - NC + 2, x_tiles)
            sp.wait_ge(w_hi, STEPS + 7)
            sp.wait_ge(w_lo, STEPS + 7)
            sp.dma_start(wraw[:], w_att[STEPS - 1 + NC]).then_inc(wr_in, 16)
            sp.wait_ge(pT_done, STEPS)
            sp.dma_start(draw[:], w_shd).then_inc(shd_in, 16)
            sp.dma_start(slotbuf.rearrange("(p b) o -> p (b o)", p=P), zi[:]).then_inc(zero_st, 16)
            for n in range(2 * (NC - 2), NT):
                sp.wait_ge(x1_done, n - 1)
                sp.dma_start(xt3[n % 2][:], x[n]).then_inc(x3_in[n % 2], 16)
            with sp.Fori(0, NT // 4) as m:
                for q in range(4):
                    sp.wait_ge(h2_done, 4 * m + q + 1)
                    sp.dma_start(h2_t[4 * m + q], h2[q][:]).then_inc(h2_stored[q], 16)
            for q in range(4):
                sp.wait_ge(h2_stored[q], 16 * (NT // 4) + 16)
            sp.wait_ge(shd_lo, 1)
            sp.wait_ge(slot_ok, 1)
            sp.dma_start(wdn[:], w_dn.rearrange("e p n -> p e n")).then_inc(wdn_in, 16)
            def load_gate_up(c):
                sp.wait_ge(gu_done, 8 * c + 8)
                sp.dma_start(wgu[:, bass.ds(4 * c, 4), :],
                             w_gu[bass.ds(4 * c, 4)].rearrange("e p n -> p e n")).then_inc(wgu_in, 16)

            with sp.Fori(0, 3) as c:
                load_gate_up(c)
            sp.wait_ge(scat, 16 * 2 * NT)
            sp.dma_start(srow[:], slotbuf.rearrange("(b p) o -> b (p o)", p=P)).then_inc(srow_in, 16)
            load_gate_up(3)
            with sp.Fori(0, NB // 2) as bb:
                for q in range(2):
                    b = 2 * bb + q
                    sp.wait_ge(ye_ok, b + 3)
                    sp.dma_start(y_t[b], ye[q][:]).then_inc(y_st[q], 16)
            with sp.Fori(0, NT) as n:
                sp.wait_ge(add2, n + 1)
                sp.dma_start(out[n], acc[:, n, :]).then_inc(out_st, 16)
            sp.wait_ge(out_st, 16 * NT)
            sp.wait_ge(wdn_in, 16)

        @block.gpsimd
        def _(pool):
            pool.memset(mhalf[:], -0.5).then_inc(pool_const, 1)
            pool.memset(ident[:], 0.0).then_inc(ident_ok, 1)
            pool.wait_ge(ident_ok, 1)
            pool.affine_select(out=ident[:], in_=ident[:], compare_op=ALU.not_equal, fill=1.0, base=0,
                               pattern=[[-1, P]], channel_multiplier=1).then_inc(ident_ok, 1)
            pool.memset(zi[:], 0).then_inc(pool_const, 1)
            pool.memset(sidx[:], 0).then_inc(pool_const, 1)
            pool.memset(ones[:], 1.0).then_inc(pool_const, 1)
            pool.memset(onesb[:], 1.0).then_inc(pool_const, 1)
            pool.memset(tri[:], 1.0).then_inc(pool_const, 1)
            pool.wait_ge(pool_const, 6)
            pool.affine_select(out=tri[:], in_=tri[:], compare_op=ALU.is_gt, fill=0.0, base=0,
                               pattern=[[1, P]], channel_multiplier=-1).then_inc(pool_const, 1)
            pool.iota(iota_e[:], pattern=[[1, E]], base=0, channel_multiplier=0,
                      allow_small_or_imprecise_dtypes=True).then_inc(pool_const, 1)
            pool.iota(iota_b[:], pattern=[[1, NBX]], base=0, channel_multiplier=0,
                      allow_small_or_imprecise_dtypes=True).then_inc(pool_const, 1)
            pool.iota(tok[:], pattern=[[P, NT]], base=0, channel_multiplier=1).then_inc(pool_const, 1)
            pool.wait_ge(pool_const, 10)
            with pool.Fori(0, NT) as n:
                pool.wait_ge(ln_var, n + 1)
                pool.tensor_tensor(rs1[:], ve1[:], mhalf[:, 0:1], ALU.pow).then_inc(ln_rt, 1)
                pool.wait_ge(k_var, n + 1)
                pool.tensor_tensor(kr[:], kv_[:], mhalf[:, 0:KVH], ALU.pow).then_inc(k_rt, 1)
            pool.wait_ge(w_hi, 8)
            pool.wait_ge(w_lo, 8)
            pool.wait_ge(v_stored, 16 * NT + 16)
            pool.wait_ge(k_stored, 16 * NT + 16)
            pool.memset(onec[:], 1.0).then_inc(acc_zero, 1)
            for t in (ah, al):
                pool.memset(t[:, 1].rearrange("p h b s -> p (h b s)").bitcast(F32), 0.0).then_inc(acc_zero, 1)
            pool.memset(accf, 0.0).then_inc(acc_zero, 1)

            def split_squares(j):
                flat = lambda t: t.rearrange("p b h s -> p (b h s)")
                part = [flat(sqb[:, z, 0]) for z in range(3)]
                pool.wait_ge(q_sq, 2 * j + 1)
                pool.wait_ge(sq_b1, 2 * j + 1)
                pool.tensor_tensor(flat(sq[:, 0]), flat(sq[:, 0]), part[0], ALU.subtract).then_inc(sq_pool, 1)
                pool.wait_ge(sq_pool, 3 * j + 1)
                pool.sem_inc(pool_mark, 1)
                pool.tensor_copy(part[1], flat(sq[:, 0])).then_inc(sq_pool, 1)
                pool.wait_ge(sq_pool, 3 * j + 2)
                pool.tensor_tensor(part[2], flat(sq[:, 0]), part[1], ALU.subtract).then_inc(sq_pool, 1)

            def inverse_root(j):
                pool.wait_ge(q_var, j + 1)
                pool.tensor_tensor(qr[:], qv[:], mhalf[:, 0:8], ALU.pow).then_inc(q_rt, 1)

            with pool.Fori(0, STEPS) as j:
                split_squares(j)
                inverse_root(j)
                pool.wait_ge(vt_in, 16 * j + 16)
                pool.wait_ge(pv_done, 2 * j + 2)
                pool.sem_inc(pool_mark, 1)
                pool.tensor_copy(vhl[0][:], vt[:]).then_inc(v_split, 1)
                pool.wait_ge(v_split, 2 * j + 1)
                pool.tensor_tensor(vhl[1][:], vt[:], vhl[0][:], ALU.subtract).then_inc(v_split, 1)
            for z in range(2):
                ts = slice(z * 8, z * 8 + 8)
                pool.wait_ge(var3, z + 1)
                pool.tensor_tensor(rs3[:, ts], ve3[:, ts], mhalf[:, 0:8], ALU.pow).then_inc(rt3, 1)
            pool.wait_ge(shd_hi, 1)
            pool.wait_ge(o_done, 2 * STEPS + 1)
            pool.tensor_tensor(W[1][0][:, 2048:4096], draw[:], W[1][0][:, 0:2048], ALU.subtract).then_inc(shd_lo, 1)
            pool.wait_ge(slot_ok, 1)
            pool.wait_ge(zero_st, 16)
            for s in range(2):
                for n in range(NT):
                    pool.indirect_dma_start(slotbuf, bass.IndirectOffsetOnAxis(sli[:, s, n:n + 1], 0),
                                            tok[:, n:n + 1], None).then_inc(scat, 16)
            pool.wait_ge(sidx_ok, 1)
            for q in range(4):
                pool.wait_ge(h2_stored[q], 16 * (NT // 4) + 16)
            pool.wait_ge(gu_done, 32)
            with pool.Fori(0, NBX // 2) as m:
                for q in range(2):
                    b = 2 * m + q
                    pool.wait_ge(xgT_done, b + 1)
                    pool.tensor_copy(icur[q][:], sidx[:, bass.ds(b, 1)]).then_inc(ic_ok, 1)
                    pool.wait_ge(ic_ok, b + 1)
                    pool.sem_inc(pool_mark, 1)
                    pool.indirect_dma_start(xg[q][:], None, h2buf,
                                            bass.IndirectOffsetOnAxis(icur[q][:, 0:1], 0)).then_inc(xg_in[q], 16)
            pool.wait_ge(y_st[0], 16 * (NB // 2) + 16)
            pool.wait_ge(y_st[1], 16 * (NB // 2) + 16)
            for n in range(NT):
                if n >= 4:
                    pool.wait_ge(add2, n - 3)
                for s, (y, y_in) in enumerate(((y1, y1_in), (y2, y2_in))):
                    pool.indirect_dma_start(y[n % 4][:], None, ybuf,
                                            bass.IndirectOffsetOnAxis(sli[:, s, n:n + 1], 0)).then_inc(y_in[n % 4], 16)

        def pv_view(bp, b2):
            return PS[4 + b2][:, bp * 256:(bp + 1) * 256].rearrange("p (h s) -> p h s", s=S)

        def split_product(pe, dst, l_hi, l_lo, r_hi, r_lo, first, last):
            pe.matmul(dst, l_hi, r_lo, start=first, stop=False)
            pe.matmul(dst, l_lo, r_hi, start=False, stop=False)
            return pe.matmul(dst, l_hi, r_hi, start=False, stop=last)

        @block.tensor
        def _(pe):
            pe.wait_ge(ident_ok, 2)
            pe.sem_inc(xgT_done, 2)
            pe.sem_inc(ss_done, 1)
            pe.sem_inc(pv_done, 2)

            def kv_half(j, cp, tt):
                for k in range(KD):
                    w = slice((j % 2) * 2048 + k * 512, (j % 2) * 2048 + (k + 1) * 512)
                    ts = slice(tt * P, (tt + 1) * P)
                    mm = split_product(pe, PS[j][:], c_hi[cp][:, k, ts], c_lo[cp][:, k, ts],
                                       W[j // 2][0][:, w], W[j // 2][1][:, w], k == 0, k == KD - 1)
                return mm

            with pe.Fori(0, NC // 2) as m:
                for cp in range(2):
                    for tt in range(2):
                        c = 2 * m + cp
                        n = 4 * m + 2 * cp + tt
                        if tt == 0:
                            pe.wait_ge(ctx_hi, c + 1)
                            pe.wait_ge(ctx_lo, c + 1)
                        for j in range(2):
                            pe.wait_ge(kvw_lo, j + 1)
                            pe.wait_ge(kn_done, 2 * n + 1 + j)
                            kv_half(j, cp, tt).then_inc(k_done, 1)
                        pe.wait_ge(h_done, n + 1)
                        for k in range(KD):
                            mm = pe.transpose(PS[6][:, k * P:(k + 1) * P], h1[:, k * P:(k + 1) * P], ident[:])
                        mm.then_inc(hT_done, 1)
                        for j in range(2):
                            pe.wait_ge(kvw_lo, j + 3)
                            pe.wait_ge(v_evac, 2 * n + 1 + j)
                            kv_half(2 + j, cp, tt).then_inc(v_done, 1)
                        for j in range(2):
                            pe.wait_ge(kn_done, 2 * n + 3 + j)
                            pe.wait_ge(kT_evac, 2 * n + 1 + j)
                            for q in range(4):
                                mm = pe.transpose(PS[4 + j][:, q * P:(q + 1) * P], kn[:, 4 * j + q, :], ident[:])
                            mm.then_inc(kT_done, 1)

            def q_head(hp, h, chunk, w):
                for k in range(KD):
                    c0 = k * 512 + (2 * hp + h) * P
                    hc = [hT[:, bass.ds(chunk, 1), x_, k, :].rearrange("p a t -> p (a t)") for x_ in range(2)]
                    mm = split_product(pe, PS[hp][:, h * CT:(h + 1) * CT], w[0][:, c0:c0 + P],
                                       w[1][:, c0:c0 + P], hc[0], hc[1], k == 0, k == KD - 1)
                return mm

            def scores(j):
                pe.wait_ge(q_copy, 2 * j + 2)
                pe.wait_ge(kt_in, 16 * j + 16)
                for hp in range(2):
                    for b in range(CB):
                        for h in range(2):
                            mm = pe.matmul(PS[3][h * S:(h + 1) * S, (CB * hp + b) * S:(CB * hp + b + 1) * S],
                                           qs[:, hp, b, h], kt[:, b, :], start=True, stop=True)
                mm.then_inc(s_done, 1)

            def q_sums(j):
                pe.wait_ge(sq_pool, 3 * j + 3)
                pe.wait_ge(sq_b1, 2 * j + 2)
                pe.wait_ge(sq_b2, j + 1)
                pe.wait_ge(sq_b3, j + 1)
                for hp in range(2):
                    for b in range(CB):
                        for z in range(3):
                            mm = pe.matmul(PS[2][:, CB * hp + b:CB * hp + b + 1],
                                           sqb[:, z, hp, b].rearrange("p h s -> p (h s)"), onec[:],
                                           start=(z == 0), stop=(z == 2))
                mm.then_inc(ss_done, 1)

            def project_out(bp, w_o, heads):
                for h in heads:
                    c0 = 2048 + h * 512
                    lh, ll = (t[:, bp, h].rearrange("p b s -> p (b s)") for t in (ah, al))
                    mm = split_product(pe, PS[6 + bp][:], lh, ll, w_o[0][:, c0:c0 + 512],
                                       w_o[1][:, c0:c0 + 512], h == 0, h == HG - 1)
                if heads[-1] == HG - 1:
                    mm.then_inc(o_done, 1)

            def transpose_probs(i):
                for m in range(4):
                    if m % 2 == 0:
                        pe.wait_ge(p_ready, 2 * i + 1 + m // 2)
                    src = pb[:, CB * (m // 2) + 2 * (m % 2):CB * (m // 2) + 2 * (m % 2) + 2, :]
                    mm = pe.transpose(PS[2 + m % 2][:, m // 2 * P:(m // 2 + 1) * P], src.rearrange("p b s -> p (b s)"), ident[:])
                mm.then_inc(pT_done, 1)

            def probs_v(i):
                pe.wait_ge(v_split, 2 * i + 2)
                pe.wait_ge(a_hi, 4 * i + 4)
                pe.wait_ge(a_lo, 4 * i + 4)
                for b2 in range(2):
                    rows = slice(b2 * S, (b2 + 1) * S)
                    for bp in range(2):
                        if b2 == 0:
                            pe.wait_ge(pT_hi, 2 * i + 1 + bp)
                            pe.wait_ge(pT_evac, 2 * i + 1 + bp)
                        probs = [t[rows, bp, :] for t in pt]
                        mm = split_product(pe, PS[4 + b2][:, bp * 256:(bp + 1) * 256], vhl[0][rows, bp, :],
                                           vhl[1][rows, bp, :], probs[0], probs[1], True, True)
                    mm.then_inc(pv_done, 1)

            def step(i, chunk_q, w_q, w_o, w_before, q_ready, o_ready):
                if q_ready is not None:
                    pe.wait_ge(w_lo, q_ready)
                pe.wait_ge(sq_b1, 2 * i + 1)
                q_head(0, 0, chunk_q, w_q)
                q_head(0, 1, chunk_q, w_q).then_inc(q_done, 1)
                pe.wait_ge(sq_b1, 2 * i + 2)
                q_head(1, 0, chunk_q, w_q)
                transpose_probs(i)
                q_head(1, 1, chunk_q, w_q).then_inc(q_done, 1)
                probs_v(i)
                scores(i + 1)
                pe.wait_ge(acc_done, 2 * i + 1)
                project_out(1, w_before, (0, 1, 2))
                q_sums(i + 1)
                project_out(1, w_before, (3,))
                pe.wait_ge(w_lo, o_ready)
                pe.wait_ge(a_hi, 4 * i + 6)
                pe.wait_ge(a_lo, 4 * i + 6)
                pe.wait_ge(acc_done, 2 * i + 2)
                project_out(0, w_o, (0, 1, 2, 3))

            pe.wait_ge(w_lo, 4)
            for hp in range(2):
                q_head(hp, 0, 0, W[0])
                q_head(hp, 1, 0, W[0]).then_inc(q_done, 1)
            scores(0)
            pe.wait_ge(acc_zero, 3)
            q_sums(0)
            def group(i0, p, last=False):
                step(i0, 1, W[p], W[p], W[1 - p], None, i0 + 8)
                with pe.Fori(0, NC - 2) as t:
                    step(i0 + 1 + t, t + 2, W[p], W[p], W[p], None, i0 + 8)
                if not last:
                    step(i0 + NC - 1, 0, W[1 - p], W[p], W[p], i0 + 12, i0 + 8)

            with pe.Fori(0, KVH // 2 - 1) as gg:
                for p in range(2):
                    group(2 * NC * gg + NC * p, p)
            group(STEPS - 2 * NC, 0)
            group(STEPS - NC, 1, last=True)
            pe.wait_ge(acc_done, 2 * STEPS - 1)
            pe.wait_ge(a_hi, 4 * STEPS)
            pe.wait_ge(a_lo, 4 * STEPS)
            project_out(1, W[1], (0, 1, 2, 3))
            transpose_probs(STEPS - 1)
            probs_v(STEPS - 1)
            pe.wait_ge(a_hi, 4 * STEPS + 2)
            pe.wait_ge(a_lo, 4 * STEPS + 2)
            pe.wait_ge(acc_done, 2 * STEPS)
            project_out(0, W[1], (0, 1, 2, 3))
            pe.wait_ge(a_hi, 4 * STEPS + 4)
            pe.wait_ge(a_lo, 4 * STEPS + 4)
            pe.wait_ge(acc_done, 2 * STEPS + 1)
            project_out(1, W[1], (0, 1, 2, 3))

            pe.wait_ge(g_lo_ok, 1)

            def transpose_h2(n):
                pe.wait_ge(h2_done, n + 1)
                if n >= 4:
                    pe.wait_ge(h2T_lo, n - 3)
                for k in range(KD):
                    mm = pe.transpose(PS[n % 4][:, k * P:(k + 1) * P], h2[n % 4][:, k * P:(k + 1) * P], ident[:])
                mm.then_inc(h2T_done, 1)

            for n in range(4):
                transpose_h2(n)
            for c in range(4):
                if c < 3:
                    for n in range(4 * c + 4, 4 * c + 8):
                        transpose_h2(n)
                pe.wait_ge(h2T_hi, 4 * c + 4)
                pe.wait_ge(h2T_lo, 4 * c + 4)
                if c == 2:
                    pe.wait_ge(acc_done, 2 * STEPS + 3)
                for k in range(KD):
                    mm = split_product(pe, PS[4 + c][:], g_hi[:, k, :], g_lo[:, k, :],
                                       hT[:, 2 * c:2 * c + 2, 0, k, :], hT[:, 2 * c:2 * c + 2, 1, k, :],
                                       k == 0, k == KD - 1)
                mm.then_inc(lg_done, 1)

            def gate_up(c, it, halves=(0, 1)):
                if halves[0] == 0:
                    pe.wait_ge(act_f, 4 * c + it + 1)
                for u in halves:
                    for k in range(KD):
                        c0 = k * 2 * SI + u * SI + it * P
                        mm = split_product(pe, PS[2 * (it % 2) + u][:], W[0][0][:, c0:c0 + P],
                                           W[0][1][:, c0:c0 + P], hT[:, bass.ds(2 * c, 2), 0, k, :],
                                           hT[:, bass.ds(2 * c, 2), 1, k, :], k == 0, k == KD - 1)
                    mm.then_inc(gu_done, 1)

            def down(c, it):
                pe.wait_ge(act_lo, 4 * c + it + 1)
                for tl in range(4):
                    if it == 0:
                        pe.wait_ge(sh_done, 4 * c + tl + 1)
                    c0 = it * 512
                    mm = split_product(pe, PS[4 + tl][:], W[1][1][:, c0 + tl * P:c0 + (tl + 1) * P],
                                       W[1][1][:, 2048 + c0 + tl * P:2048 + c0 + (tl + 1) * P],
                                       W[1][0][:, c0:c0 + 512], W[1][0][:, 2048 + c0:2048 + c0 + 512],
                                       it == 0, it == 3)
                    if it == 3:
                        mm.then_inc(dn_done, 1)

            def shared(c):
                for it in range(3):
                    gate_up(c, it)
                down(c, 0)
                gate_up(c, 3)
                for it in range(1, 4):
                    down(c, it)

            gate_up(0, 0, (0,))
            pe.wait_ge(lg_evac, 4)
            for n in range(NT):
                mm = pe.transpose(PS[4][:, n * E:(n + 1) * E], lgT[:, n * P:(n + 1) * P], ident[0:E, 0:E])
            mm.then_inc(lgt_done, 1)
            gate_up(0, 0, (1,))
            gate_up(0, 1)
            gate_up(0, 2)
            pe.wait_ge(tri_ok, 1)
            pe.wait_ge(rank_in, 1)
            counts = rab[:].rearrange("p n e -> p (n e)")
            pe.matmul(PS[5][:, 0:NT * E], trib[:], counts, start=True, stop=False)
            for d in range(1, NT):
                pe.matmul(PS[5][:, d * E:NT * E], onesb[:], counts[:, 0:(NT - d) * E], start=False, stop=(d == NT - 1))
            for n in range(NT):
                mm = pe.matmul(PS[6][:, 0:E], onesb[:], rab[:, n, :], start=(n == 0), stop=(n == NT - 1))
            mm.then_inc(rank_done, 1)
            gate_up(0, 3)
            pe.wait_ge(shd_lo, 1)
            pe.wait_ge(rank_out, 2)
            for it in range(4):
                down(0, it)
            with pe.Fori(1, 3) as c:
                shared(c)
            pe.wait_ge(srow_f, 1)
            pe.wait_ge(sh_done, 16)
            pe.transpose(PS[7][:, 0:NB], srowf[:], ident[0:NB, 0:NB]).then_inc(srowT, 1)
            pe.wait_ge(sidx_ok, 1)
            shared(3)

            def expert_T(b, q):
                pe.wait_ge(xg_in[q], 8 * (b - q) + 16)
                for k in range(KD):
                    mm = pe.transpose(PS[q][:, k * P:(k + 1) * P], xg[q][:, k * P:(k + 1) * P], ident[:])
                mm.then_inc(xgT_done, 1)

            def expert_gate_up(b, q, e, ks):
                for k in ks:
                    mm = pe.matmul(PS[2 + q][:, 0:2 * EI], xgT[q][:, k, :],
                                   wgu[:, bass.ds(e, 1), k * 2 * EI:(k + 1) * 2 * EI].rearrange("p a n -> p (a n)"),
                                   start=(k == 0), stop=(k == KD - 1))
                if ks[-1] == KD - 1:
                    mm.then_inc(eg_done, 1)

            def expert_of(b):
                return pe.value_load(ebi[0:1, bass.ds(b, 1)], min_val=0, max_val=E - 1)

            def expert_down(b, q):
                e = expert_of(b)
                pe.wait_ge(eT_evac, b + 1)
                pe.wait_ge(ye_ok, b + 1)
                pe.matmul(PS[5 + q][:], acteT[:], wdn[:, bass.ds(e, 1), :].rearrange("p a n -> p (a n)"),
                          start=True, stop=True).then_inc(ed_done, 1)

            pe.wait_ge(wdn_in, 16)
            pe.wait_ge(wgu_in, 64)
            pe.wait_ge(sh_done, 20)
            expert_T(0, 0)
            expert_T(1, 1)
            pe.wait_ge(xgT_evac, 1)
            expert_gate_up(0, 0, expert_of(0), range(KD))
            with pe.Fori(0, NB // 2) as m:
                for q in range(2):
                    b = 2 * m + q
                    expert_T(b + 2, q)
                    e = expert_of(b + 1)
                    pe.wait_ge(xgT_evac, b + 2)
                    expert_gate_up(b + 1, 1 - q, e, (0, 1))
                    pe.wait_ge(e_act, b + 1)
                    pe.transpose(PS[4][:, 0:P], acte[:], ident[:]).then_inc(eT_done, 1)
                    expert_gate_up(b + 1, 1 - q, e, (2, 3))
                    expert_down(b, q)

        @block.scalar
        def _(act):
            act.sem_inc(v_evac, 2)
            act.sem_inc(kT_evac, 2)
            act.sem_inc(a_hi, 4)
            act.wait_ge(setup_in, 96)
            act.activation(tg[:], gcol[:], ACT.Tanh).then_inc(const_act, 1)
            act.wait_ge(ctx_in, 16)
            act.copy(c_hi[0][:], craw[:]).then_inc(ctx_hi, 1)
            for j in range(4):
                act.wait_ge(kvw_in[j], 16)
                act.copy(W[j // 2][0][:, (j % 2) * 2048:(j % 2 + 1) * 2048],
                         accf[:, j * 2048:(j + 1) * 2048]).then_inc(kvw_hi, 1)
            act.wait_ge(const_dve, 1)
            with act.Fori(0, NC // 2) as m:
                for cp in range(2):
                    for tt in range(2):
                        c = 2 * m + cp
                        n = 4 * m + 2 * cp + tt
                        if tt == 1:
                            act.wait_ge(ctx_in, 16 * c + 32)
                            act.copy(c_hi[1 - cp][:], craw[:]).then_inc(ctx_hi, 1)
                        for j in range(2):
                            act.wait_ge(k_done, 2 * n + 1 + j)
                            act.activation(ksq[:, j].rearrange("p g d -> p (g d)"), PS[j][:],
                                           ACT.Square).then_inc(k_sq, 1)
                        act.wait_ge(hT_done, n + 1)
                        act.copy(hT[:, bass.ds(c, 1), 0, :, tt * P:(tt + 1) * P].rearrange("p a k t -> p (a k) t"),
                                 PS[6][:].rearrange("p (k t) -> p k t", k=KD)).then_inc(hT_hi, 1)
                        act.wait_ge(v_stored, 16 * n + 16)
                        for j in range(2):
                            act.wait_ge(v_done, 2 * n + 1 + j)
                            act.copy(vo[:, j * 512:(j + 1) * 512], PS[2 + j][:]).then_inc(v_evac, 1)
                        act.wait_ge(k_stored, 16 * n + 16)
                        for j in range(2):
                            act.wait_ge(kT_done, 2 * n + 1 + j)
                            act.activation(ko[:, 4 * j:4 * j + 4, :].rearrange("p g t -> p (g t)"), PS[4 + j][:],
                                           ACT.Copy, scale=wqk[:, 0:1]).then_inc(kT_evac, 1)
            act.wait_ge(w0_in, 16)
            for s in range(8):
                act.copy(W[0][0][:, s * 512:(s + 1) * 512], accf[:, s * 512:(s + 1) * 512]).then_inc(w_hi, 1)
            act.wait_ge(v_stored, 16 * NT + 16)
            act.wait_ge(k_stored, 16 * NT + 16)
            act.wait_ge(w_lo, 8)

            act.wait_ge(g_in, 16)
            act.wait_ge(const_dve, 3)
            act.copy(g_hi[:, :, 0:E], graw[:].rearrange("p (k e) -> p k e", k=KD)).then_inc(g_hi_ok, 1)

            q_view = lambda hp: PS[hp][:].rearrange("p (h b s) -> p b h s", h=2, b=CB)

            def q_out(hp, j):
                act.wait_ge(q_done, 2 * j + 1 + hp)
                act.copy(qs[:, hp], q_view(hp)).then_inc(q_copy, 1)

            def squares(hp, j):
                act.wait_ge(ss_done, j + 1)
                act.activation(sq[:, hp], q_view(hp), ACT.Square).then_inc(q_sq, 1)
                act.activation(sqb[:, 0, hp], q_view(hp), ACT.Square).then_inc(sq_b1, 1)


            def squares_2(j):
                act.wait_ge(sq_r, j + 1)
                act.copy(sqb[:, 1, 1], sq[:, 1]).then_inc(sq_b2, 1)

            def exps(j):
                for hp in range(2):
                    act.wait_ge(s_sub, 2 * j + 1 + hp)
                    act.activation(pb[:, CB * hp:CB * hp + CB, :], pb[:, CB * hp:CB * hp + CB, :], ACT.Exp).then_inc(
                        s_exp, 1)

            for hp in range(2):
                q_out(hp, 0)
                squares(hp, 0)
            squares_2(0)
            exps(0)

            def probs_hi(i):
                act.wait_ge(pT_done, i + 1)
                for bp in range(2):
                    act.copy(pt[0][:, bp, :], PS[2 + bp][:, 0:HG * S]).then_inc(pT_hi, 1)

            def a_hi_tile(i, bp):
                if bp == 1:
                    act.wait_ge(o_done, 2 * i + 1)
                    act.wait_ge(a_lo, 4 * i + 6)
                for b2 in range(2):
                    act.wait_ge(pv_done, 2 * i + 3 + b2)
                    act.copy(ah[:, bp, :, b2, :], pv_view(bp, b2)).then_inc(a_hi, 1)

            def split_slice(i, w, sl):
                act.wait_ge(wr_in, 16 * i + 16)
                act.copy(w[0][:, bass.ds(sl * 512, 512)] if not isinstance(sl, int) else
                         w[0][:, sl * 512:(sl + 1) * 512], wraw[:]).then_inc(w_hi, 1)

            def act_step(i, w, sl):
                act.wait_ge(s_done, i + 1)
                q_out(0, i + 1)
                squares(0, i + 1)
                probs_hi(i)
                q_out(1, i + 1)
                squares(1, i + 1)
                a_hi_tile(i, 0)
                squares_2(i + 1)
                a_hi_tile(i, 1)
                split_slice(i, w, sl)
                exps(i + 1)

            with act.Fori(0, KVH // 2 - 1) as gg:
                for p in range(2):
                    i0 = 2 * NC * gg + NC * p
                    with act.Fori(0, NC) as t:
                        act_step(i0 + t, W[1 - p], t)
            for p in range(2):
                i0 = STEPS - 2 * NC + NC * p
                with act.Fori(0, NC - p) as t:
                    act_step(i0 + t, W[1 - p], t)
            probs_hi(STEPS - 1)
            a_hi_tile(STEPS - 1, 0)
            a_hi_tile(STEPS - 1, 1)
            split_slice(STEPS - 1, W[0], NC - 1)

            act.wait_ge(shd_in, 16)
            act.copy(W[1][0][:, 0:2048], draw[:]).then_inc(shd_hi, 1)
            with act.Fori(0, NT // 4) as m:
                for q in range(4):
                    act.wait_ge(h2T_done, 4 * m + q + 1)
                    act.copy(hT[:, bass.ds(2 * m + q // 2, 1), 0, :, (q % 2) * P:(q % 2 + 1) * P].rearrange(
                        "p a k t -> p (a k) t"), PS[q][:].rearrange("p (k t) -> p k t", k=KD)).then_inc(h2T_hi, 1)
            for c in range(4):
                act.wait_ge(lg_done, c + 1)
                act.copy(lgT[:, c * 512:(c + 1) * 512], PS[4 + c][0:E, :]).then_inc(lg_evac, 1)
            def silu_split(c, first=False):
                for it in range(4):
                    act.wait_ge(gu_done, 8 * c + 2 * it + 1)
                    act.wait_ge(act_f, 4 * c + it + 2)
                    act.activation(sgt[0][:], PS[2 * (it % 2)][:], ACT.Silu).then_inc(sil, 1)
                    if first and it == 0:
                        act.wait_ge(rt_sub, 1)
                        act.activation(rb[:], ra[:], ACT.Exp).then_inc(rt_exp, 1)
                    act.wait_ge(act_f, 4 * c + it + 3)
                    act.copy(W[1][1][:, it * 512:(it + 1) * 512], aft[0][:]).then_inc(act_hi, 1)

            silu_split(0, first=True)
            with act.Fori(1, 4) as c:
                silu_split(c)

            def xT_out(b, q):
                act.wait_ge(xgT_done, b + 3)
                act.copy(xgT[q][:].rearrange("p k t -> p (k t)"), PS[q][:]).then_inc(xgT_evac, 1)

            def silu(b, q):
                act.wait_ge(eg_done, b + 1)
                act.activation(sge[:], PS[2 + q][:, 0:EI], ACT.Silu).then_inc(e_sil, 1)

            xT_out(0, 0)
            xT_out(1, 1)
            silu(0, 0)
            with act.Fori(0, NB // 2) as m:
                for q in range(2):
                    b = 2 * m + q
                    act.wait_ge(eg_done, b + 1)
                    xT_out(b + 2, q)
                    act.wait_ge(e_act, b + 1)
                    silu(b + 1, 1 - q)

        @block.vector
        def _(dve):
            dve.sem_inc(kn_done, 2)
            dve.sem_inc(a_lo, 4)
            dve.sem_inc(acc_done, 2)
            dve.sem_inc(act_f, 2)
            dve.sem_inc(sh_done, 4)
            dve.sem_inc(ye_ok, 2)
            dve.wait_ge(setup_in, 96)
            dve.tensor_tensor(wqk[:], qkw[:, 0:1], qkw[:, 1:2], ALU.mult).then_inc(const_dve, 1)
            dve.wait_ge(ctx_hi, 1)
            dve.tensor_tensor(c_lo[0][:], craw[:], c_hi[0][:], ALU.subtract).then_inc(ctx_lo, 1)
            for j in range(4):
                dve.wait_ge(kvw_hi, j + 1)
                cs = slice((j % 2) * 2048, (j % 2 + 1) * 2048)
                dve.tensor_tensor(W[j // 2][1][:, cs], accf[:, j * 2048:(j + 1) * 2048],
                                  W[j // 2][0][:, cs], ALU.subtract).then_inc(kvw_lo, 1)
            with dve.Fori(0, NC // 2) as m:
                for cp in range(2):
                    for tt in range(2):
                        c = 2 * m + cp
                        n = 4 * m + 2 * cp + tt
                        dve.wait_ge(x_in, 16 * n + 16)
                        dve.bn_stats(st1[:], xt[tt][:]).then_inc(ln_st, 1)
                        dve.wait_ge(ln_st, n + 1)
                        dve.sem_inc(dve_mark, 1)
                        dve.bn_aggr(mv1[:], st1[:]).then_inc(ln_mv, 1)
                        dve.wait_ge(ln_mv, n + 1)
                        dve.tensor_scalar(ve1[:], mv1[:, 1:2], EPS, None, ALU.add).then_inc(ln_var, 1)
                        if tt == 1:
                            dve.wait_ge(ctx_hi, c + 2)
                            dve.tensor_tensor(c_lo[1 - cp][:], craw[:], c_hi[1 - cp][:],
                                              ALU.subtract).then_inc(ctx_lo, 1)
                        dve.wait_ge(ln_rt, n + 1)
                        dve.tensor_scalar(h1[:], xt[tt][:], mv1[:, 0:1], rs1[:, 0:1], ALU.subtract,
                                          ALU.mult).then_inc(h_done, 1)
                        dve.wait_ge(k_sq, 2 * n + 2)
                        dve.tensor_reduce(kss[:], ksq[:].rearrange("p j g d -> p (j g) d"), AX,
                                          ALU.add).then_inc(k_ss, 1)
                        dve.wait_ge(k_ss, n + 1)
                        dve.tensor_scalar(kv_[:], kss[:], 1.0 / HD, EPS, ALU.mult, ALU.add).then_inc(k_var, 1)
                        dve.wait_ge(hT_hi, n + 1)
                        ts = slice(tt * P, (tt + 1) * P)
                        dve.tensor_tensor(hT[:, bass.ds(c, 1), 1, :, ts].rearrange("p a k t -> p (a k) t"),
                                          PS[6][:].rearrange("p (k t) -> p k t", k=KD),
                                          hT[:, bass.ds(c, 1), 0, :, ts].rearrange("p a k t -> p (a k) t"),
                                          ALU.subtract).then_inc(hT_lo, 1)
                        dve.wait_ge(k_rt, n + 1)
                        for j in range(2):
                            dve.tensor_tensor(kn[:, 4 * j:4 * j + 4, :],
                                              PS[j][:].rearrange("p (g d) -> p g d", d=HD),
                                              kr[:, 4 * j:4 * j + 4].unsqueeze(2).to_broadcast([P, 4, HD]),
                                              ALU.mult).then_inc(kn_done, 1)
            for s in range(8):
                dve.wait_ge(w_hi, s + 1)
                cs = slice(s * 512, (s + 1) * 512)
                dve.tensor_tensor(W[0][1][:, cs], accf[:, cs], W[0][0][:, cs], ALU.subtract).then_inc(w_lo, 1)

            def squares_rest(j):
                dve.wait_ge(sq_b1, 2 * j + 2)
                dve.wait_ge(q_sq, 2 * j + 2)
                dve.tensor_tensor(sq[:, 1], sq[:, 1], sqb[:, 0, 1], ALU.subtract).then_inc(sq_r, 1)

            def squares_last(j):
                dve.wait_ge(sq_r, j + 1)
                dve.wait_ge(sq_b2, j + 1)
                dve.tensor_tensor(sqb[:, 2, 1], sq[:, 1], sqb[:, 1, 1], ALU.subtract).then_inc(sq_b3, 1)

            def add_out(count, bp, tile):
                dve.wait_ge(o_done, count)
                dst = accf[:, bass.ds(tile * D, D)] if not isinstance(tile, int) else \
                    accf[:, tile * D:(tile + 1) * D]
                dve.tensor_tensor(dst, PS[6 + bp][:], dst, ALU.add).then_inc(acc_done, 1)

            def a_rest(i, bp):
                for b2 in range(2):
                    dve.wait_ge(a_hi, 4 * i + 5 + 2 * bp + b2)
                    dve.tensor_tensor(al[:, bp, :, b2, :], pv_view(bp, b2), ah[:, bp, :, b2, :],
                                      ALU.subtract).then_inc(a_lo, 1)

            def softmax(j, *meanwhile):
                per_row = lambda t: t[:].unsqueeze(2).to_broadcast([P, 8, S])
                dve.wait_ge(ss_done, j + 2)
                dve.tensor_scalar(qv[:], PS[2][:, 0:8], HD * EPS, None, ALU.add).then_inc(q_var, 1)
                half = lambda t, hp: t[:, CB * hp:CB * hp + CB, :]
                half_row = lambda t, hp: t[:, CB * hp:CB * hp + CB].unsqueeze(2).to_broadcast([P, CB, S])
                if meanwhile:
                    meanwhile[0]()
                dve.wait_ge(q_rt, j + 1)
                dve.wait_ge(s_done, j + 1)
                dve.tensor_tensor(pb[:], PS[3][:].rearrange("p (b s) -> p b s", s=S), per_row(qr),
                                  ALU.mult).then_inc(s_scaled, 1)
                dve.wait_ge(s_scaled, j + 1)
                dve.tensor_tensor(pb[:], pb[:], maskb[:].unsqueeze(1).to_broadcast([P, 8, S]),
                                  ALU.add).then_inc(s_masked, 1)
                dve.wait_ge(s_masked, j + 1)
                dve.tensor_reduce(mx[:], pb[:], AX, ALU.max).then_inc(s_max, 1)
                dve.wait_ge(s_max, j + 1)
                for hp in range(2):
                    dve.tensor_tensor(half(pb, hp), half(pb, hp), half_row(mx, hp), ALU.subtract).then_inc(s_sub, 1)
                if meanwhile:
                    meanwhile[1]()
                dve.wait_ge(s_exp, 2 * j + 2)
                dve.tensor_reduce(sm[:], pb[:], AX, ALU.add).then_inc(s_sum, 1)
                dve.wait_ge(s_sum, j + 1)
                dve.reciprocal(rc[:], sm[:]).then_inc(s_rcp, 1)
                dve.wait_ge(s_rcp, j + 1)
                for hp in range(2):
                    dve.tensor_tensor(half(pb, hp), half(pb, hp), half_row(rc, hp), ALU.mult).then_inc(p_ready, 1)

            def probs_lo(i):
                for bp in range(2):
                    dve.wait_ge(pT_hi, 2 * i + 1 + bp)
                    dve.tensor_tensor(pt[1][:, bp, :], PS[2 + bp][:, 0:HG * S], pt[0][:, bp, :],
                                      ALU.subtract).then_inc(pT_evac, 1)

            def slice_lo(i, w, sl):
                dve.wait_ge(w_hi, i + 9)
                ws = bass.ds(sl * 512, 512) if not isinstance(sl, int) else slice(sl * 512, (sl + 1) * 512)
                dve.tensor_tensor(w[1][:, ws], wraw[:], w[0][:, ws], ALU.subtract).then_inc(w_lo, 1)

            def residual(n, b):
                row = acc[:, n, :] if isinstance(n, int) else acc[:, bass.ds(n, 1), :].rearrange("p a d -> p (a d)")
                st = st3[:, n, :] if isinstance(n, int) else st3[:, bass.ds(n, 1), :].rearrange("p a d -> p (a d)")
                dve.wait_ge(x3_in[b], 8 * (n - b) + 16)
                dve.scalar_tensor_tensor(out=row, in0=row, scalar=tg[:, 0:1], in1=xt3[b][:],
                                         op0=ALU.mult, op1=ALU.add).then_inc(x1_done, 1)
                dve.wait_ge(x1_done, n + 1)
                dve.bn_stats(st, row).then_inc(st_done, 1)

            def dve_step(i, w, sl, tile, tile_before, complete=(None, None)):
                probs_lo(i)
                if complete[0] is not None:
                    residual(complete[0], 1)
                squares_rest(i + 1)
                a_rest(i, 0)
                squares_last(i + 1)
                if complete[1] is not None:
                    residual(complete[1], 0)

                def while_root():
                    add_out(2 * i + 1, 1, tile_before)
                    a_rest(i, 1)

                softmax(i + 1, while_root, lambda: add_out(2 * i + 2, 0, tile))
                slice_lo(i, w, sl)

            dve.wait_ge(v_stored, 16 * NT + 16)
            dve.wait_ge(k_stored, 16 * NT + 16)
            dve.wait_ge(pool_const, 10)
            dve.tensor_copy(trib[:], tri[:]).then_inc(tri_ok, 1)
            dve.memset(g_hi[:].rearrange("p k e -> p (k e)").bitcast(F32), 0.0).then_inc(const_dve, 1)
            dve.memset(g_lo[:].rearrange("p k e -> p (k e)").bitcast(F32), 0.0).then_inc(const_dve, 1)
            dve.wait_ge(g_hi_ok, 1)
            dve.wait_ge(const_dve, 3)
            dve.tensor_tensor(g_lo[:, :, 0:E], graw[:].rearrange("p (k e) -> p k e", k=KD), g_hi[:, :, 0:E],
                              ALU.subtract).then_inc(g_lo_ok, 1)
            dve.wait_ge(acc_zero, 4)
            squares_rest(0)
            squares_last(0)
            softmax(0)
            def group(i0, p):
                dve_step(i0, W[1 - p], 0, 0, NT - 1)
                with dve.Fori(0, NC - 2) as t:
                    dve_step(i0 + 1 + t, W[1 - p], t + 1, 2 * t + 2, 2 * t + 1)
                dve_step(i0 + NC - 1, W[1 - p], NC - 1, NT - 2, NT - 3)

            with dve.Fori(0, KVH // 2 - 1) as gg:
                for p in range(2):
                    group(2 * NC * gg + NC * p, p)
            group(STEPS - 2 * NC, 0)
            i0 = STEPS - NC
            dve_step(i0, W[0], 0, 0, NT - 1)
            dve.wait_ge(const_act, 1)
            dve_step(i0 + 1, W[0], 1, 2, 1, (None, 0))
            with dve.Fori(0, NC - 3) as t:
                dve_step(i0 + 2 + t, W[0], t + 2, 2 * t + 4, 2 * t + 3, (2 * t + 1, 2 * t + 2))

            def statistics(z):
                for n in range(8 * z, 8 * z + 8):
                    dve.wait_ge(st_done, n + 1)
                    dve.bn_aggr(mv3[:, n, :], st3[:, n, :]).then_inc(mv_done, 1)
                dve.wait_ge(mv_done, 8 * z + 8)
                dve.tensor_scalar(ve3[:, 8 * z:8 * z + 8], mv3[:, 8 * z:8 * z + 8, 1], EPS, None,
                                  ALU.add).then_inc(var3, 1)

            def normalise(n):
                dve.wait_ge(rt3, n // 8 + 1)
                dve.wait_ge(h2_stored[n % 4], 16 * (n // 4) + 16)
                dve.tensor_scalar(h2[n % 4][:], acc[:, n, :], mv3[:, n, 0:1], rs3[:, n:n + 1], ALU.subtract,
                                  ALU.mult).then_inc(h2_done, 1)

            def h2T_rest(n):
                dve.wait_ge(h2T_hi, n + 1)
                part = [hT[:, n // 2, x_, :, (n % 2) * P:(n % 2 + 1) * P] for x_ in range(2)]
                dve.tensor_tensor(part[1], PS[n % 4][:].rearrange("p (k t) -> p k t", k=KD), part[0],
                                  ALU.subtract).then_inc(h2T_lo, 1)

            i = STEPS - 1
            add_out(2 * i + 1, 1, 13)
            probs_lo(i)
            statistics(0)
            a_rest(i, 0)
            a_rest(i, 1)
            residual(11, 1)
            residual(12, 0)
            for n in range(4):
                normalise(n)
            dve.wait_ge(acc_done, 2 * i + 3)
            residual(13, 1)
            slice_lo(i, W[0], NC - 1)
            add_out(2 * i + 2, 0, 14)
            dve.wait_ge(acc_done, 2 * i + 4)
            residual(14, 0)
            add_out(2 * i + 3, 1, 15)
            dve.wait_ge(acc_done, 2 * i + 5)
            residual(15, 1)
            statistics(1)
            for n in range(NT):
                h2T_rest(n)
                if n + 4 < NT:
                    normalise(n + 4)

            def shared_in(c, it):
                dve.wait_ge(sil, 4 * c + it + 1)
                dve.wait_ge(gu_done, 8 * c + 2 * it + 2)
                if not (isinstance(c, int) and c == 0 and it == 0):
                    dve.wait_ge(act_lo, 4 * c + it)
                dve.tensor_tensor(aft[0][:], PS[2 * (it % 2) + 1][:], sgt[0][:], ALU.mult).then_inc(act_f, 1)
                dve.wait_ge(act_f, 4 * c + it + 3)
                dve.wait_ge(act_hi, 4 * c + it + 1)
                dve.tensor_tensor(W[1][1][:, 2048 + it * 512:2048 + (it + 1) * 512], aft[0][:],
                                  W[1][1][:, it * 512:(it + 1) * 512], ALU.subtract).then_inc(act_lo, 1)

            def shared_out(c):
                for tl in range(4):
                    dve.wait_ge(dn_done, 4 * c + tl + 1)
                    n = 4 * c + tl
                    dst = accf[:, n * D:(n + 1) * D] if isinstance(n, int) else accf[:, bass.ds(n * D, D)]
                    dve.scalar_tensor_tensor(out=dst, in0=PS[4 + tl][:], scalar=tg[:, 1:2], in1=dst,
                                             op0=ALU.mult, op1=ALU.add).then_inc(sh_done, 1)

            def shared(c):
                for it in range(4):
                    shared_in(c, it)
                shared_out(c)

            links = [0]

            def link(ins):
                links[0] += 1
                ins.then_inc(rt_dve, 1)
                dve.wait_ge(rt_dve, links[0])

            over_e = lambda t: t.unsqueeze(2).to_broadcast([P, NT, E])
            over_n = lambda t: t.unsqueeze(1).to_broadcast([P, NT, E])
            dve.wait_ge(lgt_done, 1)
            logits = PS[4][:, 0:NT * E].rearrange("p (n e) -> p n e", e=E)
            link(dve.tensor_reduce(rsm[:], logits, AX, ALU.max))
            dve.tensor_tensor(ra[:], logits, over_e(rsm[:]), ALU.subtract).then_inc(rt_sub, 1)
            dve.wait_ge(rt_exp, 1)
            link(dve.tensor_reduce(rsm[:], rb[:], AX, ALU.add))
            link(dve.reciprocal(rsr[:], rsm[:]))
            link(dve.tensor_tensor(rb[:], rb[:], over_e(rsr[:]), ALU.mult))
            for n in range(NT):
                dve.max(m8[:, n, :], rb[:, n, :]).then_inc(mv_done, 1)
            for n in range(NT):
                dve.wait_ge(mv_done, NT + n + 1)
                dve.max_index(i8[:, n, :], m8[:, n, :], rb[:, n, :]).then_inc(st_done, 1)
            shared_in(0, 0)
            link(dve.tensor_tensor(rsm[:], m8[:, :, 0], m8[:, :, 1], ALU.add))
            link(dve.reciprocal(rsr[:], rsm[:]))
            link(dve.tensor_tensor(cw[:, 0, :], m8[:, :, 0], rsr[:], ALU.mult))
            link(dve.tensor_tensor(cw[:, 1, :], m8[:, :, 1], rsr[:], ALU.mult))
            link(dve.tensor_scalar(cw[:], cw[:], tg[:, 1:2], None, ALU.mult))
            dve.wait_ge(st_done, 2 * NT)
            for s, oh in enumerate((oh1, oh2)):
                link(dve.tensor_copy(slf[:, s, :], i8[:, :, s]))
                link(dve.tensor_tensor(oh[:], over_n(iota_e[:]), over_e(slf[:, s, :]), ALU.is_equal))
            dve.tensor_tensor(rab[:], oh1[:], oh2[:], ALU.add).then_inc(rank_in, 1)
            shared_in(0, 1)
            dve.wait_ge(rank_done, 1)
            dve.tensor_copy(ra[:].rearrange("p n e -> p (n e)"), PS[5][:, 0:NT * E]).then_inc(rank_out, 1)
            dve.tensor_scalar(stb[:], PS[6][:, 0:E], 1.0 / P, None, ALU.mult).then_inc(rank_out, 1)
            shared_in(0, 2)
            dve.wait_ge(rank_out, 2)
            link(dve.tensor_tensor(rb[:], over_e(stb[:]), over_n(iota_e[:]), ALU.is_gt))
            link(dve.tensor_reduce(nbk[:], rb[:], AX, ALU.add))
            link(dve.tensor_tensor_scan(endb[:], ones[:, 0:E], nbk[:], 0.0, ALU.mult, ALU.add))
            link(dve.tensor_tensor(stb[:], endb[:], nbk[:], ALU.subtract))
            link(dve.tensor_scalar(stb[:], stb[:], float(P), None, ALU.mult))
            link(dve.tensor_tensor(ra[:], ra[:], over_n(stb[:]), ALU.add))
            shared_in(0, 3)
            for s, oh in enumerate((oh1, oh2)):
                link(dve.tensor_tensor(rb[:], oh[:], ra[:], ALU.mult))
                link(dve.tensor_reduce(slf[:, s, :], rb[:], AX, ALU.add))
            ebt = lgT[0:1, 0:NBX * E].rearrange("p (b e) -> p b e", e=E)
            link(dve.tensor_tensor(ebt, endb[0:1, :].unsqueeze(1).to_broadcast([1, NBX, E]),
                                   iota_b[0:1, :].unsqueeze(2).to_broadcast([1, NBX, E]), ALU.is_le))
            link(dve.tensor_reduce(ebf[:], ebt, AX, ALU.add))
            link(dve.tensor_scalar(ebf[:], ebf[:], float(E - 1), None, ALU.min))
            link(dve.tensor_copy(ebi[:], ebf[:]))
            dve.tensor_copy(sli[:], slf[:]).then_inc(slot_ok, 1)
            shared_out(0)
            with dve.Fori(1, 3) as c:
                shared(c)
            dve.wait_ge(srow_in, 16)
            dve.tensor_copy(srowf[:], srow[:]).then_inc(srow_f, 1)
            dve.wait_ge(srowT, 1)
            dve.tensor_copy(sidx[:, 0:NB], PS[7][:, 0:NB]).then_inc(sidx_ok, 1)
            shared(3)

            def gated(b, q):
                dve.wait_ge(e_sil, b + 1)
                dve.tensor_tensor(acte[:], PS[2 + q][:, EI:2 * EI], sge[:], ALU.mult).then_inc(e_act, 1)

            gated(0, 0)
            with dve.Fori(0, NB // 2) as m:
                for q in range(2):
                    b = 2 * m + q
                    dve.wait_ge(eT_done, b + 1)
                    dve.tensor_copy(acteT[:], PS[4][:, 0:P]).then_inc(eT_evac, 1)
                    gated(b + 1, 1 - q)
                    dve.wait_ge(ed_done, b + 1)
                    dve.wait_ge(y_st[q], 16 * m + 16)
                    dve.tensor_copy(ye[q][:], PS[5 + q][:]).then_inc(ye_ok, 1)

            with dve.Fori(0, NT // 4) as m:
                for q in range(4):
                    n = 4 * m + q
                    row = acc[:, bass.ds(n, 1), :].rearrange("p a d -> p (a d)")
                    dve.wait_ge(y1_in[q], 16 * m + 16)
                    dve.scalar_tensor_tensor(out=row, in0=y1[q][:], scalar=cw[:, 0, bass.ds(n, 1)], in1=row,
                                             op0=ALU.mult, op1=ALU.add).then_inc(add1, 1)
                    dve.wait_ge(add1, n + 1)
                    dve.wait_ge(y2_in[q], 16 * m + 16)
                    dve.scalar_tensor_tensor(out=row, in0=y2[q][:], scalar=cw[:, 1, bass.ds(n, 1)], in1=row,
                                             op0=ALU.mult, op1=ALU.add).then_inc(add2, 1)


def kernel(**inputs):
    import numpy as np
    import concourse.bacc as bacc
    from concourse.bass_utils import run_bass_kernel_spmd

    a = {k: np.asarray(v) for k, v in inputs.items()}
    pt = np.ascontiguousarray

    def by_k(w):
        return w.reshape(w.shape[0], KD, P).transpose(2, 1, 0)

    def halves(w):
        return pt(by_k(w).reshape(P, KD, 2, 512).transpose(0, 2, 1, 3).reshape(P, 4096))

    wq = a["L0_xattn_Wq"].reshape(KVH, HG * HD, KD, P).transpose(0, 3, 2, 1).reshape(KVH, P, 2048)
    wo = a["L0_xattn_Wo"].reshape(D, KVH, HG, HD).transpose(1, 3, 2, 0).reshape(KVH, P, 2048)
    shared = by_k(a["L0_ffn_shared_w_gate_up"]).reshape(1, P, 4096)
    w_att = np.concatenate([np.concatenate([wq, wo], axis=2), shared], axis=0)
    w_att = w_att.reshape(KVH + 1, P, NC, 512).transpose(0, 2, 1, 3).reshape(-1, P, 512)
    arrays = {
        "x": pt(a["x"].reshape(NT, P, D)),
        "ctxT": pt(a["ctx_4096"].reshape(NC, CT, KD, P).transpose(0, 3, 2, 1)),
        "wk": halves(a["L0_xattn_Wk"]),
        "wv": halves(a["L0_xattn_Wv"]),
        "w_att": pt(w_att),
        "w_shd": pt(a["L0_ffn_shared_w_down"].reshape(D, SI // P, P).transpose(2, 1, 0).reshape(P, 2048)),
        "mask": pt(a["mask_1x1xSxS2_ff0"].reshape(S, S)),
        "g_x": pt(a["g_xattn"].reshape(1, 1)),
        "g_f": pt(a["g_ffn"].reshape(1, 1)),
        "q_w": pt(a["L0_xattn_q_norm_w"].reshape(HD, 1)),
        "k_w": pt(a["L0_xattn_k_norm_w"].reshape(HD, 1)),
        "gate": pt(by_k(a["L0_ffn_gate_w"]).reshape(P, KD * E)),
        "w_gu": pt(a["L0_ffn_w_gate_up"].reshape(E, 2 * EI, KD, P).transpose(0, 3, 2, 1).reshape(E, P, KD * 2 * EI)),
        "w_dn": pt(a["L0_ffn_w_down"].transpose(0, 2, 1)),
    }
    nc = bacc.Bacc("TRN2", target_bir_lowering=False, num_devices=1)
    aps = {k: nc.dram_tensor(f"in_{k}", v.shape, mybir.dt.from_np(v.dtype), kind="ExternalInput").ap()
           for k, v in arrays.items()}
    out = nc.dram_tensor("out_0", (NT, P, D), F32, kind="ExternalOutput").ap()
    build(nc, **aps, out=out)
    r = run_bass_kernel_spmd(nc, [{f"in_{k}": v for k, v in arrays.items()}], core_ids=[0])
    return np.asarray(r.results[0]["out_0"]).reshape(B, S, D)
```

```python
from contextlib import ExitStack

import numpy as np

import concourse.bass as bass
from concourse import mybir

F32 = mybir.dt.float32
F32R = mybir.dt.float32r
BF16 = mybir.dt.bfloat16
I32 = mybir.dt.int32
U32 = mybir.dt.uint32
ALU = mybir.AluOpType
ACT = mybir.ActivationFunctionType
AX = mybir.AxisListType.X

P = 128
B, S, D = 32, 64, 512
T = B * S
KD = D // P
H, KVH, HD = 32, 8, 128
HG = H // KVH
NT = T // P
CT = 2 * P
NC = T // CT
CB = CT // S
STEPS = KVH * NC
E, EI = 16, 128
SI = 512
NB = (2 * T + E * (P - 1)) // P
PAIRS = (NB - 3) // 2
EPS = 1e-5
LN2_GROUPS = ((0, 8), (8, 14), (14, 16))
KV_PIECES = ((0, 1024), (1024, 2048), (2048, 4096), (4096, 6144), (6144, 8192))


def build(nc, x, ctxT, wk, wv, w_att, w_shd, mask, g_x, g_f, q_w, k_w, gate, w_gu, w_dn, out):
    kbuf = nc.dram_tensor("kbuf", [STEPS, P, CT], F32, kind="Internal").ap()
    vbuf = nc.dram_tensor("vbuf", [STEPS, P, CT], F32, kind="Internal").ap()
    h2buf = nc.dram_tensor("h2buf", [T, D], F32, kind="Internal").ap()
    ybuf = nc.dram_tensor("ybuf", [NB * P, D], F32, kind="Internal").ap()
    slotbuf = nc.dram_tensor("slotbuf", [NB * P, 1], I32, kind="Internal").ap()
    k_st = kbuf.rearrange("(g c) p (b t) -> c b p g t", g=KVH, b=2)
    v_st = vbuf.rearrange("(g c) p (b t) -> c b p g t", g=KVH, b=2)
    h2_t = h2buf.rearrange("(n p) d -> n p d", p=P)
    y_t = ybuf.rearrange("(n p) d -> n p d", p=P)

    with ExitStack() as ctx:
        def sb(name, shape, dt=F32, stack=ctx):
            return stack.enter_context(nc.sbuf_tensor(name, shape, dt))

        def sem(name):
            return ctx.enter_context(nc.semaphore(name))

        ident = sb("ident", [P, P])
        mhalf = sb("mhalf", [P, 16])
        maskb = sb("maskb", [P, S])
        gcol = sb("gcol", [P, 2])
        tg = sb("tg", [P, 2])
        qkw = sb("qkw", [P, 2])
        wqk = sb("wqk", [P, 1])
        tok = sb("tok", [P, NT], I32)
        tri = sb("tri", [P, P])
        trib = sb("trib", [P, P], BF16)
        onesb = sb("onesb", [P, P], BF16)
        ones = sb("ones", [P, E])
        iota_e = sb("iota_e", [P, E])
        iota_b = sb("iota_b", [P, NB])
        sidx = sb("sidx", [P, NB], I32)
        zi = sb("zi", [P, NB], I32)
        acc = sb("acc", [P, NT, D])
        accf = acc[:].rearrange("p n d -> p (n d)")
        with ExitStack() as a:
            hT = sb("hT", [P, NC, 2, KD, CT], F32R, a)
        wgu = sb("wgu", [P, E, KD * 2 * EI])
        with ExitStack() as a:
            W = [[sb(f"w{p}{'hl'[q]}", [P, 4096], F32R, a) for q in range(2)] for p in range(2)]
        with ExitStack() as a:
            xgT = [sb(f"xgT{q}", [P, KD, P], F32, a) for q in range(2)]
            sge = sb("sge", [P, EI], F32, a)
            acte = sb("acte", [P, EI], F32, a)
            acteT = sb("acteT", [P, P], F32, a)
            ye = [sb(f"ye{q}", [P, D], F32, a) for q in range(2)]
            y1 = [sb(f"y1{q}", [P, D], F32, a) for q in range(4)]
            y2 = [sb(f"y2{q}", [P, D], F32, a) for q in range(4)]
        wpad = sb("wpad", [P, 4 * 4096])
        with ExitStack() as a:
            craw = sb("craw", [P, KD, CT], F32, a)
            c_hi = [sb(f"c_hi{q}", [P, KD, CT], F32R, a) for q in range(2)]
            c_lo = [sb(f"c_lo{q}", [P, KD, CT], F32R, a) for q in range(2)]
            vo = sb("vo", [P, KVH * HD], F32, a)
            kn = sb("kn", [P, KVH, HD], F32, a)
            ko = sb("ko", [P, KVH, P], F32, a)
            ksq = sb("ksq", [P, 2, 4, HD], F32, a)
            kss = sb("kss", [P, KVH], F32, a)
            kv_ = sb("kv_", [P, KVH], F32, a)
            kr = sb("kr", [P, KVH], F32, a)
            xt = [sb(f"xt{q}", [P, D], F32, a) for q in range(2)]
            h1 = sb("h1", [P, D], F32, a)
            st1 = sb("st1", [P, 6], F32, a)
            mv1 = sb("mv1", [P, 2], F32, a)
            ve1 = sb("ve1", [P, 1], F32, a)
            rs1 = sb("rs1", [P, 1], F32, a)
        with ExitStack() as a:
            qs = sb("qs", [P, 2, CB, 2, S], F32, a)
            sq = sb("sq", [P, 2, CB, 2, S], F32, a)
            pb = sb("pb", [P, 8, S], F32, a)
            sqb = sb("sqb", [P, 3, 2, CB, 2, S], BF16, a)
            pt = [sb(f"pt{'hl'[q]}", [P, 2, HG * S], F32R, a) for q in range(2)]
            ah = sb("ah", [P, 2, HG, 2, S], F32R, a)
            al = sb("al", [P, 2, HG, 2, S], F32R, a)
            kt = sb("kt", [P, CB, S], F32, a)
            vt = sb("vt", [P, 2, HD], F32, a)
            wraw = sb("wraw", [P, 512], F32, a)
            vhl = [sb(f"vt{'hl'[q]}", [P, 2, HD], F32R, a) for q in range(2)]
            onec = sb("onec", [P, 1], BF16, a)
            qv = sb("qv", [P, 8], F32, a)
            qr = sb("qr", [P, 8], F32, a)
            mx = sb("mx", [P, 8], F32, a)
            sm = sb("sm", [P, 8], F32, a)
            rc = sb("rc", [P, 8], F32, a)
        with ExitStack() as a:
            h2 = [sb(f"h2{q}", [P, D], F32, a) for q in range(4)]
            draw = sb("draw", [P, 4 * D], F32, a)
            lgT = sb("lgT", [E, T], F32, a)
            lgT2 = sb("lgT2", [E, T], F32, a)
        wdn = sb("wdn", [P, E, D])
        m8 = sb("m8", [P, NT, 8])
        i8 = sb("i8", [P, NT, 8], U32)
        rsm = sb("rsm", [P, NT])
        rsr = sb("rsr", [P, NT])
        cw = sb("cw", [P, 2, NT])
        slf = sb("slf", [P, 2, NT])
        sli = sb("sli", [P, 2, NT], I32)
        nbk = sb("nbk", [P, E])
        endb = sb("endb", [P, E])
        stb = sb("stb", [P, E])
        ebf = sb("ebf", [1, NB])
        ebi = sb("ebi", [1, NB], I32)
        ebw = sb("ebw", [1, NB], I32)
        srow = sb("srow", [NB, P], I32)
        srowf = sb("srowf", [NB, P])
        icur = [sb(f"icur{q}", [P, 1], I32) for q in range(2)]
        st3 = sb("st3", [P, NT, 6])
        mv3 = sb("mv3", [P, NT, 2])
        ve3 = sb("ve3", [P, NT])
        rs3 = sb("rs3", [P, NT])
        nb3 = sb("nb3", [P, NT])
        graw = sb("graw", [P, KD * E])
        with ExitStack() as a:
            g_hl = sb("g_hl", [P, KD, P], F32R, a)
        with ExitStack() as a:
            xg = [sb(f"xg{q}", [P, D], F32, a) for q in range(2)]
        ra = sb("ra", [P, NT, E])
        rb = sb("rb", [P, NT, E])
        oh1 = sb("oh1", [P, NT, E])
        oh2 = sb("oh2", [P, NT, E])
        sgt = [sb(f"sgt{q}", [P, D]) for q in range(1)]
        aft = [sb(f"aft{q}", [P, D]) for q in range(1)]
        rab = sb("rab", [P, NT, E], BF16)
        xt3 = (sgt[0], aft[0])

        PS = [ctx.enter_context(nc.psum_tensor(f"ps{q}", [P, 512], F32)) for q in range(8)]

        setup_in, ident_ok, pool_const, const_act, const_dve = (
            sem("setup_in"), sem("ident_ok"), sem("pool_const"), sem("const_act"), sem("const_dve"))
        ctx_in, x_in, k_stored, v_stored = sem("ctx_in"), sem("x_in"), sem("k_stored"), sem("v_stored")
        kvw_in = [sem(f"kvw_in{q}") for q in range(len(KV_PIECES))]
        kvw_hi, kvw_lo, ctx_hi, ctx_lo = sem("kvw_hi"), sem("kvw_lo"), sem("ctx_hi"), sem("ctx_lo")
        k_done, k_sq, k_ss, k_var, k_rt, kn_done = (
            sem("k_done"), sem("k_sq"), sem("k_ss"), sem("k_var"), sem("k_rt"), sem("kn_done"))
        v_done, v_evac, kT_done, kT_evac = sem("v_done"), sem("v_evac"), sem("kT_done"), sem("kT_evac")
        ln_st, ln_mv, ln_var, ln_rt, h_done, hT_done, hT_hi, hT_lo = (
            sem("ln_st"), sem("ln_mv"), sem("ln_var"), sem("ln_rt"), sem("h_done"), sem("hT_done"),
            sem("hT_hi"), sem("hT_lo"))
        w0_in, w_hi, w_lo, acc_zero = sem("w0_in"), sem("w_hi"), sem("w_lo"), sem("acc_zero")
        wr_in, kt_in, vt_in = sem("wr_in"), sem("kt_in"), sem("vt_in")
        q_done, q_copy, q_sq, ss_done, q_var, q_rt = (
            sem("q_done"), sem("q_copy"), sem("q_sq"), sem("ss_done"), sem("q_var"), sem("q_rt"))
        s_done, s_scaled, s_masked, s_max, s_sub, s_exp, s_sum, s_rcp, p_ready = (
            sem("s_done"), sem("s_scaled"), sem("s_masked"), sem("s_max"), sem("s_sub"), sem("s_exp"),
            sem("s_sum"), sem("s_rcp"), sem("p_ready"))
        sq_pool, sq_b1, sq_r, sq_b2, sq_b3, v_split, pT_hi = (
            sem("sq_pool"), sem("sq_b1"), sem("sq_r"), sem("sq_b2"), sem("sq_b3"), sem("v_split"), sem("pT_hi"))
        pT_done, pT_evac, pv_done, a_hi, a_lo, o_done, acc_done = (
            sem("pT_done"), sem("pT_evac"), sem("pv_done"), sem("a_hi"), sem("a_lo"), sem("o_done"),
            sem("acc_done"))
        x3_in, x1_done, st_done, mv_done, var3, rt3, nb_ok, h2_done, h2_act, h2_stored, h2T_done, h2T_hi, h2T_lo = (
            [sem("x3_in0"), sem("x3_in1")], sem("x1_done"), sem("st_done"), sem("mv_done"), sem("var3"), sem("rt3"),
            sem("nb_ok"), sem("h2_done"), sem("h2_act"), [sem(f"h2_stored{q}") for q in range(4)], sem("h2T_done"), sem("h2T_hi"), sem("h2T_lo"))
        shd_in, shd_hi, shd_lo = sem("shd_in"), sem("shd_hi"), sem("shd_lo")
        g_in, g_hi_ok, g_lo_ok, lg_done, lg_evac, lgt_done = (
            sem("g_in"), sem("g_hi_ok"), sem("g_lo_ok"), sem("lg_done"), sem("lg_evac"), sem("lgt_done"))
        tri_ok, rank_out = sem("tri_ok"), sem("rank_out")
        rt_sub, rt_exp, rt_dve, rank_in, rank_done, slot_ok = (
            sem("rt_sub"), sem("rt_exp"), sem("rt_dve"), sem("rank_in"), sem("rank_done"), sem("slot_ok"))
        zero_st, scat, srow_in, srow_f, srowT, sidx_ok = (
            sem("zero_st"), sem("scat"), sem("srow_in"), sem("srow_f"), sem("srowT"),
            sem("sidx_ok"))
        gu_done, sil, act_f, act_hi, act_lo, dn_done, sh_done = (
            sem("gu_done"), sem("sil"), sem("act_f"), sem("act_hi"), sem("act_lo"), sem("dn_done"),
            sem("sh_done"))
        wgu_in, wgu_last, wdn_in = sem("wgu_in"), sem("wgu_last"), sem("wdn_in")
        ic_ok, xg_in, xgT_done, xgT_evac, eg_done, e_sil, e_act, eT_done, eT_evac, ed_done, ye_ok, y_st = (
            sem("ic_ok"), [sem("xg_in0"), sem("xg_in1")], sem("xgT_done"), sem("xgT_evac"), sem("eg_done"),
            sem("e_sil"), sem("e_act"), sem("eT_done"), sem("eT_evac"), sem("ed_done"), sem("ye_ok"),
            [sem("y_st0"), sem("y_st1")])
        y1_in, y2_in, add1, add2, out_st = (
            [sem(f"y1_in{q}") for q in range(4)], [sem(f"y2_in{q}") for q in range(4)], sem("add1"), sem("add2"), sem("out_st"))

        dve_mark, pool_mark = sem("dve_mark"), sem("pool_mark")

        block = ctx.enter_context(nc.Block())

        @block.sync
        def _(sp):
            for s in (v_stored, k_stored, *y_st, *h2_stored, wgu_last):
                sp.sem_inc(s, 16)
            sp.dma_start(craw[:], ctxT[0]).then_inc(ctx_in, 16)
            for z, (c0, c1) in enumerate(KV_PIECES):
                if z == 3:
                    sp.dma_start(xt[0][:], x[0]).then_inc(x_in, 16)
                src = (wk, wv)[c0 // 4096][:, c0 % 4096:c0 % 4096 + c1 - c0]
                sp.dma_start(accf[:, c0:c1], src).then_inc(kvw_in[z], 16)
            sp.dma_start(qkw[:, 0:1], q_w).then_inc(setup_in, 16)
            sp.dma_start(qkw[:, 1:2], k_w).then_inc(setup_in, 16)
            for j, g in enumerate((g_x, g_f)):
                sp.dma_start(gcol[:, j:j + 1], g.to_broadcast([P, 1])).then_inc(setup_in, 16)
            for j in range(2):
                sp.dma_start(maskb[j * S:(j + 1) * S, :], mask).then_inc(setup_in, 16)
            for n in range(NT):
                if n + 1 < NT:
                    if n >= 1:
                        sp.wait_ge(h_done, n)
                    sp.wait_ge(x_in, 16 * (n + 1))
                    sp.dma_start(xt[(n + 1) % 2][:], x[n + 1]).then_inc(x_in, 16)
                if n % 2 == 0:
                    c = n // 2 + 1
                    sp.wait_ge(ctx_hi, c)
                    sp.wait_ge(ctx_lo, c)
                    sp.dma_start(craw[:], ctxT[c % NC]).then_inc(ctx_in, 16)
                if n == 1:
                    sp.wait_ge(kvw_lo, 3)
                    sp.dma_start(accf[:, 0:4096].rearrange("p (s n) -> p s n", s=NC),
                                 w_att[0:NC].rearrange("s p n -> p s n")).then_inc(w0_in, 16)
                sp.wait_ge(v_evac, 2 * n + 4)
                sp.dma_start(v_st[n // 2, n % 2], vo[:].rearrange("p (g t) -> p g t", g=KVH)).then_inc(v_stored, 16)
                sp.wait_ge(kT_evac, 2 * n + 4)
                sp.dma_start(k_st[n // 2, n % 2], ko[:]).then_inc(k_stored, 16)
            sp.wait_ge(v_stored, 16 * NT + 16)
            sp.wait_ge(k_stored, 16 * NT + 16)
            sp.wait_ge(hT_lo, NT)
            sp.dma_start(kt[:].rearrange("p b t -> p (b t)"), kbuf[0]).then_inc(kt_in, 16)
            sp.dma_start(vt[:].rearrange("p b t -> p (b t)"), vbuf[0]).then_inc(vt_in, 16)
            sp.dma_start(graw[:], gate).then_inc(g_in, 16)

            def next_loads(i, x_tiles=None):
                sp.wait_ge(s_done, i + 1)
                sp.dma_start(kt[:].rearrange("p b t -> p (b t)"), kbuf[i + 1]).then_inc(kt_in, 16)
                sp.wait_ge(v_split, 2 * i + 2)
                sp.dma_start(vt[:].rearrange("p b t -> p (b t)"), vbuf[i + 1]).then_inc(vt_in, 16)
                if x_tiles is not None:
                    x_tiles()
                sp.wait_ge(w_hi, i + 8)
                sp.wait_ge(w_lo, i + 8)
                sp.dma_start(wraw[:], w_att[i + NC]).then_inc(wr_in, 16)

            with sp.Fori(0, STEPS - NC) as i:
                next_loads(i)
            next_loads(STEPS - NC)
            sp.dma_start(xt3[0][:], x[0]).then_inc(x3_in[0], 16)
            sp.dma_start(xt3[1][:], x[1]).then_inc(x3_in[1], 16)
            next_loads(STEPS - NC + 1)
            with sp.Fori(0, NC - 3) as t:
                def x_tiles():
                    for q in range(2):
                        sp.wait_ge(x1_done, 2 * t + 1 + q)
                        sp.dma_start(xt3[q][:], x[2 * t + 2 + q]).then_inc(x3_in[q], 16)

                next_loads(t + STEPS - NC + 2, x_tiles)
            sp.wait_ge(w_hi, STEPS + 7)
            sp.wait_ge(w_lo, STEPS + 7)
            sp.dma_start(wraw[:], w_att[STEPS - 1 + NC]).then_inc(wr_in, 16)
            sp.wait_ge(pT_done, STEPS)
            sp.dma_start(draw[:], w_shd).then_inc(shd_in, 16)
            sp.dma_start(slotbuf.rearrange("(p b) o -> p (b o)", p=P), zi[:]).then_inc(zero_st, 16)
            for n in range(2 * (NC - 2), NT):
                sp.wait_ge(x1_done, n - 1)
                sp.dma_start(xt3[n % 2][:], x[n]).then_inc(x3_in[n % 2], 16)
            for q in range(4):
                sp.wait_ge(h2_done, q + 1)
                sp.dma_start(h2_t[q], h2[q][:]).then_inc(h2_stored[q], 16)
            with sp.Fori(0, NT // 4 - 1) as m:
                for q in range(4):
                    if q % 2:
                        sp.wait_ge(h2_done, 2 * m + 5 + q // 2)
                    else:
                        sp.wait_ge(h2_act, 2 * m + 1 + q // 2)
                    sp.dma_start(h2_t[4 * m + q + 4], h2[q][:]).then_inc(h2_stored[q], 16)
            for q in range(4):
                sp.wait_ge(h2_stored[q], 16 * (NT // 4) + 16)
            sp.wait_ge(shd_lo, 1)
            sp.wait_ge(slot_ok, 1)
            sp.dma_start(wdn[:], w_dn.rearrange("e p n -> p e n")).then_inc(wdn_in, 16)
            def load_gate_up(c, done=wgu_in):
                sp.wait_ge(gu_done, 8 * c + 8)
                sp.dma_start(wgu[:, bass.ds(4 * c, 4), :],
                             w_gu[bass.ds(4 * c, 4)].rearrange("e p n -> p e n")).then_inc(done, 16)

            with sp.Fori(0, 3) as c:
                load_gate_up(c)
            sp.wait_ge(scat, 16 * 2 * NT)
            sp.dma_start(srow[:], slotbuf.rearrange("(b p) o -> b (p o)", p=P)).then_inc(srow_in, 16)
            load_gate_up(3, done=wgu_last)
            def store_block(b, q):
                sp.wait_ge(ye_ok, b + 3)
                sp.dma_start(y_t[b], ye[q][:]).then_inc(y_st[q], 16)

            with sp.Fori(0, NB // 2) as m:
                for q in range(2):
                    store_block(2 * m + q, q)
            store_block(NB - 1, 0)
            with sp.Fori(0, NT) as n:
                sp.wait_ge(add2, n + 1)
                sp.dma_start(out[n], acc[:, n, :]).then_inc(out_st, 16)
            sp.wait_ge(out_st, 16 * NT)
            sp.wait_ge(wdn_in, 16)
            sp.wait_ge(wgu_last, 32)

        @block.gpsimd
        def _(pool):
            pool.memset(mhalf[:], -0.5).then_inc(pool_const, 1)
            pool.memset(ident[:], 0.0).then_inc(ident_ok, 1)
            pool.wait_ge(ident_ok, 1)
            pool.affine_select(out=ident[:], in_=ident[:], compare_op=ALU.not_equal, fill=1.0, base=0,
                               pattern=[[-1, P]], channel_multiplier=1).then_inc(ident_ok, 1)
            pool.memset(zi[:], 0).then_inc(pool_const, 1)
            pool.memset(sidx[:], 0).then_inc(pool_const, 1)
            pool.memset(ones[:], 1.0).then_inc(pool_const, 1)
            pool.memset(onesb[:], 1.0).then_inc(pool_const, 1)
            pool.memset(tri[:], 1.0).then_inc(pool_const, 1)
            pool.wait_ge(pool_const, 6)
            pool.affine_select(out=tri[:], in_=tri[:], compare_op=ALU.is_gt, fill=0.0, base=0,
                               pattern=[[1, P]], channel_multiplier=-1).then_inc(pool_const, 1)
            pool.iota(iota_e[:], pattern=[[1, E]], base=0, channel_multiplier=0,
                      allow_small_or_imprecise_dtypes=True).then_inc(pool_const, 1)
            pool.iota(iota_b[:], pattern=[[1, NB]], base=0, channel_multiplier=0,
                      allow_small_or_imprecise_dtypes=True).then_inc(pool_const, 1)
            pool.iota(tok[:], pattern=[[P, NT]], base=0, channel_multiplier=1).then_inc(pool_const, 1)
            pool.wait_ge(pool_const, 10)
            with pool.Fori(0, NT) as n:
                pool.wait_ge(ln_var, n + 1)
                pool.tensor_tensor(rs1[:], ve1[:], mhalf[:, 0:1], ALU.pow).then_inc(ln_rt, 1)
                pool.wait_ge(k_var, n + 1)
                pool.tensor_tensor(kr[:], kv_[:], mhalf[:, 0:KVH], ALU.pow).then_inc(k_rt, 1)
            pool.wait_ge(kvw_lo, len(KV_PIECES))
            pool.memset(accf[:, 4096:8192], 0.0).then_inc(acc_zero, 1)
            pool.wait_ge(hT_lo, NT)
            pool.wait_ge(v_stored, 16 * NT + 16)
            pool.wait_ge(k_stored, 16 * NT + 16)
            pool.memset(onec[:], 1.0).then_inc(acc_zero, 1)
            for t in (ah, al):
                pool.memset(t[:, 1].rearrange("p h b s -> p (h b s)").bitcast(F32), 0.0).then_inc(acc_zero, 1)

            def split_squares(j):
                flat = lambda t: t.rearrange("p b h s -> p (b h s)")
                part = [flat(sqb[:, z, 0]) for z in range(3)]
                pool.wait_ge(q_sq, 2 * j + 1)
                pool.wait_ge(sq_b1, 2 * j + 1)
                pool.tensor_tensor(flat(sq[:, 0]), flat(sq[:, 0]), part[0], ALU.subtract).then_inc(sq_pool, 1)
                pool.wait_ge(sq_pool, 3 * j + 1)
                pool.sem_inc(pool_mark, 1)
                pool.tensor_copy(part[1], flat(sq[:, 0])).then_inc(sq_pool, 1)
                pool.wait_ge(sq_pool, 3 * j + 2)
                pool.tensor_tensor(part[2], flat(sq[:, 0]), part[1], ALU.subtract).then_inc(sq_pool, 1)

            def inverse_root(j):
                pool.wait_ge(q_var, j + 1)
                pool.tensor_tensor(qr[:], qv[:], mhalf[:, 0:8], ALU.pow).then_inc(q_rt, 1)

            def split_v(j):
                pool.wait_ge(vt_in, 16 * j + 16)
                pool.wait_ge(pv_done, 2 * j + 2)
                pool.sem_inc(pool_mark, 1)
                pool.tensor_copy(vhl[0][:], vt[:]).then_inc(v_split, 1)
                pool.wait_ge(v_split, 2 * j + 1)
                pool.tensor_tensor(vhl[1][:], vt[:], vhl[0][:], ALU.subtract).then_inc(v_split, 1)

            split_squares(0)
            inverse_root(0)
            split_v(0)
            pool.wait_ge(w_hi, 8)
            pool.wait_ge(w_lo, 8)
            pool.memset(accf[:, 0:4096], 0.0).then_inc(acc_zero, 1)
            with pool.Fori(1, STEPS) as j:
                split_squares(j)
                inverse_root(j)
                split_v(j)
            for z, (n0, n1) in enumerate(LN2_GROUPS):
                pool.wait_ge(var3, z + 1)
                pool.tensor_tensor(rs3[:, n0:n1], ve3[:, n0:n1], mhalf[:, 0:n1 - n0], ALU.pow).then_inc(rt3, 1)
            pool.wait_ge(shd_hi, 1)
            pool.wait_ge(o_done, 2 * STEPS + 1)
            pool.tensor_tensor(W[1][0][:, 2048:4096], draw[:], W[1][0][:, 0:2048], ALU.subtract).then_inc(shd_lo, 1)
            pool.wait_ge(slot_ok, 1)
            pool.wait_ge(zero_st, 16)
            for s in range(2):
                for n in range(NT):
                    pool.indirect_dma_start(slotbuf, bass.IndirectOffsetOnAxis(sli[:, s, n:n + 1], 0),
                                            tok[:, n:n + 1], None).then_inc(scat, 16)
            pool.wait_ge(sidx_ok, 1)
            for q in range(4):
                pool.wait_ge(h2_stored[q], 16 * (NT // 4) + 16)

            def gather_block(b, q):
                pool.wait_ge(xgT_done, b + 1)
                pool.tensor_copy(icur[q][:], sidx[:, bass.ds(b, 1)]).then_inc(ic_ok, 1)
                pool.wait_ge(ic_ok, b + 1)
                pool.sem_inc(pool_mark, 1)
                pool.indirect_dma_start(xg[q][:], None, h2buf,
                                        bass.IndirectOffsetOnAxis(icur[q][:, 0:1], 0)).then_inc(xg_in[q], 16)

            with pool.Fori(0, NB // 2) as m:
                for q in range(2):
                    gather_block(2 * m + q, q)
            gather_block(NB - 1, 0)
            pool.wait_ge(y_st[0], 16 * (NB // 2) + 32)
            pool.wait_ge(y_st[1], 16 * (NB // 2) + 16)
            for n in range(NT):
                if n >= 4:
                    pool.wait_ge(add2, n - 3)
                for s, (y, y_in) in enumerate(((y1, y1_in), (y2, y2_in))):
                    pool.indirect_dma_start(y[n % 4][:], None, ybuf,
                                            bass.IndirectOffsetOnAxis(sli[:, s, n:n + 1], 0)).then_inc(y_in[n % 4], 16)

        def group_of(n):
            return 1 + sum(n >= n1 for n0, n1 in LN2_GROUPS)

        def h2_ready(n):
            if n < 4:
                return h2_done, n + 1
            return (h2_done, 5 + (n - 5) // 2) if n % 2 else (h2_act, 1 + (n - 4) // 2)

        def pv_view(bp, b2):
            return PS[4 + b2][:, bp * 256:(bp + 1) * 256].rearrange("p (h s) -> p h s", s=S)

        def split_product(pe, dst, l_hi, l_lo, r_hi, r_lo, first, last):
            pe.matmul(dst, l_hi, r_lo, start=first, stop=False)
            pe.matmul(dst, l_lo, r_hi, start=False, stop=False)
            return pe.matmul(dst, l_hi, r_hi, start=False, stop=last)

        @block.tensor
        def _(pe):
            pe.wait_ge(ident_ok, 2)
            pe.sem_inc(xgT_done, 2)
            pe.sem_inc(ss_done, 1)
            pe.sem_inc(pv_done, 2)

            def kv_half(j, cp, tt):
                for k in range(KD):
                    if j == 0 and k % 2 == 0:
                        pe.wait_ge(kvw_lo, k // 2 + 1)
                    w = slice((j % 2) * 2048 + k * 512, (j % 2) * 2048 + (k + 1) * 512)
                    ts = slice(tt * P, (tt + 1) * P)
                    mm = split_product(pe, PS[j][:], c_hi[cp][:, k, ts], c_lo[cp][:, k, ts],
                                       W[j // 2][0][:, w], W[j // 2][1][:, w], k == 0, k == KD - 1)
                return mm

            with pe.Fori(0, NC // 2) as m:
                for cp in range(2):
                    for tt in range(2):
                        c = 2 * m + cp
                        n = 4 * m + 2 * cp + tt
                        if tt == 0:
                            pe.wait_ge(ctx_hi, c + 1)
                            pe.wait_ge(ctx_lo, c + 1)
                        for j in range(2):
                            if j == 1:
                                pe.wait_ge(kvw_lo, 3)
                            pe.wait_ge(kn_done, 2 * n + 1 + j)
                            kv_half(j, cp, tt).then_inc(k_done, 1)
                        for j in range(2):
                            pe.wait_ge(kvw_lo, j + 4)
                            pe.wait_ge(v_evac, 2 * n + 1 + j)
                            kv_half(2 + j, cp, tt).then_inc(v_done, 1)
                        pe.wait_ge(h_done, n + 1)
                        for k in range(KD):
                            mm = pe.transpose(PS[6][:, k * P:(k + 1) * P], h1[:, k * P:(k + 1) * P], ident[:])
                        mm.then_inc(hT_done, 1)
                        for j in range(2):
                            pe.wait_ge(kn_done, 2 * n + 3 + j)
                            pe.wait_ge(kT_evac, 2 * n + 1 + j)
                            for q in range(4):
                                mm = pe.transpose(PS[4 + j][:, q * P:(q + 1) * P], kn[:, 4 * j + q, :], ident[:])
                            mm.then_inc(kT_done, 1)

            def q_head(hp, h, chunk, w):
                for k in range(KD):
                    c0 = k * 512 + (2 * hp + h) * P
                    hc = [hT[:, bass.ds(chunk, 1), x_, k, :].rearrange("p a t -> p (a t)") for x_ in range(2)]
                    mm = split_product(pe, PS[hp][:, h * CT:(h + 1) * CT], w[0][:, c0:c0 + P],
                                       w[1][:, c0:c0 + P], hc[0], hc[1], k == 0, k == KD - 1)
                return mm

            def scores(j):
                pe.wait_ge(q_copy, 2 * j + 2)
                pe.wait_ge(kt_in, 16 * j + 16)
                for hp in range(2):
                    for b in range(CB):
                        for h in range(2):
                            mm = pe.matmul(PS[3][h * S:(h + 1) * S, (CB * hp + b) * S:(CB * hp + b + 1) * S],
                                           qs[:, hp, b, h], kt[:, b, :], start=True, stop=True)
                mm.then_inc(s_done, 1)

            def q_sums(j):
                pe.wait_ge(sq_pool, 3 * j + 3)
                pe.wait_ge(sq_b1, 2 * j + 2)
                pe.wait_ge(sq_b2, j + 1)
                pe.wait_ge(sq_b3, j + 1)
                for hp in range(2):
                    for b in range(CB):
                        for z in range(3):
                            mm = pe.matmul(PS[2][:, CB * hp + b:CB * hp + b + 1],
                                           sqb[:, z, hp, b].rearrange("p h s -> p (h s)"), onec[:],
                                           start=(z == 0), stop=(z == 2))
                mm.then_inc(ss_done, 1)

            def project_out(bp, w_o, heads):
                for h in heads:
                    c0 = 2048 + h * 512
                    lh, ll = (t[:, bp, h].rearrange("p b s -> p (b s)") for t in (ah, al))
                    mm = split_product(pe, PS[6 + bp][:], lh, ll, w_o[0][:, c0:c0 + 512],
                                       w_o[1][:, c0:c0 + 512], h == 0, h == HG - 1)
                if heads[-1] == HG - 1:
                    mm.then_inc(o_done, 1)

            def transpose_probs(i):
                for m in range(4):
                    if m % 2 == 0:
                        pe.wait_ge(p_ready, 2 * i + 1 + m // 2)
                    src = pb[:, CB * (m // 2) + 2 * (m % 2):CB * (m // 2) + 2 * (m % 2) + 2, :]
                    mm = pe.transpose(PS[2 + m % 2][:, m // 2 * P:(m // 2 + 1) * P], src.rearrange("p b s -> p (b s)"), ident[:])
                mm.then_inc(pT_done, 1)

            def probs_v(i):
                pe.wait_ge(v_split, 2 * i + 2)
                pe.wait_ge(a_hi, 4 * i + 4)
                pe.wait_ge(a_lo, 4 * i + 4)
                for bp in range(2):
                    pe.wait_ge(pT_hi, 2 * i + 1 + bp)
                    pe.wait_ge(pT_evac, 2 * i + 1 + bp)
                    for z, (v_part, p_part) in enumerate(((0, 1), (1, 0), (0, 0))):
                        for b2 in range(2):
                            rows = slice(b2 * S, (b2 + 1) * S)
                            mm = pe.matmul(PS[4 + b2][:, bp * 256:(bp + 1) * 256], vhl[v_part][rows, bp, :],
                                           pt[p_part][rows, bp, :], start=(z == 0), stop=(z == 2))
                            if bp == 1 and z == 2:
                                mm.then_inc(pv_done, 1)

            def step(i, chunk_q, w_q, w_o, w_before, q_ready, o_ready):
                if q_ready is not None:
                    pe.wait_ge(w_lo, q_ready)
                pe.wait_ge(sq_b1, 2 * i + 1)
                q_head(0, 0, chunk_q, w_q)
                q_head(0, 1, chunk_q, w_q).then_inc(q_done, 1)
                pe.wait_ge(sq_b1, 2 * i + 2)
                q_head(1, 0, chunk_q, w_q)
                transpose_probs(i)
                q_head(1, 1, chunk_q, w_q).then_inc(q_done, 1)
                probs_v(i)
                scores(i + 1)
                pe.wait_ge(acc_done, 2 * i + 1)
                project_out(1, w_before, (0, 1, 2))
                q_sums(i + 1)
                project_out(1, w_before, (3,))
                pe.wait_ge(w_lo, o_ready)
                pe.wait_ge(a_hi, 4 * i + 6)
                pe.wait_ge(a_lo, 4 * i + 6)
                pe.wait_ge(acc_done, 2 * i + 2)
                project_out(0, w_o, (0, 1, 2, 3))

            pe.wait_ge(w_lo, 4)
            for hp in range(2):
                q_head(hp, 0, 0, W[0])
                q_head(hp, 1, 0, W[0]).then_inc(q_done, 1)
            scores(0)
            pe.wait_ge(acc_zero, 4)
            q_sums(0)
            def group(i0, p, last=False):
                step(i0, 1, W[p], W[p], W[1 - p], None, i0 + 8)
                with pe.Fori(0, NC - 2) as t:
                    step(i0 + 1 + t, t + 2, W[p], W[p], W[p], None, i0 + 8)
                if not last:
                    step(i0 + NC - 1, 0, W[1 - p], W[p], W[p], i0 + 12, i0 + 8)

            with pe.Fori(0, KVH // 2 - 1) as gg:
                for p in range(2):
                    group(2 * NC * gg + NC * p, p)
            group(STEPS - 2 * NC, 0)
            group(STEPS - NC, 1, last=True)
            pe.wait_ge(acc_done, 2 * STEPS - 1)
            pe.wait_ge(a_hi, 4 * STEPS)
            pe.wait_ge(a_lo, 4 * STEPS)
            project_out(1, W[1], (0, 1, 2, 3))
            transpose_probs(STEPS - 1)
            probs_v(STEPS - 1)
            pe.wait_ge(a_hi, 4 * STEPS + 2)
            pe.wait_ge(a_lo, 4 * STEPS + 2)
            pe.wait_ge(acc_done, 2 * STEPS)
            project_out(0, W[1], (0, 1, 2, 3))
            pe.wait_ge(a_hi, 4 * STEPS + 4)
            pe.wait_ge(a_lo, 4 * STEPS + 4)
            pe.wait_ge(acc_done, 2 * STEPS + 1)
            project_out(1, W[1], (0, 1, 2, 3))

            pe.wait_ge(g_lo_ok, 1)

            def transpose_h2(n):
                pe.wait_ge(*h2_ready(n))
                if n >= 4:
                    pe.wait_ge(h2T_lo, n - 3)
                for k in range(KD):
                    mm = pe.transpose(PS[n % 4][:, k * P:(k + 1) * P], h2[n % 4][:, k * P:(k + 1) * P], ident[:])
                mm.then_inc(h2T_done, 1)

            for n in range(4):
                transpose_h2(n)
            for c in range(4):
                if c < 3:
                    for n in range(4 * c + 4, 4 * c + 8):
                        transpose_h2(n)
                pe.wait_ge(h2T_hi, 4 * c + 4)
                pe.wait_ge(h2T_lo, 4 * c + 4)
                if c == 2:
                    pe.wait_ge(acc_done, 2 * STEPS + 3)
                for k in range(KD):
                    for x_ in (1, 0):
                        mm = pe.matmul(PS[4 + c][:], g_hl[:, k, :], hT[:, 2 * c:2 * c + 2, x_, k, :],
                                       start=(k == 0 and x_ == 1), stop=(k == KD - 1 and x_ == 0))
                mm.then_inc(lg_done, 1)

            def gate_up(c, it, halves=(0, 1)):
                if halves[0] == 0:
                    pe.wait_ge(act_f, 4 * c + it + 1)
                for u in halves:
                    for k in range(KD):
                        c0 = k * 2 * SI + u * SI + it * P
                        mm = split_product(pe, PS[2 * (it % 2) + u][:], W[0][0][:, c0:c0 + P],
                                           W[0][1][:, c0:c0 + P], hT[:, bass.ds(2 * c, 2), 0, k, :],
                                           hT[:, bass.ds(2 * c, 2), 1, k, :], k == 0, k == KD - 1)
                    mm.then_inc(gu_done, 1)

            def down(c, it):
                pe.wait_ge(act_lo, 4 * c + it + 1)
                for tl in range(4):
                    if it == 0:
                        pe.wait_ge(sh_done, 4 * c + tl + 1)
                    c0 = it * 512
                    mm = split_product(pe, PS[4 + tl][:], W[1][1][:, c0 + tl * P:c0 + (tl + 1) * P],
                                       W[1][1][:, 2048 + c0 + tl * P:2048 + c0 + (tl + 1) * P],
                                       W[1][0][:, c0:c0 + 512], W[1][0][:, 2048 + c0:2048 + c0 + 512],
                                       it == 0, it == 3)
                    if it == 3:
                        mm.then_inc(dn_done, 1)

            def shared(c):
                for it in range(3):
                    gate_up(c, it)
                down(c, 0)
                gate_up(c, 3)
                for it in range(1, 4):
                    down(c, it)

            gate_up(0, 0, (0,))
            pe.wait_ge(lg_evac, 8)
            for n in range(NT):
                pe.transpose(PS[4][:, n * E:(n + 1) * E], lgT[:, n * P:(n + 1) * P], ident[0:E, 0:E])
                mm = pe.transpose(PS[4][:, (NT + n) * E:(NT + n + 1) * E], lgT2[:, n * P:(n + 1) * P],
                                  ident[0:E, 0:E])
            mm.then_inc(lgt_done, 1)
            gate_up(0, 0, (1,))
            gate_up(0, 1)
            gate_up(0, 2)
            pe.wait_ge(tri_ok, 1)
            pe.wait_ge(rank_in, 1)
            counts = rab[:].rearrange("p n e -> p (n e)")
            pe.matmul(PS[5][:, 0:NT * E], trib[:], counts, start=True, stop=False)
            for d in range(1, NT):
                pe.matmul(PS[5][:, d * E:NT * E], onesb[:], counts[:, 0:(NT - d) * E], start=False, stop=(d == NT - 1))
            for n in range(NT):
                mm = pe.matmul(PS[6][:, 0:E], onesb[:], rab[:, n, :], start=(n == 0), stop=(n == NT - 1))
            mm.then_inc(rank_done, 1)
            gate_up(0, 3)
            pe.wait_ge(shd_lo, 1)
            pe.wait_ge(rank_out, 2)
            for it in range(4):
                down(0, it)
            with pe.Fori(1, 3) as c:
                shared(c)
            gate_up(3, 0)
            pe.wait_ge(srow_f, 1)
            pe.wait_ge(sh_done, 16)
            pe.transpose(PS[7][:, 0:NB], srowf[:], ident[0:NB, 0:NB]).then_inc(srowT, 1)
            gate_up(3, 1)
            gate_up(3, 2)

            def expert_T(b, q):
                pe.wait_ge(xg_in[q], 8 * (b - q) + 16)
                for k in range(KD):
                    mm = pe.transpose(PS[q][:, k * P:(k + 1) * P], xg[q][:, k * P:(k + 1) * P], ident[:])
                mm.then_inc(xgT_done, 1)

            def expert_gate_up(b, q, e, ks):
                for k in ks:
                    mm = pe.matmul(PS[2 + q][:, 0:2 * EI], xgT[q][:, k, :],
                                   wgu[:, bass.ds(e, 1), k * 2 * EI:(k + 1) * 2 * EI].rearrange("p a n -> p (a n)"),
                                   start=(k == 0), stop=(k == KD - 1))
                if ks[-1] == KD - 1:
                    mm.then_inc(eg_done, 1)

            def expert_of(b, early=False):
                e = pe.value_load(ebi[0:1, bass.ds(b, 1)], min_val=0, max_val=E - 1)
                if early:
                    return e, pe.value_load(ebw[0:1, bass.ds(b, 1)], min_val=16, max_val=32)
                return e

            def expert_down(b, q):
                e = expert_of(b)
                pe.wait_ge(eT_evac, b + 1)
                pe.wait_ge(ye_ok, b + 1)
                pe.matmul(PS[5 + q][:], acteT[:], wdn[:, bass.ds(e, 1), :].rearrange("p a n -> p (a n)"),
                          start=True, stop=True).then_inc(ed_done, 1)

            gate_up(3, 3, (0,))
            pe.wait_ge(act_f, 17)
            expert_T(0, 0)
            expert_T(1, 1)
            e0, loads0 = expert_of(0, early=True)
            gate_up(3, 3, (1,))
            pe.wait_ge(wdn_in, 16)
            pe.wait_ge(wgu_in, 48)
            pe.wait_ge(wgu_last, loads0)
            pe.wait_ge(sil, 16)
            pe.wait_ge(xgT_evac, 1)
            expert_gate_up(0, 0, e0, range(KD))
            pe.wait_ge(act_f, 18)
            def expert_step(b, q, early=False):
                if not isinstance(b, int) or b + 2 < NB:
                    expert_T(b + 2, q)
                e = expert_of(b + 1, early)
                if early:
                    e, loads = e
                    pe.wait_ge(wgu_last, loads)
                pe.wait_ge(xgT_evac, b + 2)
                expert_gate_up(b + 1, 1 - q, e, (0, 1))
                pe.wait_ge(e_act, b + 1)
                pe.transpose(PS[4][:, 0:P], acte[:], ident[:]).then_inc(eT_done, 1)
                expert_gate_up(b + 1, 1 - q, e, (2, 3))
                expert_down(b, q)

            for b in range(2):
                expert_step(b, b, early=True)
            pe.wait_ge(wgu_last, 32)
            with pe.Fori(1, PAIRS) as m:
                for q in range(2):
                    expert_step(2 * m + q, q)
            expert_step(NB - 3, 0)
            expert_step(NB - 2, 1)
            pe.wait_ge(e_act, NB)
            pe.transpose(PS[4][:, 0:P], acte[:], ident[:]).then_inc(eT_done, 1)
            expert_down(NB - 1, 0)
            pe.wait_ge(ye_ok, NB + 2)
            pe.wait_ge(eT_evac, NB)
            pe.wait_ge(sidx_ok, 1)
            for it in range(4):
                down(3, it)

        @block.scalar
        def _(act):
            act.sem_inc(v_evac, 2)
            act.sem_inc(kT_evac, 2)
            act.sem_inc(a_hi, 4)
            act.wait_ge(ctx_in, 16)
            act.copy(c_hi[0][:], craw[:]).then_inc(ctx_hi, 1)
            for z, (c0, c1) in enumerate(KV_PIECES):
                act.wait_ge(kvw_in[z], 16)
                act.copy(W[c0 // 4096][0][:, c0 % 4096:c0 % 4096 + c1 - c0], accf[:, c0:c1]).then_inc(kvw_hi, 1)
            act.wait_ge(setup_in, 96)
            act.activation(tg[:], gcol[:], ACT.Tanh).then_inc(const_act, 1)
            act.wait_ge(const_dve, 1)
            def split_first(slices):
                for z in slices:
                    act.copy(W[0][0][:, z * 512:(z + 1) * 512], accf[:, z * 512:(z + 1) * 512]).then_inc(w_hi, 1)

            def kv_tile(c, n, cp, tt, n_last=False):
                if tt == 1:
                    act.wait_ge(ctx_in, 16 * c + 32)
                    act.copy(c_hi[1 - cp][:], craw[:]).then_inc(ctx_hi, 1)
                for j in range(2):
                    act.wait_ge(k_done, 2 * n + 1 + j)
                    act.activation(ksq[:, j].rearrange("p g d -> p (g d)"), PS[j][:],
                                   ACT.Square).then_inc(k_sq, 1)
                if n_last:
                    act.wait_ge(w0_in, 16)
                    act.wait_ge(k_done, 2 * NT)
                    split_first(range(0, 4))
                act.wait_ge(v_stored, 16 * n + 16)
                for j in range(2):
                    act.wait_ge(v_done, 2 * n + 1 + j)
                    act.copy(vo[:, j * 512:(j + 1) * 512], PS[2 + j][:]).then_inc(v_evac, 1)
                act.wait_ge(hT_done, n + 1)
                act.copy(hT[:, bass.ds(c, 1), 0, :, tt * P:(tt + 1) * P].rearrange("p a k t -> p (a k) t"),
                         PS[6][:].rearrange("p (k t) -> p k t", k=KD)).then_inc(hT_hi, 1)
                act.wait_ge(k_stored, 16 * n + 16)
                for j in range(2):
                    act.wait_ge(kT_done, 2 * n + 1 + j)
                    act.activation(ko[:, 4 * j:4 * j + 4, :].rearrange("p g t -> p (g t)"), PS[4 + j][:],
                                   ACT.Copy, scale=wqk[:, 0:1]).then_inc(kT_evac, 1)

            with act.Fori(0, NC // 2 - 1) as m:
                for cp in range(2):
                    for tt in range(2):
                        kv_tile(2 * m + cp, 4 * m + 2 * cp + tt, cp, tt)
            for n in range(NT - 4, NT):
                kv_tile(n // 2, n, n // 2 % 2, n % 2, n_last=(n == NT - 1))
            act.wait_ge(v_stored, 16 * NT + 16)
            act.wait_ge(k_stored, 16 * NT + 16)
            act.wait_ge(hT_lo, NT)

            q_view = lambda hp: PS[hp][:].rearrange("p (h b s) -> p b h s", h=2, b=CB)

            def q_out(hp, j):
                act.wait_ge(q_done, 2 * j + 1 + hp)
                act.copy(qs[:, hp], q_view(hp)).then_inc(q_copy, 1)

            def squares(hp, j):
                act.wait_ge(ss_done, j + 1)
                act.activation(sq[:, hp], q_view(hp), ACT.Square).then_inc(q_sq, 1)
                act.activation(sqb[:, 0, hp], q_view(hp), ACT.Square).then_inc(sq_b1, 1)


            def squares_2(j):
                act.wait_ge(sq_r, j + 1)
                act.copy(sqb[:, 1, 1], sq[:, 1]).then_inc(sq_b2, 1)

            def exps(j):
                for hp in range(2):
                    act.wait_ge(s_sub, 2 * j + 1 + hp)
                    act.activation(pb[:, CB * hp:CB * hp + CB, :], pb[:, CB * hp:CB * hp + CB, :], ACT.Exp).then_inc(
                        s_exp, 1)

            for hp in range(2):
                q_out(hp, 0)
                squares(hp, 0)
            squares_2(0)
            split_first(range(4, 8))
            exps(0)

            def probs_hi(i):
                act.wait_ge(pT_done, i + 1)
                for bp in range(2):
                    act.copy(pt[0][:, bp, :], PS[2 + bp][:, 0:HG * S]).then_inc(pT_hi, 1)

            def a_hi_tile(i, bp):
                if bp == 1:
                    act.wait_ge(o_done, 2 * i + 1)
                    act.wait_ge(a_lo, 4 * i + 6)
                for b2 in range(2):
                    act.wait_ge(pv_done, 2 * i + 3 + b2)
                    act.copy(ah[:, bp, :, b2, :], pv_view(bp, b2)).then_inc(a_hi, 1)

            def split_slice(i, w, sl):
                act.wait_ge(wr_in, 16 * i + 16)
                act.copy(w[0][:, bass.ds(sl * 512, 512)] if not isinstance(sl, int) else
                         w[0][:, sl * 512:(sl + 1) * 512], wraw[:]).then_inc(w_hi, 1)

            def act_step(i, w, sl):
                act.wait_ge(s_done, i + 1)
                q_out(0, i + 1)
                squares(0, i + 1)
                probs_hi(i)
                q_out(1, i + 1)
                squares(1, i + 1)
                a_hi_tile(i, 0)
                squares_2(i + 1)
                a_hi_tile(i, 1)
                split_slice(i, w, sl)
                exps(i + 1)

            with act.Fori(0, KVH // 2 - 1) as gg:
                for p in range(2):
                    i0 = 2 * NC * gg + NC * p
                    with act.Fori(0, NC) as t:
                        act_step(i0 + t, W[1 - p], t)
            act.wait_ge(g_in, 16)
            act.wait_ge(const_dve, 2)
            act.copy(g_hl[:, :, 0:E], graw[:].rearrange("p (k e) -> p k e", k=KD)).then_inc(g_hi_ok, 1)
            for p in range(2):
                i0 = STEPS - 2 * NC + NC * p
                with act.Fori(0, NC - p) as t:
                    act_step(i0 + t, W[1 - p], t)
            probs_hi(STEPS - 1)
            a_hi_tile(STEPS - 1, 0)
            a_hi_tile(STEPS - 1, 1)
            split_slice(STEPS - 1, W[0], NC - 1)

            act.wait_ge(shd_in, 16)
            act.copy(W[1][0][:, 0:2048], draw[:]).then_inc(shd_hi, 1)
            for n in range(NT):
                act.wait_ge(h2T_done, n + 1)
                act.copy(hT[:, n // 2, 0, :, (n % 2) * P:(n % 2 + 1) * P],
                         PS[n % 4][:].rearrange("p (k t) -> p k t", k=KD)).then_inc(h2T_hi, 1)
                if n + 4 < NT and n % 2 == 0:
                    act.wait_ge(nb_ok, group_of(n + 4))
                    act.wait_ge(rt3, group_of(n + 4))
                    act.wait_ge(h2_stored[n % 4], 16 * (n // 4) + 32)
                    act.activation(h2[n % 4][:], acc[:, n + 4, :], ACT.Identity, bias=nb3[:, n + 4:n + 5],
                                   scale=rs3[:, n + 4:n + 5]).then_inc(h2_act, 1)
            for c in range(4):
                act.wait_ge(lg_done, c + 1)
                act.copy(lgT[:, c * 512:(c + 1) * 512], PS[4 + c][0:E, :]).then_inc(lg_evac, 1)
                act.copy(lgT2[:, c * 512:(c + 1) * 512], PS[4 + c][2 * E:3 * E, :]).then_inc(lg_evac, 1)
            def xT_out(b, q):
                act.wait_ge(xgT_done, b + 3)
                act.copy(xgT[q][:].rearrange("p k t -> p (k t)"), PS[q][:]).then_inc(xgT_evac, 1)

            def silu_split(c, first=False):
                for it in range(4):
                    act.wait_ge(gu_done, 8 * c + 2 * it + 1)
                    act.wait_ge(act_f, 4 * c + it + 2)
                    act.activation(sgt[0][:], PS[2 * (it % 2)][:], ACT.Silu).then_inc(sil, 1)
                    if first and it == 0:
                        act.wait_ge(rt_sub, 1)
                        act.activation(rb[:], ra[:], ACT.Exp).then_inc(rt_exp, 1)
                    if isinstance(c, int) and c == 3 and it == 3:
                        act.wait_ge(gu_done, 32)
                        xT_out(0, 0)
                    act.wait_ge(act_f, 4 * c + it + 3)
                    act.copy(W[1][1][:, it * 512:(it + 1) * 512], aft[0][:]).then_inc(act_hi, 1)

            silu_split(0, first=True)
            with act.Fori(1, 3) as c:
                silu_split(c)
            silu_split(3)

            def silu(b, q):
                act.wait_ge(eg_done, b + 1)
                act.activation(sge[:], PS[2 + q][:, 0:EI], ACT.Silu).then_inc(e_sil, 1)

            xT_out(1, 1)
            silu(0, 0)

            def act_block(b, q):
                if not isinstance(b, int) or b + 2 < NB:
                    act.wait_ge(eg_done, b + 1)
                    xT_out(b + 2, q)
                act.wait_ge(e_act, b + 1)
                silu(b + 1, 1 - q)

            with act.Fori(0, PAIRS) as m:
                for q in range(2):
                    act_block(2 * m + q, q)
            act_block(NB - 3, 0)
            act_block(NB - 2, 1)

        @block.vector
        def _(dve):
            dve.sem_inc(kn_done, 2)
            dve.sem_inc(a_lo, 4)
            dve.sem_inc(acc_done, 2)
            dve.sem_inc(act_f, 2)
            dve.sem_inc(sh_done, 4)
            dve.sem_inc(ye_ok, 2)
            dve.wait_ge(ctx_hi, 1)
            dve.tensor_tensor(c_lo[0][:], craw[:], c_hi[0][:], ALU.subtract).then_inc(ctx_lo, 1)
            for z, (c0, c1) in enumerate(KV_PIECES):
                dve.wait_ge(kvw_hi, z + 1)
                cs = slice(c0 % 4096, c0 % 4096 + c1 - c0)
                dve.tensor_tensor(W[c0 // 4096][1][:, cs], accf[:, c0:c1], W[c0 // 4096][0][:, cs],
                                  ALU.subtract).then_inc(kvw_lo, 1)
            dve.wait_ge(setup_in, 96)
            dve.tensor_tensor(wqk[:], qkw[:, 0:1], qkw[:, 1:2], ALU.mult).then_inc(const_dve, 1)
            def rest_first(slices):
                for z in slices:
                    dve.wait_ge(w_hi, z + 1)
                    cs = slice(z * 512, (z + 1) * 512)
                    dve.tensor_tensor(W[0][1][:, cs], accf[:, cs], W[0][0][:, cs], ALU.subtract).then_inc(w_lo, 1)

            def kv_tile(c, n, cp, tt, n_last=False):
                dve.wait_ge(x_in, 16 * n + 16)
                dve.bn_stats(st1[:], xt[tt][:]).then_inc(ln_st, 1)
                dve.wait_ge(ln_st, n + 1)
                dve.sem_inc(dve_mark, 1)
                dve.bn_aggr(mv1[:], st1[:]).then_inc(ln_mv, 1)
                dve.wait_ge(ln_mv, n + 1)
                dve.tensor_scalar(ve1[:], mv1[:, 1:2], EPS, None, ALU.add).then_inc(ln_var, 1)
                if tt == 1:
                    dve.wait_ge(ctx_hi, c + 2)
                    dve.tensor_tensor(c_lo[1 - cp][:], craw[:], c_hi[1 - cp][:],
                                      ALU.subtract).then_inc(ctx_lo, 1)
                dve.wait_ge(ln_rt, n + 1)
                dve.tensor_scalar(h1[:], xt[tt][:], mv1[:, 0:1], rs1[:, 0:1], ALU.subtract,
                                  ALU.mult).then_inc(h_done, 1)
                dve.wait_ge(k_sq, 2 * n + 2)
                dve.tensor_reduce(kss[:], ksq[:].rearrange("p j g d -> p (j g) d"), AX,
                                  ALU.add).then_inc(k_ss, 1)
                dve.wait_ge(k_ss, n + 1)
                dve.tensor_scalar(kv_[:], kss[:], 1.0 / HD, EPS, ALU.mult, ALU.add).then_inc(k_var, 1)
                dve.wait_ge(k_rt, n + 1)
                for j in range(2):
                    dve.tensor_tensor(kn[:, 4 * j:4 * j + 4, :],
                                      PS[j][:].rearrange("p (g d) -> p g d", d=HD),
                                      kr[:, 4 * j:4 * j + 4].unsqueeze(2).to_broadcast([P, 4, HD]),
                                      ALU.mult).then_inc(kn_done, 1)
                if n_last:
                    rest_first(range(0, 4))
                dve.wait_ge(hT_hi, n + 1)
                ts = slice(tt * P, (tt + 1) * P)
                dve.tensor_tensor(hT[:, bass.ds(c, 1), 1, :, ts].rearrange("p a k t -> p (a k) t"),
                                  PS[6][:].rearrange("p (k t) -> p k t", k=KD),
                                  hT[:, bass.ds(c, 1), 0, :, ts].rearrange("p a k t -> p (a k) t"),
                                  ALU.subtract).then_inc(hT_lo, 1)

            with dve.Fori(0, NC // 2 - 1) as m:
                for cp in range(2):
                    for tt in range(2):
                        kv_tile(2 * m + cp, 4 * m + 2 * cp + tt, cp, tt)
            for n in range(NT - 4, NT):
                kv_tile(n // 2, n, n // 2 % 2, n % 2, n_last=(n == NT - 1))

            def squares_rest(j):
                dve.wait_ge(sq_b1, 2 * j + 2)
                dve.wait_ge(q_sq, 2 * j + 2)
                dve.tensor_tensor(sq[:, 1], sq[:, 1], sqb[:, 0, 1], ALU.subtract).then_inc(sq_r, 1)

            def squares_last(j):
                dve.wait_ge(sq_r, j + 1)
                dve.wait_ge(sq_b2, j + 1)
                dve.tensor_tensor(sqb[:, 2, 1], sq[:, 1], sqb[:, 1, 1], ALU.subtract).then_inc(sq_b3, 1)

            def add_out(count, bp, tile):
                dve.wait_ge(o_done, count)
                dst = accf[:, bass.ds(tile * D, D)] if not isinstance(tile, int) else \
                    accf[:, tile * D:(tile + 1) * D]
                dve.tensor_tensor(dst, PS[6 + bp][:], dst, ALU.add).then_inc(acc_done, 1)

            def a_rest(i, bp):
                for b2 in range(2):
                    dve.wait_ge(a_hi, 4 * i + 5 + 2 * bp + b2)
                    dve.tensor_tensor(al[:, bp, :, b2, :], pv_view(bp, b2), ah[:, bp, :, b2, :],
                                      ALU.subtract).then_inc(a_lo, 1)

            def softmax(j, *meanwhile):
                per_row = lambda t: t[:].unsqueeze(2).to_broadcast([P, 8, S])
                dve.wait_ge(ss_done, j + 2)
                dve.tensor_scalar(qv[:], PS[2][:, 0:8], HD * EPS, None, ALU.add).then_inc(q_var, 1)
                half = lambda t, hp: t[:, CB * hp:CB * hp + CB, :]
                half_row = lambda t, hp: t[:, CB * hp:CB * hp + CB].unsqueeze(2).to_broadcast([P, CB, S])
                if meanwhile:
                    meanwhile[0]()
                dve.wait_ge(q_rt, j + 1)
                dve.wait_ge(s_done, j + 1)
                dve.tensor_tensor(pb[:], PS[3][:].rearrange("p (b s) -> p b s", s=S), per_row(qr),
                                  ALU.mult).then_inc(s_scaled, 1)
                dve.wait_ge(s_scaled, j + 1)
                dve.tensor_tensor(pb[:], pb[:], maskb[:].unsqueeze(1).to_broadcast([P, 8, S]),
                                  ALU.add).then_inc(s_masked, 1)
                dve.wait_ge(s_masked, j + 1)
                dve.tensor_reduce(mx[:], pb[:], AX, ALU.max).then_inc(s_max, 1)
                dve.wait_ge(s_max, j + 1)
                for hp in range(2):
                    dve.tensor_tensor(half(pb, hp), half(pb, hp), half_row(mx, hp), ALU.subtract).then_inc(s_sub, 1)
                if meanwhile:
                    meanwhile[1]()
                dve.wait_ge(s_exp, 2 * j + 2)
                dve.tensor_reduce(sm[:], pb[:], AX, ALU.add).then_inc(s_sum, 1)
                dve.wait_ge(s_sum, j + 1)
                dve.reciprocal(rc[:], sm[:]).then_inc(s_rcp, 1)
                dve.wait_ge(s_rcp, j + 1)
                for hp in range(2):
                    dve.tensor_tensor(half(pb, hp), half(pb, hp), half_row(rc, hp), ALU.mult).then_inc(p_ready, 1)

            def probs_lo(i):
                for bp in range(2):
                    dve.wait_ge(pT_hi, 2 * i + 1 + bp)
                    dve.tensor_tensor(pt[1][:, bp, :], PS[2 + bp][:, 0:HG * S], pt[0][:, bp, :],
                                      ALU.subtract).then_inc(pT_evac, 1)

            def slice_lo(i, w, sl):
                dve.wait_ge(w_hi, i + 9)
                ws = bass.ds(sl * 512, 512) if not isinstance(sl, int) else slice(sl * 512, (sl + 1) * 512)
                dve.tensor_tensor(w[1][:, ws], wraw[:], w[0][:, ws], ALU.subtract).then_inc(w_lo, 1)

            def residual(n, b):
                row = acc[:, n, :] if isinstance(n, int) else acc[:, bass.ds(n, 1), :].rearrange("p a d -> p (a d)")
                st = st3[:, n, :] if isinstance(n, int) else st3[:, bass.ds(n, 1), :].rearrange("p a d -> p (a d)")
                dve.wait_ge(x3_in[b], 8 * (n - b) + 16)
                dve.scalar_tensor_tensor(out=row, in0=row, scalar=tg[:, 0:1], in1=xt3[b][:],
                                         op0=ALU.mult, op1=ALU.add).then_inc(x1_done, 1)
                dve.wait_ge(x1_done, n + 1)
                dve.bn_stats(st, row).then_inc(st_done, 1)

            def dve_step(i, w, sl, tile, tile_before, complete=(None, None)):
                probs_lo(i)
                if complete[0] is not None:
                    residual(complete[0], 1)
                squares_rest(i + 1)
                a_rest(i, 0)
                squares_last(i + 1)
                if complete[1] is not None:
                    residual(complete[1], 0)

                def while_root():
                    add_out(2 * i + 1, 1, tile_before)
                    a_rest(i, 1)

                softmax(i + 1, while_root, lambda: add_out(2 * i + 2, 0, tile))
                slice_lo(i, w, sl)

            dve.wait_ge(v_stored, 16 * NT + 16)
            dve.wait_ge(k_stored, 16 * NT + 16)
            squares_rest(0)
            squares_last(0)
            softmax(0, lambda: rest_first(range(4, 8)), lambda: None)
            dve.wait_ge(pool_const, 10)
            dve.tensor_copy(trib[:], tri[:]).then_inc(tri_ok, 1)
            dve.memset(g_hl[:].rearrange("p k e -> p (k e)").bitcast(F32), 0.0).then_inc(const_dve, 1)
            dve.wait_ge(acc_zero, 5)
            def group(i0, p):
                dve_step(i0, W[1 - p], 0, 0, NT - 1)
                with dve.Fori(0, NC - 2) as t:
                    dve_step(i0 + 1 + t, W[1 - p], t + 1, 2 * t + 2, 2 * t + 1)
                dve_step(i0 + NC - 1, W[1 - p], NC - 1, NT - 2, NT - 3)

            with dve.Fori(0, KVH // 2 - 1) as gg:
                for p in range(2):
                    group(2 * NC * gg + NC * p, p)
            dve.wait_ge(g_hi_ok, 1)
            dve.wait_ge(const_dve, 2)
            dve.tensor_tensor(g_hl[:, :, 2 * E:3 * E], graw[:].rearrange("p (k e) -> p k e", k=KD), g_hl[:, :, 0:E],
                              ALU.subtract).then_inc(g_lo_ok, 1)
            group(STEPS - 2 * NC, 0)
            i0 = STEPS - NC
            dve_step(i0, W[0], 0, 0, NT - 1)
            dve.wait_ge(const_act, 1)
            dve_step(i0 + 1, W[0], 1, 2, 1, (None, 0))
            with dve.Fori(0, NC - 3) as t:
                dve_step(i0 + 2 + t, W[0], t + 2, 2 * t + 4, 2 * t + 3, (2 * t + 1, 2 * t + 2))

            def statistics(z):
                n0, n1 = LN2_GROUPS[z]
                for n in range(n0, n1):
                    dve.wait_ge(st_done, n + 1)
                    dve.bn_aggr(mv3[:, n, :], st3[:, n, :]).then_inc(mv_done, 1)
                dve.wait_ge(mv_done, n1)
                dve.tensor_scalar(ve3[:, n0:n1], mv3[:, n0:n1, 1], EPS, None, ALU.add).then_inc(var3, 1)

            def normalise(n):
                dve.wait_ge(rt3, group_of(n))
                if n >= 4:
                    dve.wait_ge(h2_stored[n % 4], 16 * (n // 4) + 16)
                dve.tensor_scalar(h2[n % 4][:], acc[:, n, :], mv3[:, n, 0:1], rs3[:, n:n + 1], ALU.subtract,
                                  ALU.mult).then_inc(h2_done, 1)

            def shift(z):
                ts = slice(*LN2_GROUPS[z])
                dve.wait_ge(rt3, z + 1)
                dve.scalar_tensor_tensor(out=nb3[:, ts], in0=mv3[:, ts, 0], scalar=-1.0, in1=rs3[:, ts],
                                         op0=ALU.mult, op1=ALU.mult).then_inc(nb_ok, 1)

            def h2T_rest(n):
                dve.wait_ge(h2T_hi, n + 1)
                part = [hT[:, n // 2, x_, :, (n % 2) * P:(n % 2 + 1) * P] for x_ in range(2)]
                dve.tensor_tensor(part[1], PS[n % 4][:].rearrange("p (k t) -> p k t", k=KD), part[0],
                                  ALU.subtract).then_inc(h2T_lo, 1)

            i = STEPS - 1
            add_out(2 * i + 1, 1, 13)
            probs_lo(i)
            statistics(0)
            a_rest(i, 0)
            a_rest(i, 1)
            residual(11, 1)
            residual(12, 0)
            for n in range(4):
                normalise(n)
            shift(0)
            dve.wait_ge(acc_done, 2 * i + 3)
            residual(13, 1)
            statistics(1)
            slice_lo(i, W[0], NC - 1)
            add_out(2 * i + 2, 0, 14)
            dve.wait_ge(acc_done, 2 * i + 4)
            residual(14, 0)
            add_out(2 * i + 3, 1, 15)
            shift(1)
            for n in range(4):
                h2T_rest(n)
                if n % 2:
                    normalise(n + 4)
            dve.wait_ge(acc_done, 2 * i + 5)
            residual(15, 1)
            statistics(2)
            for n in range(4, NT):
                h2T_rest(n)
                if n % 2 and n + 4 < NT:
                    normalise(n + 4)
                if n == 6:
                    shift(2)

            def shared_in(c, it):
                dve.wait_ge(sil, 4 * c + it + 1)
                dve.wait_ge(gu_done, 8 * c + 2 * it + 2)
                if not (isinstance(c, int) and c == 0 and it == 0):
                    dve.wait_ge(act_lo, 4 * c + it)
                dve.tensor_tensor(aft[0][:], PS[2 * (it % 2) + 1][:], sgt[0][:], ALU.mult).then_inc(act_f, 1)
                dve.wait_ge(act_f, 4 * c + it + 3)
                dve.wait_ge(act_hi, 4 * c + it + 1)
                dve.tensor_tensor(W[1][1][:, 2048 + it * 512:2048 + (it + 1) * 512], aft[0][:],
                                  W[1][1][:, it * 512:(it + 1) * 512], ALU.subtract).then_inc(act_lo, 1)

            def shared_out(c):
                for tl in range(4):
                    dve.wait_ge(dn_done, 4 * c + tl + 1)
                    n = 4 * c + tl
                    dst = accf[:, n * D:(n + 1) * D] if isinstance(n, int) else accf[:, bass.ds(n * D, D)]
                    dve.scalar_tensor_tensor(out=dst, in0=PS[4 + tl][:], scalar=tg[:, 1:2], in1=dst,
                                             op0=ALU.mult, op1=ALU.add).then_inc(sh_done, 1)

            def shared(c):
                for it in range(4):
                    shared_in(c, it)
                shared_out(c)

            links = [0]

            def link(ins):
                links[0] += 1
                ins.then_inc(rt_dve, 1)
                dve.wait_ge(rt_dve, links[0])

            over_e = lambda t: t.unsqueeze(2).to_broadcast([P, NT, E])
            over_n = lambda t: t.unsqueeze(1).to_broadcast([P, NT, E])
            dve.wait_ge(lgt_done, 1)
            logits, logits2 = (PS[4][:, z * NT * E:(z + 1) * NT * E].rearrange("p (n e) -> p n e", e=E)
                               for z in range(2))
            link(dve.tensor_copy(ra[:], logits2))
            link(dve.tensor_tensor(ra[:], logits, ra[:], ALU.add))
            link(dve.tensor_reduce(rsm[:], ra[:], AX, ALU.max))
            dve.tensor_tensor(ra[:], ra[:], over_e(rsm[:]), ALU.subtract).then_inc(rt_sub, 1)
            dve.wait_ge(rt_exp, 1)
            link(dve.tensor_reduce(rsm[:], rb[:], AX, ALU.add))
            link(dve.reciprocal(rsr[:], rsm[:]))
            link(dve.tensor_tensor(rb[:], rb[:], over_e(rsr[:]), ALU.mult))
            for n in range(NT):
                dve.max(m8[:, n, :], rb[:, n, :]).then_inc(mv_done, 1)
            for n in range(NT):
                dve.wait_ge(mv_done, NT + n + 1)
                dve.max_index(i8[:, n, :], m8[:, n, :], rb[:, n, :]).then_inc(st_done, 1)
            shared_in(0, 0)
            link(dve.tensor_tensor(rsm[:], m8[:, :, 0], m8[:, :, 1], ALU.add))
            link(dve.reciprocal(rsr[:], rsm[:]))
            link(dve.tensor_tensor(cw[:, 0, :], m8[:, :, 0], rsr[:], ALU.mult))
            link(dve.tensor_tensor(cw[:, 1, :], m8[:, :, 1], rsr[:], ALU.mult))
            link(dve.tensor_scalar(cw[:], cw[:], tg[:, 1:2], None, ALU.mult))
            dve.wait_ge(st_done, 2 * NT)
            for s, oh in enumerate((oh1, oh2)):
                link(dve.tensor_copy(slf[:, s, :], i8[:, :, s]))
                link(dve.tensor_tensor(oh[:], over_n(iota_e[:]), over_e(slf[:, s, :]), ALU.is_equal))
            dve.tensor_tensor(rab[:], oh1[:], oh2[:], ALU.add).then_inc(rank_in, 1)
            shared_in(0, 1)
            dve.wait_ge(rank_done, 1)
            dve.tensor_copy(ra[:].rearrange("p n e -> p (n e)"), PS[5][:, 0:NT * E]).then_inc(rank_out, 1)
            dve.tensor_scalar(stb[:], PS[6][:, 0:E], 1.0 / P, None, ALU.mult).then_inc(rank_out, 1)
            shared_in(0, 2)
            dve.wait_ge(rank_out, 2)
            link(dve.tensor_tensor(rb[:], over_e(stb[:]), over_n(iota_e[:]), ALU.is_gt))
            link(dve.tensor_reduce(nbk[:], rb[:], AX, ALU.add))
            link(dve.tensor_tensor_scan(endb[:], ones[:, 0:E], nbk[:], 0.0, ALU.mult, ALU.add))
            link(dve.tensor_tensor(stb[:], endb[:], nbk[:], ALU.subtract))
            link(dve.tensor_scalar(stb[:], stb[:], float(P), None, ALU.mult))
            link(dve.tensor_tensor(ra[:], ra[:], over_n(stb[:]), ALU.add))
            shared_in(0, 3)
            for s, oh in enumerate((oh1, oh2)):
                link(dve.tensor_tensor(rb[:], oh[:], ra[:], ALU.mult))
                link(dve.tensor_reduce(slf[:, s, :], rb[:], AX, ALU.add))
            ebt = lgT[0:1, 0:NB * E].rearrange("p (b e) -> p b e", e=E)
            link(dve.tensor_tensor(ebt, endb[0:1, :].unsqueeze(1).to_broadcast([1, NB, E]),
                                   iota_b[0:1, :].unsqueeze(2).to_broadcast([1, NB, E]), ALU.is_le))
            link(dve.tensor_reduce(ebf[:], ebt, AX, ALU.add))
            link(dve.tensor_scalar(ebf[:], ebf[:], float(E - 1), None, ALU.min))
            link(dve.tensor_copy(ebi[:], ebf[:]))
            link(dve.tensor_scalar(ebf[:], ebf[:], float(3 * E // 4), 16.0, ALU.is_ge, ALU.mult))
            link(dve.tensor_scalar(ebf[:], ebf[:], 16.0, None, ALU.add))
            link(dve.tensor_copy(ebw[:], ebf[:]))
            dve.tensor_copy(sli[:], slf[:]).then_inc(slot_ok, 1)
            shared_out(0)
            with dve.Fori(1, 3) as c:
                shared(c)
            dve.wait_ge(srow_in, 16)
            dve.tensor_copy(srowf[:], srow[:]).then_inc(srow_f, 1)
            shared_in(3, 0)
            dve.wait_ge(srowT, 1)
            dve.tensor_copy(sidx[:, 0:NB], PS[7][:, 0:NB]).then_inc(sidx_ok, 1)
            for it in range(1, 4):
                shared_in(3, it)

            def gated(b, q):
                dve.wait_ge(e_sil, b + 1)
                dve.tensor_tensor(acte[:], PS[2 + q][:, EI:2 * EI], sge[:], ALU.mult).then_inc(e_act, 1)

            gated(0, 0)

            def dve_block(b, q):
                dve.wait_ge(eT_done, b + 1)
                dve.tensor_copy(acteT[:], PS[4][:, 0:P]).then_inc(eT_evac, 1)
                if not isinstance(b, int) or b + 1 < NB:
                    gated(b + 1, 1 - q)
                dve.wait_ge(ed_done, b + 1)
                dve.wait_ge(y_st[q], 8 * (b - q) + 16)
                dve.tensor_copy(ye[q][:], PS[5 + q][:]).then_inc(ye_ok, 1)

            with dve.Fori(0, PAIRS) as m:
                for q in range(2):
                    dve_block(2 * m + q, q)
            for b in range(NB - 3, NB):
                dve_block(b, b % 2)

            def combine(m):
                for q in range(4):
                    n = 4 * m + q
                    row = acc[:, n, :] if isinstance(n, int) else \
                        acc[:, bass.ds(n, 1), :].rearrange("p a d -> p (a d)")
                    w = [cw[:, z, n:n + 1] if isinstance(n, int) else cw[:, z, bass.ds(n, 1)] for z in range(2)]
                    dve.wait_ge(y1_in[q], 16 * m + 16)
                    dve.scalar_tensor_tensor(out=row, in0=y1[q][:], scalar=w[0], in1=row,
                                             op0=ALU.mult, op1=ALU.add).then_inc(add1, 1)
                    dve.wait_ge(add1, n + 1)
                    dve.wait_ge(y2_in[q], 16 * m + 16)
                    dve.scalar_tensor_tensor(out=row, in0=y2[q][:], scalar=w[1], in1=row,
                                             op0=ALU.mult, op1=ALU.add).then_inc(add2, 1)

            combine(0)
            shared_out(3)
            dve.wait_ge(sh_done, 20)
            with dve.Fori(1, NT // 4) as m:
                combine(m)


def kernel(**inputs):
    import numpy as np
    import concourse.bacc as bacc
    from concourse.bass_utils import run_bass_kernel_spmd

    a = {k: np.asarray(v) for k, v in inputs.items()}
    pt = np.ascontiguousarray

    def by_k(w):
        return w.reshape(w.shape[0], KD, P).transpose(2, 1, 0)

    def halves(w):
        return pt(by_k(w).reshape(P, KD, 2, 512).transpose(0, 2, 1, 3).reshape(P, 4096))

    wq = a["L0_xattn_Wq"].reshape(KVH, HG * HD, KD, P).transpose(0, 3, 2, 1).reshape(KVH, P, 2048)
    wo = a["L0_xattn_Wo"].reshape(D, KVH, HG, HD).transpose(1, 3, 2, 0).reshape(KVH, P, 2048)
    shared = by_k(a["L0_ffn_shared_w_gate_up"]).reshape(1, P, 4096)
    w_att = np.concatenate([np.concatenate([wq, wo], axis=2), shared], axis=0)
    w_att = w_att.reshape(KVH + 1, P, NC, 512).transpose(0, 2, 1, 3).reshape(-1, P, 512)
    arrays = {
        "x": pt(a["x"].reshape(NT, P, D)),
        "ctxT": pt(a["ctx_4096"].reshape(NC, CT, KD, P).transpose(0, 3, 2, 1)),
        "wk": halves(a["L0_xattn_Wk"]),
        "wv": halves(a["L0_xattn_Wv"]),
        "w_att": pt(w_att),
        "w_shd": pt(a["L0_ffn_shared_w_down"].reshape(D, SI // P, P).transpose(2, 1, 0).reshape(P, 2048)),
        "mask": pt(a["mask_1x1xSxS2_ff0"].reshape(S, S)),
        "g_x": pt(a["g_xattn"].reshape(1, 1)),
        "g_f": pt(a["g_ffn"].reshape(1, 1)),
        "q_w": pt(a["L0_xattn_q_norm_w"].reshape(HD, 1)),
        "k_w": pt(a["L0_xattn_k_norm_w"].reshape(HD, 1)),
        "gate": pt(by_k(a["L0_ffn_gate_w"]).reshape(P, KD * E)),
        "w_gu": pt(a["L0_ffn_w_gate_up"].reshape(E, 2 * EI, KD, P).transpose(0, 3, 2, 1).reshape(E, P, KD * 2 * EI)),
        "w_dn": pt(a["L0_ffn_w_down"].transpose(0, 2, 1)),
    }
    nc = bacc.Bacc("TRN2", target_bir_lowering=False, num_devices=1)
    aps = {k: nc.dram_tensor(f"in_{k}", v.shape, mybir.dt.from_np(v.dtype), kind="ExternalInput").ap()
           for k, v in arrays.items()}
    out = nc.dram_tensor("out_0", (NT, P, D), F32, kind="ExternalOutput").ap()
    build(nc, **aps, out=out)
    r = run_bass_kernel_spmd(nc, [{f"in_{k}": v for k, v in arrays.items()}], core_ids=[0])
    return np.asarray(r.results[0]["out_0"]).reshape(B, S, D)
```
